# Optimizing a Trainium2 kernel written in Bass

```python
import numpy as np
import jax
import jax.numpy as jnp

def _softmax(x, axis=-1):
    return jax.nn.softmax(x, axis=axis)
def _gelu(x):
    return jax.nn.gelu(x, approximate=True)
def _silu(x):
    return jax.nn.silu(x)
def _sigmoid(x):
    return jax.nn.sigmoid(x)
def _layernorm(x, axis=-1, eps=1e-5):
    m = jnp.mean(x, axis=axis, keepdims=True)
    v = jnp.var(x, axis=axis, keepdims=True)
    return (x - m) / jnp.sqrt(v + eps)
def _scatter_add(tgt, idx, src, axis=0):
    return tgt.at[idx].add(src)
def _segment_sum(src, seg, n):
    return jax.ops.segment_sum(src, seg, n)

kernel_name = 'mk_conv_preact_d4_conv_nhwc192_9daa61'

def setup_inputs(seed: int = 0):
    np.random.seed(seed)
    _w = jnp.asarray
    def _rec_inputs():
        import jax
        import jax.numpy as jnp
        _gk = jax.random.key(seed)
        x = -9.309e-05 + 1 * jax.random.normal(jax.random.fold_in(_gk, 1), (8, 56, 56, 192), jnp.float32)
        return x
    x = _rec_inputs()
    def _L0_conv_setup():
        import jax, jax.numpy as jnp
        import numpy as np
        EMBED = 192
        EXPAND = 3
        D1 = EMBED * EXPAND
        RPE_IN = 32
        LAYERS = 3
        LAMBDA = 0.95

        def _rpe_mlp(t, w0, b0, ws, bs, wo, bo):
            h = t @ w0.T + b0
            for i in range(ws.shape[0]):
                h = jax.nn.relu(h) @ ws[i].T + bs[i]
            return jax.nn.relu(h) @ wo.T + bo

        def _toeplitz(x, a):
            n = x.shape[1]
            m = 2 * n
            xf = jnp.fft.rfft(x, m, axis=1)
            af = jnp.fft.rfft(a, m, axis=0)
            return jnp.fft.irfft(xf * af[None], m, axis=1)[:, :n]

        def _forward(x, p_w, p_b, q_w, q_b, v_w, v_b, o_w, o_b, slope, t1_w0, t1_b0, t1_ws, t1_bs, t1_wo, t1_bo, t2_w0, t2_b0, t2_ws, t2_bs, t2_wo, t2_bo):
            b, h, w, d = x.shape
            n = h
            dt = x.dtype
            pos = jnp.arange(1, n, dtype=dt).reshape(-1, 1)
            zero = jnp.zeros((1, 1), dt)
            rpe_input = jnp.concatenate([zero, pos, zero, -pos], axis=0)
            p = jax.nn.silu(x @ p_w.T + p_b)
            q = jax.nn.silu(x @ q_w.T + q_b)
            v = jax.nn.silu(x @ v_w.T + v_b)
            sl = LAMBDA + (1.0 - LAMBDA) * jnp.clip(slope, 0.0, 1.0)
            idx = jnp.arange(1, n, dtype=dt).reshape(1, -1, 1)
            gamma = sl ** idx
            one = jnp.ones((1, 1, D1), dt)
            decay = jnp.concatenate([one, gamma, one, gamma[:, ::-1]], axis=1)[0]
            a1 = _rpe_mlp(rpe_input, t1_w0, t1_b0, t1_ws, t1_bs, t1_wo, t1_bo) * decay
            a2 = _rpe_mlp(rpe_input, t2_w0, t2_b0, t2_ws, t2_bs, t2_wo, t2_bo) * decay
            qv = q * v
            o1 = _toeplitz(qv.reshape(b * h, w, D1), a1).reshape(b, h, w, D1)
            o2 = _toeplitz(jnp.transpose(qv, (0, 2, 1, 3)).reshape(b * w, h, D1), a2)
            o2 = jnp.transpose(o2.reshape(b, w, h, D1), (0, 2, 1, 3))
            out = p * (o1 + o2)
            return out @ o_w.T + o_b
        key = jax.random.key(seed)
        ks = jax.random.split(key, 8)

        def lin(k, out_d, in_d):
            k1, k2 = jax.random.split(k)
            s = 1.0 / np.sqrt(in_d)
            return (jax.random.uniform(k1, (out_d, in_d), jnp.float32, -s, s), jax.random.uniform(k2, (out_d,), jnp.float32, -s, s))
        x = jax.random.normal(ks[0], (8, 56, 56, EMBED), jnp.float32)
        p_w, p_b = lin(ks[1], D1, EMBED)
        q_w, q_b = lin(ks[2], D1, EMBED)
        v_w, v_b = lin(ks[3], D1, EMBED)
        o_w, o_b = lin(ks[4], EMBED, D1)
        slope = (1.0 / jnp.arange(1, D1 + 1, dtype=jnp.float32)).reshape(1, -1)

        def tno_params(kb):
            kk = jax.random.split(kb, 2 + LAYERS)
            w0, b0 = lin(kk[0], RPE_IN, 1)
            ws, bs = ([], [])
            for i in range(LAYERS):
                wi, bi = lin(kk[1 + i], RPE_IN, RPE_IN)
                ws.append(wi)
                bs.append(bi)
            wo, bo = lin(kk[1 + LAYERS], D1, RPE_IN)
            return (w0, b0, jnp.stack(ws), jnp.stack(bs), wo, bo)
        t1 = tno_params(ks[5])
        t2 = tno_params(ks[6])
        return {'x': x, 'p_w': p_w, 'p_b': p_b, 'q_w': q_w, 'q_b': q_b, 'v_w': v_w, 'v_b': v_b, 'o_w': o_w, 'o_b': o_b, 'slope': slope, 't1_w0': t1[0], 't1_b0': t1[1], 't1_ws': t1[2], 't1_bs': t1[3], 't1_wo': t1[4], 't1_bo': t1[5], 't2_w0': t2[0], 't2_b0': t2[1], 't2_ws': t2[2], 't2_bs': t2[3], 't2_wo': t2[4], 't2_bo': t2[5]}
    _L0_conv_all = _L0_conv_setup()
    _L0_conv_in = {k: v for k, v in _L0_conv_all.items() if k in ('p_w', 'p_b', 'q_w', 'q_b', 'v_w', 'v_b', 'o_w', 'o_b', 'slope', 't1_w0', 't1_b0', 't1_ws', 't1_bs', 't1_wo', 't1_bo', 't2_w0', 't2_b0', 't2_ws', 't2_bs', 't2_wo', 't2_bo', )}
    del _L0_conv_all

    def _L1_conv_setup():
        import jax, jax.numpy as jnp
        import numpy as np
        EMBED = 192
        EXPAND = 3
        D1 = EMBED * EXPAND
        RPE_IN = 32
        LAYERS = 3
        LAMBDA = 0.95

        def _rpe_mlp(t, w0, b0, ws, bs, wo, bo):
            h = t @ w0.T + b0
            for i in range(ws.shape[0]):
                h = jax.nn.relu(h) @ ws[i].T + bs[i]
            return jax.nn.relu(h) @ wo.T + bo

        def _toeplitz(x, a):
            n = x.shape[1]
            m = 2 * n
            xf = jnp.fft.rfft(x, m, axis=1)
            af = jnp.fft.rfft(a, m, axis=0)
            return jnp.fft.irfft(xf * af[None], m, axis=1)[:, :n]

        def _forward(x, p_w, p_b, q_w, q_b, v_w, v_b, o_w, o_b, slope, t1_w0, t1_b0, t1_ws, t1_bs, t1_wo, t1_bo, t2_w0, t2_b0, t2_ws, t2_bs, t2_wo, t2_bo):
            b, h, w, d = x.shape
            n = h
            dt = x.dtype
            pos = jnp.arange(1, n, dtype=dt).reshape(-1, 1)
            zero = jnp.zeros((1, 1), dt)
            rpe_input = jnp.concatenate([zero, pos, zero, -pos], axis=0)
            p = jax.nn.silu(x @ p_w.T + p_b)
            q = jax.nn.silu(x @ q_w.T + q_b)
            v = jax.nn.silu(x @ v_w.T + v_b)
            sl = LAMBDA + (1.0 - LAMBDA) * jnp.clip(slope, 0.0, 1.0)
            idx = jnp.arange(1, n, dtype=dt).reshape(1, -1, 1)
            gamma = sl ** idx
            one = jnp.ones((1, 1, D1), dt)
            decay = jnp.concatenate([one, gamma, one, gamma[:, ::-1]], axis=1)[0]
            a1 = _rpe_mlp(rpe_input, t1_w0, t1_b0, t1_ws, t1_bs, t1_wo, t1_bo) * decay
            a2 = _rpe_mlp(rpe_input, t2_w0, t2_b0, t2_ws, t2_bs, t2_wo, t2_bo) * decay
            qv = q * v
            o1 = _toeplitz(qv.reshape(b * h, w, D1), a1).reshape(b, h, w, D1)
            o2 = _toeplitz(jnp.transpose(qv, (0, 2, 1, 3)).reshape(b * w, h, D1), a2)
            o2 = jnp.transpose(o2.reshape(b, w, h, D1), (0, 2, 1, 3))
            out = p * (o1 + o2)
            return out @ o_w.T + o_b
        key = jax.random.key(seed)
        ks = jax.random.split(key, 8)

        def lin(k, out_d, in_d):
            k1, k2 = jax.random.split(k)
            s = 1.0 / np.sqrt(in_d)
            return (jax.random.uniform(k1, (out_d, in_d), jnp.float32, -s, s), jax.random.uniform(k2, (out_d,), jnp.float32, -s, s))
        x = jax.random.normal(ks[0], (8, 56, 56, EMBED), jnp.float32)
        p_w, p_b = lin(ks[1], D1, EMBED)
        q_w, q_b = lin(ks[2], D1, EMBED)
        v_w, v_b = lin(ks[3], D1, EMBED)
        o_w, o_b = lin(ks[4], EMBED, D1)
        slope = (1.0 / jnp.arange(1, D1 + 1, dtype=jnp.float32)).reshape(1, -1)

        def tno_params(kb):
            kk = jax.random.split(kb, 2 + LAYERS)
            w0, b0 = lin(kk[0], RPE_IN, 1)
            ws, bs = ([], [])
            for i in range(LAYERS):
                wi, bi = lin(kk[1 + i], RPE_IN, RPE_IN)
                ws.append(wi)
                bs.append(bi)
            wo, bo = lin(kk[1 + LAYERS], D1, RPE_IN)
            return (w0, b0, jnp.stack(ws), jnp.stack(bs), wo, bo)
        t1 = tno_params(ks[5])
        t2 = tno_params(ks[6])
        return {'x': x, 'p_w': p_w, 'p_b': p_b, 'q_w': q_w, 'q_b': q_b, 'v_w': v_w, 'v_b': v_b, 'o_w': o_w, 'o_b': o_b, 'slope': slope, 't1_w0': t1[0], 't1_b0': t1[1], 't1_ws': t1[2], 't1_bs': t1[3], 't1_wo': t1[4], 't1_bo': t1[5], 't2_w0': t2[0], 't2_b0': t2[1], 't2_ws': t2[2], 't2_bs': t2[3], 't2_wo': t2[4], 't2_bo': t2[5]}
    _L1_conv_all = _L1_conv_setup()
    _L1_conv_in = {k: v for k, v in _L1_conv_all.items() if k in ('p_w', 'p_b', 'q_w', 'q_b', 'v_w', 'v_b', 'o_w', 'o_b', 'slope', 't1_w0', 't1_b0', 't1_ws', 't1_bs', 't1_wo', 't1_bo', 't2_w0', 't2_b0', 't2_ws', 't2_bs', 't2_wo', 't2_bo', )}
    del _L1_conv_all

    def _L2_conv_setup():
        import math
        import jax, jax.numpy as jnp
        import numpy as np
        C_DIM, N_STATE, K_DIR = (192, 16, 4)
        D_RANK = math.ceil(C_DIM / 16)
        B_SZ, H_SZ, W_SZ = (2, 64, 64)

        def _ss2d(x, in_proj_w, conv_w, conv_b, x_proj_w, dt_w, dt_b, A_logs, Ds, ln_g, ln_b, out_w):
            B, H, W, C = x.shape
            L = H * W
            dr = dt_w.shape[1]
            N = A_logs.shape[-1]
            K = A_logs.shape[0]
            xz = x @ in_proj_w
            x_ssm, z = (xz[..., :C], xz[..., C:])
            xc = jnp.transpose(x_ssm, (0, 3, 1, 2))
            xc = jax.lax.conv_general_dilated(xc, conv_w, (1, 1), 'SAME', feature_group_count=C)
            xc = jax.nn.silu(xc + conv_b[None, :, None, None])
            x0 = xc.reshape(B, C, L)
            x1 = x0[..., ::-1]
            x2 = jnp.transpose(xc, (0, 1, 3, 2)).reshape(B, C, L)
            x3 = x2[..., ::-1]
            xs = jnp.stack([x0, x1, x2, x3], axis=0)
            proj = jnp.einsum('kbcl,kcd->kbld', xs, x_proj_w)
            dpart = proj[..., :dr]
            Bm = proj[..., dr:dr + N]
            Cm = proj[..., dr + N:]
            delta = jnp.einsum('kblr,krc->kblc', dpart, dt_w) + dt_b[:, None, None, :]
            delta = jax.nn.softplus(delta + dt_b[:, None, None, :])
            A_neg = -jnp.exp(A_logs)
            u_t = jnp.transpose(xs, (3, 0, 1, 2))
            d_t = jnp.transpose(delta, (2, 0, 1, 3))
            B_t = jnp.transpose(Bm, (2, 0, 1, 3))
            C_t = jnp.transpose(Cm, (2, 0, 1, 3))

            def step(state, inp):
                d, b, c, uu = inp
                dA = jnp.exp(d[..., None] * A_neg[:, None, :, :])
                state = dA * state + (d * uu)[..., None] * b[:, :, None, :]
                y = jnp.einsum('kbcn,kbn->kbc', state, c)
                return (state, y)
            init = jnp.zeros((K, B, C, N), jnp.float32)
            _, ys = jax.lax.scan(step, init, (d_t, B_t, C_t, u_t))
            ys = jnp.transpose(ys, (1, 2, 3, 0))
            ys = ys + Ds[:, None, :, None] * xs
            y0 = ys[0].reshape(B, C, H, W)
            y1 = ys[1][..., ::-1].reshape(B, C, H, W)
            y2 = jnp.transpose(ys[2].reshape(B, C, W, H), (0, 1, 3, 2))
            y3 = jnp.transpose(ys[3][..., ::-1].reshape(B, C, W, H), (0, 1, 3, 2))
            y = y0 + y1 + y2 + y3
            y = jnp.transpose(y, (0, 2, 3, 1))
            mu = y.mean(-1, keepdims=True)
            var = y.var(-1, keepdims=True)
            y = (y - mu) / jnp.sqrt(var + 1e-05) * ln_g + ln_b
            y = y * jax.nn.silu(z)
            return y @ out_w
        key = jax.random.key(seed)
        ks = jax.random.split(key, 8)
        C, N, K, dr = (C_DIM, N_STATE, K_DIR, D_RANK)
        x = jax.random.normal(ks[0], (B_SZ, H_SZ, W_SZ, C), jnp.float32)
        in_proj_w = jax.random.normal(ks[1], (C, 2 * C), jnp.float32) / math.sqrt(C)
        conv_w = jax.random.normal(ks[2], (C, 1, 3, 3), jnp.float32) * 0.1
        conv_b = jnp.zeros((C,), jnp.float32)
        x_proj_w = jax.random.normal(ks[3], (K, C, dr + 2 * N), jnp.float32) / math.sqrt(C)
        dt_w = jax.random.normal(ks[4], (K, dr, C), jnp.float32) / math.sqrt(dr)
        dt_min, dt_max, floor = (0.001, 0.1, 0.0001)
        r = jax.random.uniform(ks[5], (K, C), jnp.float32)
        dt_init = jnp.clip(jnp.exp(r * (math.log(dt_max) - math.log(dt_min)) + math.log(dt_min)), floor, None)
        dt_b = dt_init + jnp.log(-jnp.expm1(-dt_init))
        A_logs = jnp.tile(jnp.log(jnp.arange(1, N + 1, dtype=jnp.float32))[None, None, :], (K, C, 1))
        Ds = jnp.ones((K, C), jnp.float32)
        ln_g = jnp.ones((C,), jnp.float32)
        ln_b = jnp.zeros((C,), jnp.float32)
        out_w = jax.random.normal(ks[6], (C, C), jnp.float32) / math.sqrt(C)
        return dict(x=x, in_proj_w=in_proj_w, conv_w=conv_w, conv_b=conv_b, x_proj_w=x_proj_w, dt_w=dt_w, dt_b=dt_b, A_logs=A_logs, Ds=Ds, ln_g=ln_g, ln_b=ln_b, out_w=out_w)
    _L2_conv_all = _L2_conv_setup()
    _L2_conv_in = {k: v for k, v in _L2_conv_all.items() if k in ('in_proj_w', 'conv_w', 'conv_b', 'x_proj_w', 'dt_w', 'dt_b', 'A_logs', 'Ds', 'ln_g', 'ln_b', 'out_w', )}
    del _L2_conv_all

    def _L3_conv_setup():
        import jax, jax.numpy as jnp
        import numpy as np
        GROUP = 12
        _NEI = np.array([[2, 1], [1, 2], [0, 2], [0, 1], [1, 0], [2, 0]])

        def _d6_tables():
            k = np.arange(GROUP) % 6
            s = np.arange(GROUP) // 6
            sign = np.where(s == 0, 1, -1)
            act = (k[:, None] + sign[:, None] * np.arange(6)[None, :]) % 6
            mk = (k[:, None] + sign[:, None] * k[None, :]) % 6
            ms = s[:, None] ^ s[None, :]
            mult = mk + 6 * ms
            return (act, mult)

        def _expand_kernel_deep(kernel):
            act, mult = _d6_tables()
            C, F = (kernel.shape[2], kernel.shape[3])
            posy = np.empty((GROUP, 7), np.int32)
            posx = np.empty((GROUP, 7), np.int32)
            posy[:, 0] = 1
            posx[:, 0] = 1
            posy[:, 1:] = _NEI[act][:, :, 0]
            posx[:, 1:] = _NEI[act][:, :, 1]
            gg, tt, hh = np.meshgrid(np.arange(GROUP), np.arange(7), np.arange(GROUP), indexing='ij')
            Y, X = (posy[gg, tt], posx[gg, tt])
            H2 = mult[gg, hh]
            Ke = jnp.zeros((3, 3, GROUP, C, GROUP, F), kernel.dtype)
            Ke = Ke.at[Y, X, H2, :, gg, :].set(kernel[tt, hh])
            return Ke.reshape(3, 3, GROUP * C, GROUP * F)
        key = jax.random.key(seed)
        k1, k2 = jax.random.split(key)
        B, H, W, C, F = (16, 96, 96, 16, 16)
        x = jax.random.normal(k1, (B, H, W, GROUP * C), dtype=jnp.float32)
        kernel = jax.random.normal(k2, (7, GROUP, C, F), dtype=jnp.float32) * 0.05
        return {'x': x, 'kernel': kernel}
    _L3_conv_all = _L3_conv_setup()
    _L3_conv_in = {k: v for k, v in _L3_conv_all.items() if k in ('kernel', )}
    del _L3_conv_all

    return {
        "x": x,
        "L0_conv_p_w": _L0_conv_in["p_w"],
        "L0_conv_p_b": _L0_conv_in["p_b"],
        "L0_conv_q_w": _L0_conv_in["q_w"],
        "L0_conv_q_b": _L0_conv_in["q_b"],
        "L0_conv_v_w": _L0_conv_in["v_w"],
        "L0_conv_v_b": _L0_conv_in["v_b"],
        "L0_conv_o_w": _L0_conv_in["o_w"],
        "L0_conv_o_b": _L0_conv_in["o_b"],
        "L0_conv_slope": _L0_conv_in["slope"],
        "L0_conv_t1_w0": _L0_conv_in["t1_w0"],
        "L0_conv_t1_b0": _L0_conv_in["t1_b0"],
        "L0_conv_t1_ws": _L0_conv_in["t1_ws"],
        "L0_conv_t1_bs": _L0_conv_in["t1_bs"],
        "L0_conv_t1_wo": _L0_conv_in["t1_wo"],
        "L0_conv_t1_bo": _L0_conv_in["t1_bo"],
        "L0_conv_t2_w0": _L0_conv_in["t2_w0"],
        "L0_conv_t2_b0": _L0_conv_in["t2_b0"],
        "L0_conv_t2_ws": _L0_conv_in["t2_ws"],
        "L0_conv_t2_bs": _L0_conv_in["t2_bs"],
        "L0_conv_t2_wo": _L0_conv_in["t2_wo"],
        "L0_conv_t2_bo": _L0_conv_in["t2_bo"],
        "L1_conv_p_w": _L1_conv_in["p_w"],
        "L1_conv_p_b": _L1_conv_in["p_b"],
        "L1_conv_q_w": _L1_conv_in["q_w"],
        "L1_conv_q_b": _L1_conv_in["q_b"],
        "L1_conv_v_w": _L1_conv_in["v_w"],
        "L1_conv_v_b": _L1_conv_in["v_b"],
        "L1_conv_o_w": _L1_conv_in["o_w"],
        "L1_conv_o_b": _L1_conv_in["o_b"],
        "L1_conv_slope": _L1_conv_in["slope"],
        "L1_conv_t1_w0": _L1_conv_in["t1_w0"],
        "L1_conv_t1_b0": _L1_conv_in["t1_b0"],
        "L1_conv_t1_ws": _L1_conv_in["t1_ws"],
        "L1_conv_t1_bs": _L1_conv_in["t1_bs"],
        "L1_conv_t1_wo": _L1_conv_in["t1_wo"],
        "L1_conv_t1_bo": _L1_conv_in["t1_bo"],
        "L1_conv_t2_w0": _L1_conv_in["t2_w0"],
        "L1_conv_t2_b0": _L1_conv_in["t2_b0"],
        "L1_conv_t2_ws": _L1_conv_in["t2_ws"],
        "L1_conv_t2_bs": _L1_conv_in["t2_bs"],
        "L1_conv_t2_wo": _L1_conv_in["t2_wo"],
        "L1_conv_t2_bo": _L1_conv_in["t2_bo"],
        "L2_conv_in_proj_w": _L2_conv_in["in_proj_w"],
        "L2_conv_conv_w": _L2_conv_in["conv_w"],
        "L2_conv_conv_b": _L2_conv_in["conv_b"],
        "L2_conv_x_proj_w": _L2_conv_in["x_proj_w"],
        "L2_conv_dt_w": _L2_conv_in["dt_w"],
        "L2_conv_dt_b": _L2_conv_in["dt_b"],
        "L2_conv_A_logs": _L2_conv_in["A_logs"],
        "L2_conv_Ds": _L2_conv_in["Ds"],
        "L2_conv_ln_g": _L2_conv_in["ln_g"],
        "L2_conv_ln_b": _L2_conv_in["ln_b"],
        "L2_conv_out_w": _L2_conv_in["out_w"],
        "L3_conv_kernel": _L3_conv_in["kernel"],
    }

def reference(x, L0_conv_p_w, L0_conv_p_b, L0_conv_q_w, L0_conv_q_b, L0_conv_v_w, L0_conv_v_b, L0_conv_o_w, L0_conv_o_b, L0_conv_slope, L0_conv_t1_w0, L0_conv_t1_b0, L0_conv_t1_ws, L0_conv_t1_bs, L0_conv_t1_wo, L0_conv_t1_bo, L0_conv_t2_w0, L0_conv_t2_b0, L0_conv_t2_ws, L0_conv_t2_bs, L0_conv_t2_wo, L0_conv_t2_bo, L1_conv_p_w, L1_conv_p_b, L1_conv_q_w, L1_conv_q_b, L1_conv_v_w, L1_conv_v_b, L1_conv_o_w, L1_conv_o_b, L1_conv_slope, L1_conv_t1_w0, L1_conv_t1_b0, L1_conv_t1_ws, L1_conv_t1_bs, L1_conv_t1_wo, L1_conv_t1_bo, L1_conv_t2_w0, L1_conv_t2_b0, L1_conv_t2_ws, L1_conv_t2_bs, L1_conv_t2_wo, L1_conv_t2_bo, L2_conv_in_proj_w, L2_conv_conv_w, L2_conv_conv_b, L2_conv_x_proj_w, L2_conv_dt_w, L2_conv_dt_b, L2_conv_A_logs, L2_conv_Ds, L2_conv_ln_g, L2_conv_ln_b, L2_conv_out_w, L3_conv_kernel):
    import jax
    import jax.numpy as jnp
    def _L0_conv_ref(x, p_w, p_b, q_w, q_b, v_w, v_b, o_w, o_b, slope, t1_w0, t1_b0, t1_ws, t1_bs, t1_wo, t1_bo, t2_w0, t2_b0, t2_ws, t2_bs, t2_wo, t2_bo):
        import jax, jax.numpy as jnp
        import numpy as np
        EMBED = 192
        EXPAND = 3
        D1 = EMBED * EXPAND
        RPE_IN = 32
        LAYERS = 3
        LAMBDA = 0.95

        def _rpe_mlp(t, w0, b0, ws, bs, wo, bo):
            h = t @ w0.T + b0
            for i in range(ws.shape[0]):
                h = jax.nn.relu(h) @ ws[i].T + bs[i]
            return jax.nn.relu(h) @ wo.T + bo

        def _toeplitz(x, a):
            n = x.shape[1]
            m = 2 * n
            xf = jnp.fft.rfft(x, m, axis=1)
            af = jnp.fft.rfft(a, m, axis=0)
            return jnp.fft.irfft(xf * af[None], m, axis=1)[:, :n]

        def _forward(x, p_w, p_b, q_w, q_b, v_w, v_b, o_w, o_b, slope, t1_w0, t1_b0, t1_ws, t1_bs, t1_wo, t1_bo, t2_w0, t2_b0, t2_ws, t2_bs, t2_wo, t2_bo):
            b, h, w, d = x.shape
            n = h
            dt = x.dtype
            pos = jnp.arange(1, n, dtype=dt).reshape(-1, 1)
            zero = jnp.zeros((1, 1), dt)
            rpe_input = jnp.concatenate([zero, pos, zero, -pos], axis=0)
            p = jax.nn.silu(x @ p_w.T + p_b)
            q = jax.nn.silu(x @ q_w.T + q_b)
            v = jax.nn.silu(x @ v_w.T + v_b)
            sl = LAMBDA + (1.0 - LAMBDA) * jnp.clip(slope, 0.0, 1.0)
            idx = jnp.arange(1, n, dtype=dt).reshape(1, -1, 1)
            gamma = sl ** idx
            one = jnp.ones((1, 1, D1), dt)
            decay = jnp.concatenate([one, gamma, one, gamma[:, ::-1]], axis=1)[0]
            a1 = _rpe_mlp(rpe_input, t1_w0, t1_b0, t1_ws, t1_bs, t1_wo, t1_bo) * decay
            a2 = _rpe_mlp(rpe_input, t2_w0, t2_b0, t2_ws, t2_bs, t2_wo, t2_bo) * decay
            qv = q * v
            o1 = _toeplitz(qv.reshape(b * h, w, D1), a1).reshape(b, h, w, D1)
            o2 = _toeplitz(jnp.transpose(qv, (0, 2, 1, 3)).reshape(b * w, h, D1), a2)
            o2 = jnp.transpose(o2.reshape(b, w, h, D1), (0, 2, 1, 3))
            out = p * (o1 + o2)
            return out @ o_w.T + o_b
        return _forward(x, p_w, p_b, q_w, q_b, v_w, v_b, o_w, o_b, slope, t1_w0, t1_b0, t1_ws, t1_bs, t1_wo, t1_bo, t2_w0, t2_b0, t2_ws, t2_bs, t2_wo, t2_bo)

    def _L1_conv_ref(x, p_w, p_b, q_w, q_b, v_w, v_b, o_w, o_b, slope, t1_w0, t1_b0, t1_ws, t1_bs, t1_wo, t1_bo, t2_w0, t2_b0, t2_ws, t2_bs, t2_wo, t2_bo):
        import jax, jax.numpy as jnp
        import numpy as np
        EMBED = 192
        EXPAND = 3
        D1 = EMBED * EXPAND
        RPE_IN = 32
        LAYERS = 3
        LAMBDA = 0.95

        def _rpe_mlp(t, w0, b0, ws, bs, wo, bo):
            h = t @ w0.T + b0
            for i in range(ws.shape[0]):
                h = jax.nn.relu(h) @ ws[i].T + bs[i]
            return jax.nn.relu(h) @ wo.T + bo

        def _toeplitz(x, a):
            n = x.shape[1]
            m = 2 * n
            xf = jnp.fft.rfft(x, m, axis=1)
            af = jnp.fft.rfft(a, m, axis=0)
            return jnp.fft.irfft(xf * af[None], m, axis=1)[:, :n]

        def _forward(x, p_w, p_b, q_w, q_b, v_w, v_b, o_w, o_b, slope, t1_w0, t1_b0, t1_ws, t1_bs, t1_wo, t1_bo, t2_w0, t2_b0, t2_ws, t2_bs, t2_wo, t2_bo):
            b, h, w, d = x.shape
            n = h
            dt = x.dtype
            pos = jnp.arange(1, n, dtype=dt).reshape(-1, 1)
            zero = jnp.zeros((1, 1), dt)
            rpe_input = jnp.concatenate([zero, pos, zero, -pos], axis=0)
            p = jax.nn.silu(x @ p_w.T + p_b)
            q = jax.nn.silu(x @ q_w.T + q_b)
            v = jax.nn.silu(x @ v_w.T + v_b)
            sl = LAMBDA + (1.0 - LAMBDA) * jnp.clip(slope, 0.0, 1.0)
            idx = jnp.arange(1, n, dtype=dt).reshape(1, -1, 1)
            gamma = sl ** idx
            one = jnp.ones((1, 1, D1), dt)
            decay = jnp.concatenate([one, gamma, one, gamma[:, ::-1]], axis=1)[0]
            a1 = _rpe_mlp(rpe_input, t1_w0, t1_b0, t1_ws, t1_bs, t1_wo, t1_bo) * decay
            a2 = _rpe_mlp(rpe_input, t2_w0, t2_b0, t2_ws, t2_bs, t2_wo, t2_bo) * decay
            qv = q * v
            o1 = _toeplitz(qv.reshape(b * h, w, D1), a1).reshape(b, h, w, D1)
            o2 = _toeplitz(jnp.transpose(qv, (0, 2, 1, 3)).reshape(b * w, h, D1), a2)
            o2 = jnp.transpose(o2.reshape(b, w, h, D1), (0, 2, 1, 3))
            out = p * (o1 + o2)
            return out @ o_w.T + o_b
        return _forward(x, p_w, p_b, q_w, q_b, v_w, v_b, o_w, o_b, slope, t1_w0, t1_b0, t1_ws, t1_bs, t1_wo, t1_bo, t2_w0, t2_b0, t2_ws, t2_bs, t2_wo, t2_bo)

    def _L2_conv_ref(x, in_proj_w, conv_w, conv_b, x_proj_w, dt_w, dt_b, A_logs, Ds, ln_g, ln_b, out_w):
        import math
        import jax, jax.numpy as jnp
        import numpy as np
        C_DIM, N_STATE, K_DIR = (192, 16, 4)
        D_RANK = math.ceil(C_DIM / 16)
        B_SZ, H_SZ, W_SZ = (2, 64, 64)

        def _ss2d(x, in_proj_w, conv_w, conv_b, x_proj_w, dt_w, dt_b, A_logs, Ds, ln_g, ln_b, out_w):
            B, H, W, C = x.shape
            L = H * W
            dr = dt_w.shape[1]
            N = A_logs.shape[-1]
            K = A_logs.shape[0]
            xz = x @ in_proj_w
            x_ssm, z = (xz[..., :C], xz[..., C:])
            xc = jnp.transpose(x_ssm, (0, 3, 1, 2))
            xc = jax.lax.conv_general_dilated(xc, conv_w, (1, 1), 'SAME', feature_group_count=C)
            xc = jax.nn.silu(xc + conv_b[None, :, None, None])
            x0 = xc.reshape(B, C, L)
            x1 = x0[..., ::-1]
            x2 = jnp.transpose(xc, (0, 1, 3, 2)).reshape(B, C, L)
            x3 = x2[..., ::-1]
            xs = jnp.stack([x0, x1, x2, x3], axis=0)
            proj = jnp.einsum('kbcl,kcd->kbld', xs, x_proj_w)
            dpart = proj[..., :dr]
            Bm = proj[..., dr:dr + N]
            Cm = proj[..., dr + N:]
            delta = jnp.einsum('kblr,krc->kblc', dpart, dt_w) + dt_b[:, None, None, :]
            delta = jax.nn.softplus(delta + dt_b[:, None, None, :])
            A_neg = -jnp.exp(A_logs)
            u_t = jnp.transpose(xs, (3, 0, 1, 2))
            d_t = jnp.transpose(delta, (2, 0, 1, 3))
            B_t = jnp.transpose(Bm, (2, 0, 1, 3))
            C_t = jnp.transpose(Cm, (2, 0, 1, 3))

            def step(state, inp):
                d, b, c, uu = inp
                dA = jnp.exp(d[..., None] * A_neg[:, None, :, :])
                state = dA * state + (d * uu)[..., None] * b[:, :, None, :]
                y = jnp.einsum('kbcn,kbn->kbc', state, c)
                return (state, y)
            init = jnp.zeros((K, B, C, N), jnp.float32)
            _, ys = jax.lax.scan(step, init, (d_t, B_t, C_t, u_t))
            ys = jnp.transpose(ys, (1, 2, 3, 0))
            ys = ys + Ds[:, None, :, None] * xs
            y0 = ys[0].reshape(B, C, H, W)
            y1 = ys[1][..., ::-1].reshape(B, C, H, W)
            y2 = jnp.transpose(ys[2].reshape(B, C, W, H), (0, 1, 3, 2))
            y3 = jnp.transpose(ys[3][..., ::-1].reshape(B, C, W, H), (0, 1, 3, 2))
            y = y0 + y1 + y2 + y3
            y = jnp.transpose(y, (0, 2, 3, 1))
            mu = y.mean(-1, keepdims=True)
            var = y.var(-1, keepdims=True)
            y = (y - mu) / jnp.sqrt(var + 1e-05) * ln_g + ln_b
            y = y * jax.nn.silu(z)
            return y @ out_w
        return _ss2d(x, in_proj_w, conv_w, conv_b, x_proj_w, dt_w, dt_b, A_logs, Ds, ln_g, ln_b, out_w)

    def _L3_conv_ref(x, kernel):
        import jax, jax.numpy as jnp
        import numpy as np
        GROUP = 12
        _NEI = np.array([[2, 1], [1, 2], [0, 2], [0, 1], [1, 0], [2, 0]])

        def _d6_tables():
            k = np.arange(GROUP) % 6
            s = np.arange(GROUP) // 6
            sign = np.where(s == 0, 1, -1)
            act = (k[:, None] + sign[:, None] * np.arange(6)[None, :]) % 6
            mk = (k[:, None] + sign[:, None] * k[None, :]) % 6
            ms = s[:, None] ^ s[None, :]
            mult = mk + 6 * ms
            return (act, mult)

        def _expand_kernel_deep(kernel):
            act, mult = _d6_tables()
            C, F = (kernel.shape[2], kernel.shape[3])
            posy = np.empty((GROUP, 7), np.int32)
            posx = np.empty((GROUP, 7), np.int32)
            posy[:, 0] = 1
            posx[:, 0] = 1
            posy[:, 1:] = _NEI[act][:, :, 0]
            posx[:, 1:] = _NEI[act][:, :, 1]
            gg, tt, hh = np.meshgrid(np.arange(GROUP), np.arange(7), np.arange(GROUP), indexing='ij')
            Y, X = (posy[gg, tt], posx[gg, tt])
            H2 = mult[gg, hh]
            Ke = jnp.zeros((3, 3, GROUP, C, GROUP, F), kernel.dtype)
            Ke = Ke.at[Y, X, H2, :, gg, :].set(kernel[tt, hh])
            return Ke.reshape(3, 3, GROUP * C, GROUP * F)
        Ke = _expand_kernel_deep(kernel)
        out = jax.lax.conv_general_dilated(x, Ke, window_strides=(1, 1), padding='SAME', dimension_numbers=('NHWC', 'HWIO', 'NHWC'))
        return out

    def _gn(v, G=32, eps=1e-5):
        B_, H_, W_, C_ = v.shape
        g = v.reshape(B_, H_, W_, G, C_ // G)
        m = jnp.mean(g, axis=(1, 2, 4), keepdims=True)
        s = jnp.var(g, axis=(1, 2, 4), keepdims=True)
        return ((g - m) / jnp.sqrt(s + eps)).reshape(v.shape)

    def _ln_c(v, eps=1e-6):
        m = jnp.mean(v, axis=-1, keepdims=True)
        s = jnp.var(v, axis=-1, keepdims=True)
        return (v - m) / jnp.sqrt(s + eps)

    def _ln_t(v, eps=1e-5):
        m = jnp.mean(v, axis=-1, keepdims=True)
        s = jnp.var(v, axis=-1, keepdims=True)
        return (v - m) / jnp.sqrt(s + eps)

    def _to_tokens(v):
        B_, H_, W_, C_ = v.shape
        return v.reshape(B_, H_ * W_, C_)
    def _from_tokens(t, like):
        return t.reshape(like.shape)

    x = x + _L0_conv_ref(_gn(x), L0_conv_p_w, L0_conv_p_b, L0_conv_q_w, L0_conv_q_b, L0_conv_v_w, L0_conv_v_b, L0_conv_o_w, L0_conv_o_b, L0_conv_slope, L0_conv_t1_w0, L0_conv_t1_b0, L0_conv_t1_ws, L0_conv_t1_bs, L0_conv_t1_wo, L0_conv_t1_bo, L0_conv_t2_w0, L0_conv_t2_b0, L0_conv_t2_ws, L0_conv_t2_bs, L0_conv_t2_wo, L0_conv_t2_bo)
    x = x + _L1_conv_ref(_gn(x), L1_conv_p_w, L1_conv_p_b, L1_conv_q_w, L1_conv_q_b, L1_conv_v_w, L1_conv_v_b, L1_conv_o_w, L1_conv_o_b, L1_conv_slope, L1_conv_t1_w0, L1_conv_t1_b0, L1_conv_t1_ws, L1_conv_t1_bs, L1_conv_t1_wo, L1_conv_t1_bo, L1_conv_t2_w0, L1_conv_t2_b0, L1_conv_t2_ws, L1_conv_t2_bs, L1_conv_t2_wo, L1_conv_t2_bo)
    x = x + _L2_conv_ref(_gn(x), L2_conv_in_proj_w, L2_conv_conv_w, L2_conv_conv_b, L2_conv_x_proj_w, L2_conv_dt_w, L2_conv_dt_b, L2_conv_A_logs, L2_conv_Ds, L2_conv_ln_g, L2_conv_ln_b, L2_conv_out_w)
    x = x + _L3_conv_ref(_gn(x), L3_conv_kernel)
    return x


_drawn_inputs = setup_inputs


def setup_inputs(seed=0):
    import zlib

    import numpy as np

    out = dict(_drawn_inputs(seed))
    spreads = {'L2_conv_conv_b': (0.0, 0.1),
     'L2_conv_Ds': (1.0, 0.2),
     'L2_conv_ln_g': (1.0, 0.2),
     'L2_conv_ln_b': (0.0, 0.1)}
    factors = {'L0_conv_p_b': 8.0,
     'L0_conv_q_b': 7.426,
     'L0_conv_v_b': 7.705,
     'L0_conv_slope': 8.0,
     'L0_conv_t1_w0': 2.833,
     'L0_conv_t1_b0': 8.0,
     'L0_conv_t1_bs': 8.0,
     'L0_conv_t1_bo': 5.376,
     'L0_conv_t2_w0': 2.896,
     'L0_conv_t2_b0': 26.42,
     'L0_conv_t2_bs': 8.0,
     'L0_conv_t2_bo': 5.706,
     'L1_conv_p_b': 8.0,
     'L1_conv_q_b': 7.44,
     'L1_conv_v_b': 7.732,
     'L1_conv_slope': 8.0,
     'L1_conv_t1_w0': 2.849,
     'L1_conv_t1_b0': 8.0,
     'L1_conv_t1_bs': 8.0,
     'L1_conv_t1_bo': 5.391,
     'L1_conv_t2_w0': 2.909,
     'L1_conv_t2_b0': 28.867,
     'L1_conv_t2_bs': 8.0,
     'L1_conv_t2_bo': 5.763,
     'L2_conv_x_proj_w': 8.0,
     'L2_conv_dt_w': 8.0,
     'L2_conv_dt_b': 8.0,
     'L2_conv_A_logs': 8.0,
     'L1_conv_o_b': 2.937}
    for name, (base, spread) in spreads.items():
        noise = np.random.default_rng([zlib.crc32(name.encode()), seed]).standard_normal(out[name].shape)
        drawn = base * np.exp(spread * noise) if base else spread * noise
        out[name] = jnp.asarray(drawn.astype(out[name].dtype))
    for name, factor in factors.items():
        out[name] = (out[name] * factor).astype(out[name].dtype)
    return out
```

```python
from contextlib import ExitStack

import concourse.bass as bass
from concourse import mybir

F32 = mybir.dt.float32
BF16 = mybir.dt.bfloat16
ALU = mybir.AluOpType
ACT = mybir.ActivationFunctionType

BATCH, SIDE, CH = 8, 56, 192
TOK = SIDE * SIDE
HALF = CH // 2
D1 = 3 * CH
GROUPS = D1 // HALF
CHUNK = 8 * SIDE
NCHUNK = TOK // CHUNK
LAGS = 2 * SIDE
GN_EPS = 1e-5
BANK = 512

WCOLS = 2 * 3 * HALF
BIAS = WCOLS


class Pool:

    def __init__(self, nc, sems, tag):
        self.nc, self.sems, self.tag, self.ctx = nc, sems, tag, ExitStack()

    def sb(self, name, shape, dt=F32):
        return self.ctx.enter_context(self.nc.sbuf_tensor(f"{self.tag}.{name}", shape, dt))

    def ps(self, name, shape, dt=F32):
        return self.ctx.enter_context(self.nc.psum_tensor(f"{self.tag}.{name}", shape, dt))

    def sem(self, name):
        return self.sems.enter_context(self.nc.semaphore(f"{self.tag}.{name}"))


def toeplitz_tables(nc, sems, tag, mlp, slope, rpe, consts, lag_dram, table_dram):
    m = Pool(nc, sems, tag)
    with m.ctx:
        pos = m.sb("pos", [1, LAGS])
        expo = m.sb("expo", [HALF, LAGS])
        w0 = m.sb("w0", [1, 2, 32])
        hid = m.sb("hid", [32, 2, 3 * 32 + D1 + 4])
        bo = m.sb("bo", [HALF, 2, GROUPS])
        sl = m.sb("sl", [HALF, GROUPS])
        lnsl = m.sb("lnsl", [HALF, GROUPS])
        decay = m.sb("decay", [HALF, GROUPS, LAGS])
        h = m.sb("h", [32, 2, 4, LAGS])
        taps = m.sb("taps", [HALF, 2, GROUPS, LAGS])
        ph = m.ps("ph", [32, 2, BANK])
        pa = m.ps("pa", [HALF, 2, BANK])

        loaded = m.sem("loaded")
        hidden = m.sem("hidden")
        relu = m.sem("relu")
        clipped = m.sem("clipped")
        logged = m.sem("logged")
        decayed = m.sem("decayed")
        tap_ready = m.sem("tap_ready")
        tap_done = m.sem("tap_done")
        stored = m.sem("stored")
        skewed = m.sem("skewed")

        block = m.ctx.enter_context(nc.Block())

        @block.sync
        def _(sp):
            sp.dma_start(pos[:], rpe).then_inc(loaded, 16)
            sp.dma_start(expo[:], consts["expo"]).then_inc(loaded, 16)
            sp.dma_start(sl[:], slope).then_inc(loaded, 16)
            for k in range(2):
                sp.dma_start(w0[:, k, :], mlp[k]["w0"]).then_inc(loaded, 16)
                sp.dma_start(hid[:, k, :], mlp[k]["hid"]).then_inc(loaded, 16)
                sp.dma_start(bo[:, k, :], mlp[k]["bo"]).then_inc(loaded, 16)
            for k in range(2):
                sp.wait_ge(tap_done, GROUPS * (k + 1))
                sp.dma_start(lag_dram[k].rearrange("(g p) l -> p g l", p=HALF), taps[:, k, :, :]).then_inc(stored, 16)
                sp.wait_ge(stored, 16 * (k + 1))
                with sp.Fori(0, SIDE) as w:
                    sp.dma_start(table_dram[k][bass.ds(w, 1), :, :],
                                 lag_dram[k].unsqueeze(0)[:, :, bass.ds(SIDE - 1 - w, SIDE)]).then_inc(skewed, 16)
            sp.wait_ge(skewed, 16 * SIDE * 2)

        @block.tensor
        def _(pe):
            pe.wait_ge(loaded, 9 * 16)
            for k in range(2):
                for layer in range(4):
                    if k or layer:
                        pe.wait_ge(relu, 4 * k + layer)
                    if layer == 0:
                        pe.matmul(ph[:, k, 0:LAGS], w0[:, k, :], pos[:], start=True, stop=True).then_inc(hidden, 1)
                    else:
                        pe.matmul(ph[:, k, 0:LAGS], hid[:, k, 32 * (layer - 1):32 * layer], h[:, k, layer - 1, :],
                                  start=True, stop=True).then_inc(hidden, 1)
                pe.wait_ge(relu, 4 * k + 4)
                for g in range(GROUPS):
                    n = GROUPS * k + g
                    if n >= 2:
                        pe.wait_ge(tap_done, n - 1)
                    pe.matmul(pa[:, n % 2, 0:LAGS], hid[:, k, 96 + HALF * g:96 + HALF * (g + 1)], h[:, k, 3, :],
                              start=True, stop=True).then_inc(tap_ready, 1)

        @block.scalar
        def _(act):
            for k in range(2):
                for layer in range(4):
                    act.wait_ge(hidden, 4 * k + layer + 1)
                    act.activation(h[:, k, layer, :], ph[:, k, 0:LAGS], ACT.Relu,
                                   bias=hid[:, k, 96 + D1 + layer:97 + D1 + layer]).then_inc(relu, 1)
                if k == 0:
                    act.wait_ge(clipped, 2)
                    act.activation(lnsl[:], sl[:], ACT.Ln).then_inc(logged, 1)
                    act.wait_ge(logged, 1)
                    for g in range(GROUPS):
                        act.activation(decay[:, g, :], expo[:], ACT.Exp, scale=lnsl[:, g:g + 1]).then_inc(decayed, 1)

        @block.vector
        def _(dve):
            dve.wait_ge(loaded, 9 * 16)
            dve.tensor_scalar(sl[:], sl[:], 0.0, 1.0, ALU.max, ALU.min).then_inc(clipped, 1)
            dve.wait_ge(clipped, 1)
            dve.tensor_scalar(sl[:], sl[:], 1.0 - 0.95, 0.95, ALU.mult, ALU.add).then_inc(clipped, 1)
            dve.wait_ge(decayed, GROUPS)
            for k in range(2):
                for g in range(GROUPS):
                    n = GROUPS * k + g
                    dve.wait_ge(tap_ready, n + 1)
                    dve.scalar_tensor_tensor(out=taps[:, k, g, :], in0=pa[:, n % 2, 0:LAGS], scalar=bo[:, k, g:g + 1],
                                             in1=decay[:, g, :], op0=ALU.add, op1=ALU.mult).then_inc(tap_done, 1)


def tno_layer(nc, sems, tag, x_in, x_out, weights, out_w, out_b, tables, consts):
    m = Pool(nc, sems, tag)
    with m.ctx:
        x_res = m.sb("x_res", [HALF, 2, 2, TOK])
        xn = m.sb("xn", [HALF, 2, TOK])
        p_all = m.sb("p_all", [HALF, TOK])
        qv = m.sb("qv", [HALF, TOK])
        sq = m.sb("sq", [HALF, 2, CHUNK])
        sv = m.sb("sv", [HALF, 2, CHUNK])
        left = m.sb("left", [128, HALF, SIDE])
        right = m.sb("right", [128, HALF, SIDE])
        t_w = left[0:SIDE, :, :]
        xh = left[64:64 + SIDE, :, :]
        xw = right[0:SIDE, :, :]
        t_h = right[64:64 + SIDE, :, :]
        wg = m.sb("wg", [HALF, WCOLS + 3])
        wo = m.sb("wo", [HALF, CH])
        po = m.sb("po", [HALF, 2, CHUNK])
        ident = m.sb("ident", [HALF, HALF])
        gmean = m.sb("gmean", [HALF, HALF])
        ob = m.sb("ob", [HALF, 2])
        bn = m.sb("bn", [HALF, 2, NCHUNK, 6])
        mv = m.sb("mv", [HALF, 2, 2])
        m2 = m.sb("m2", [HALF, 2])
        gs = m.sb("gs", [HALF, 4])
        gv = m.sb("gv", [HALF, 2])
        rstd = m.sb("rstd", [HALF, 2])
        shift = m.sb("shift", [HALF, 2])

        p_proj = m.ps("p_proj", [128, 2, BANK])
        p_turn = m.ps("p_turn", [128, 4, BANK])
        p_back, p_toe = p_turn[:, 0:2, :], p_turn[:, 2:4, :]
        p_out = m.ps("p_out", [128, 2, BANK])

        const_in = m.sem("const_in")
        gap_zero = m.sem("gap_zero")
        x_loaded = m.sem("x_loaded")
        w_in = m.sem("w_in")
        wo_in = m.sem("wo_in")
        t_in = m.sem("t_in")
        x_stored = m.sem("x_stored")
        passed = m.sem("passed")
        step = m.sem("step")
        group_stats = m.sem("group_stats")
        rstd_done = m.sem("rstd_done")
        normed = m.sem("normed")
        normed_bias = m.sem("normed_bias")
        proj_ready = m.sem("proj_ready")
        silu_done = m.sem("silu_done")
        qv_done = m.sem("qv_done")
        turn_ready = m.sem("turn_ready")
        turned = [m.sem(f"turned{s}") for s in range(2)]
        toe_ready = m.sem("toe_ready")
        toe_done = [m.sem(f"toe_done{s}") for s in range(2)]
        po_done = m.sem("po_done")
        out_ready = m.sem("out_ready")
        added = m.sem("added")

        PROJ = 3 * NCHUNK
        TURNS = 28
        HTURNS = TURNS // 2
        TOES = HALF // 8
        HTOES = TOES // 2
        SHARES = 2 * NCHUNK
        STEPS = 10
        P_FIRST, P_TURNED, P_SUMMED = (0, 1), (2, 3), (4, 5, 6)

        def copy_turned(copy, n):
            k = 4 * (n % HTURNS)
            squares = p_turn[0:SIDE, n % 4, 0:4 * HALF].rearrange("p (e c) -> p e c", e=4)
            return copy((xw if n < HTURNS else xh)[:, :, k:k + 4].rearrange("p c e -> p e c"), squares)

        def copy_toeplitz(copy, n):
            return copy(xw[:, 8 * n:8 * n + 8, :],
                        p_toe[0:SIDE, n % 2, 0:CHUNK].rearrange("p (c h) -> p c h", c=8))

        def steady(eng):
            eng.sem_inc(passed, 1)

        block = m.ctx.enter_context(nc.Block())

        @block.sync
        def _(sp):
            sp.sem_inc(x_stored, 16)
            sp.dma_start(ident[:], consts["ident"][0:HALF, 0:HALF]).then_inc(const_in, 16)
            sp.dma_start(gmean[:], consts["gmean"][0:HALF, 0:HALF]).then_inc(const_in, 16)
            sp.dma_start(ob[:], out_b).then_inc(const_in, 16)
            sp.wait_ge(gap_zero, 2)
            with sp.Fori(0, BATCH) as b:
                with sp.Fori(0, GROUPS) as g:
                    it = sp.snap(b * GROUPS + g)
                    sp.wait_ge(silu_done, it * PROJ + 1)
                    sp.dma_start(wg[:], weights[bass.ds(g, 1), :, :].rearrange("a p n -> (a p) n")).then_inc(w_in, 16)
                    sp.wait_ge(toe_ready, it * TOES + 1)
                    sp.dma_start(t_w, tables[0][:, bass.ds(g * HALF, HALF), :]).then_inc(t_in, 16)
                    sp.dma_start(t_h, tables[1][:, bass.ds(g * HALF, HALF), :]).then_inc(t_in, 16)
                    sp.wait_ge(out_ready, it * SHARES + 1)
                    sp.dma_start(wo[:], out_w[bass.ds(g, 1), :, :].rearrange("a p n -> (a p) n")).then_inc(wo_in, 16)
                sp.wait_ge(added, b * (GROUPS * SHARES) + GROUPS * SHARES + 1)
                sp.dma_start(x_out[bass.ds(b, 1)].rearrange("a (j p) n -> p (a j) n", p=HALF),
                             x_res[:, bass.ds(b % 2, 1), :, :].rearrange("p a j n -> p (a j) n")).then_inc(x_stored, 16)
            sp.wait_ge(x_stored, 16 * BATCH + 16)

        @block.gpsimd
        def _(pool):
            def load(b):
                pool.dma_start(x_res[:, bass.ds(b % 2, 1), :, :].rearrange("p a j n -> p (a j) n"),
                               x_in[bass.ds(b, 1)].rearrange("a (j p) n -> p (a j) n", p=HALF)).then_inc(x_loaded, 16)

            load(0)
            with pool.Fori(1, BATCH) as b:
                pool.wait_ge(normed, b * 2)
                pool.wait_ge(x_stored, b * 16)
                load(b)

        @block.tensor
        def _(pe):
            pe.wait_ge(const_in, 48)
            pe.wait_ge(gap_zero, 2)
            pe.sem_inc(toe_ready, 1)
            pe.sem_inc(out_ready, 1)
            with pe.Fori(0, BATCH) as b:
                pe.wait_ge(step, b * STEPS + 4)
                pe.wait_ge(added, b * (GROUPS * SHARES) + 1)
                pe.matmul(p_out[0:HALF, 0, 0:4], gmean[:], mv[:].rearrange("p j s -> p (j s)"),
                          start=True, stop=True).then_inc(group_stats, 1)
                pe.wait_ge(normed, b * 2 + 2)
                steady(pe)
                with pe.Fori(0, GROUPS) as g:
                    it = pe.snap(b * GROUPS + g)
                    silu0 = pe.snap(it * PROJ + 1)
                    po0 = pe.snap(it * NCHUNK + 1)
                    added0 = pe.snap(it * SHARES + 1)
                    turned0 = pe.snap(it * HTURNS)
                    toe0 = pe.snap(it * HTOES)
                    pe.wait_ge(w_in, it * 16 + 16)

                    def project(kind, t, s, before):
                        pe.wait_ge(silu_done, silu0 + before)
                        for j in range(2):
                            mm = pe.matmul(p_proj[0:HALF, s, 0:CHUNK],
                                           wg[:, (3 * j + kind) * HALF:(3 * j + kind + 1) * HALF],
                                           xn[:, j, t * CHUNK:(t + 1) * CHUNK], start=(j == 0), stop=(j == 1))
                        mm.then_inc(proj_ready, 1)

                    for t in range(NCHUNK):
                        project(0, t, 0, max(2 * t - 1, 0))
                        project(1, t, 1, max(2 * t, 0))
                    for t in P_FIRST:
                        project(2, t, t % 2, 2 * NCHUNK - 1 + t)
                    pe.wait_ge(qv_done, it * NCHUNK + NCHUNK)
                    rows = qv[:].rearrange("p (h w) -> p h w", w=SIDE)
                    cols = qv[:].rearrange("p (h w) -> p w h", w=SIDE)
                    for n in range(TURNS):
                        s = n % 2
                        if n == 0:
                            pe.wait_ge(po_done, po0)
                        elif n >= 4:
                            pe.wait_ge(turned[s], turned0 + (n // 2 - 1))
                        if n == 0 or n >= 4:
                            steady(pe)
                        src = rows if n < HTURNS else cols
                        for e in range(4):
                            mm = pe.transpose(p_turn[0:SIDE, n % 4, e * HALF:(e + 1) * HALF],
                                              src[:, 4 * (n % HTURNS) + e, :], ident[:])
                        mm.then_inc(turn_ready, 1)
                    for t in P_TURNED:
                        project(2, t, t % 2, 2 * NCHUNK - 1 + t)
                    for s in range(2):
                        pe.wait_ge(turned[s], turned0 + HTURNS)
                    pe.wait_ge(t_in, it * 32 + 32)
                    for n in range(TOES):
                        s = n % 2
                        if n >= 2:
                            pe.wait_ge(toe_done[s], toe0 + n // 2)
                        steady(pe)
                        for e in range(8):
                            c = 8 * n + e
                            mm = pe.matmul(p_toe[0:SIDE, s, e * SIDE:(e + 1) * SIDE], left[0:64 + SIDE, c, :],
                                           right[0:64 + SIDE, c, :], start=True, stop=True)
                        mm.then_inc(toe_ready, 1)
                    for t in P_SUMMED:
                        project(2, t, t % 2, 2 * NCHUNK - 1 + t)
                    for s in range(2):
                        pe.wait_ge(toe_done[s], toe0 + HTOES)
                    pe.wait_ge(wo_in, it * 16 + 16)

                    def turn_back(t):
                        if t >= 2:
                            pe.wait_ge(po_done, po0 + (t - 1))
                        steady(pe)
                        for e in range(8):
                            mm = pe.transpose(p_back[0:HALF, t % 2, e * SIDE:(e + 1) * SIDE],
                                              xw[:, :, 8 * t + e], ident[0:SIDE, 0:SIDE])
                        mm.then_inc(turn_ready, 1)

                    def share(t):
                        pe.wait_ge(po_done, po0 + (t + 1))
                        for j in range(2):
                            pe.wait_ge(added, added0 + (2 * t + j - 1 if t else 0))
                            pe.matmul(p_out[0:HALF, j, 0:CHUNK], wo[:, j * HALF:(j + 1) * HALF], po[:, t % 2, :],
                                      start=True, stop=True).then_inc(out_ready, 1)

                    turn_back(0)
                    for t in range(NCHUNK):
                        if t + 1 < NCHUNK:
                            turn_back(t + 1)
                        share(t)

        @block.scalar
        def _(act):
            act.sem_inc(silu_done, 1)
            act.wait_ge(gap_zero, 2)
            with act.Fori(0, BATCH) as b:
                act.wait_ge(step, b * STEPS + 9)
                act.activation(rstd[:], gv[:], ACT.Sqrt).then_inc(rstd_done, 1)
                with act.Fori(0, GROUPS) as g:
                    it = act.snap(b * GROUPS + g)
                    proj0 = act.snap(it * PROJ)
                    qv0 = act.snap(it * NCHUNK)
                    turn0 = act.snap(it * (TURNS + NCHUNK))
                    toe0 = act.snap(it * TOES + 1)
                    act.wait_ge(w_in, it * 16 + 16)
                    for t in range(NCHUNK):
                        if t >= 2:
                            act.wait_ge(qv_done, qv0 + (t - 1))
                        for kind, out in ((0, sq), (1, sv)):
                            act.wait_ge(proj_ready, proj0 + (2 * t + kind + 1))
                            act.activation(out[:, t % 2, :], p_proj[0:HALF, kind, 0:CHUNK], ACT.Silu,
                                           bias=wg[:, BIAS + kind:BIAS + kind + 1]).then_inc(silu_done, 1)

                    def silu_p(t):
                        act.wait_ge(proj_ready, proj0 + (2 * NCHUNK + t + 1))
                        act.activation(p_all[:, t * CHUNK:(t + 1) * CHUNK], p_proj[0:HALF, t % 2, 0:CHUNK], ACT.Silu,
                                       bias=wg[:, BIAS + 2:BIAS + 3]).then_inc(silu_done, 1)

                    for t in P_FIRST:
                        silu_p(t)
                    for n in range(0, TURNS, 2):
                        act.wait_ge(turn_ready, turn0 + (n + 1))
                        copy_turned(act.copy, n).then_inc(turned[0], 1)
                    for t in P_TURNED:
                        silu_p(t)
                    for n in range(0, TOES, 2):
                        act.wait_ge(toe_ready, toe0 + (n + 1))
                        copy_toeplitz(act.copy, n).then_inc(toe_done[0], 1)
                    for t in P_SUMMED:
                        silu_p(t)

        @block.vector
        def _(dve):
            dve.sem_inc(po_done, 1)
            dve.sem_inc(added, 1)
            dve.memset(left[32:64, :, :], 0.0).then_inc(gap_zero, 1)
            dve.memset(right[32:64, :, :], 0.0).then_inc(gap_zero, 1)
            dve.wait_ge(gap_zero, 2)
            dve.wait_ge(const_in, 48)
            with dve.Fori(0, BATCH) as b:
                done = [0]
                step0 = dve.snap(b * STEPS)

                def own(ins):
                    done[0] += 1
                    ins.then_inc(step, 1)
                    dve.wait_ge(step, step0 + done[0])

                def image(j, lo, n):
                    return x_res[:, bass.ds(b % 2, 1), j, lo:lo + n].rearrange("p a n -> p (a n)")

                dve.wait_ge(x_loaded, b * 16 + 16)
                for j in range(2):
                    for t in range(NCHUNK):
                        ins = dve.bn_stats(bn[:, j, t, :], image(j, t * CHUNK, CHUNK))
                own(ins)
                steady(dve)
                for j in range(2):
                    ins = dve.bn_aggr(mv[:, j, :], bn[:, j, :, :].rearrange("p t s -> p (t s)"))
                own(ins)
                own(dve.tensor_tensor(m2[:], mv[:, :, 0], mv[:, :, 0], ALU.mult))
                own(dve.tensor_tensor(mv[:, :, 1], mv[:, :, 1], m2[:], ALU.add))
                dve.wait_ge(group_stats, b + 1)
                own(dve.tensor_copy(gs[:], p_out[0:HALF, 0, 0:4]))
                own(dve.tensor_tensor(m2[:], gs[:, 0:4:2], gs[:, 0:4:2], ALU.mult))
                own(dve.tensor_tensor(gv[:], gs[:, 1:4:2], m2[:], ALU.subtract))
                own(dve.tensor_scalar(gv[:], gv[:], GN_EPS, None, ALU.add))
                own(dve.reciprocal(gv[:], gv[:]))
                dve.wait_ge(rstd_done, b + 1)
                own(dve.scalar_tensor_tensor(out=shift[:], in0=gs[:, 0:4:2], scalar=-1.0, in1=rstd[:],
                                             op0=ALU.mult, op1=ALU.mult))
                assert done[0] == STEPS
                for j in range(2):
                    dve.tensor_scalar(xn[:, j, :], image(j, 0, TOK), rstd[:, j:j + 1], shift[:, j:j + 1],
                                      ALU.mult, ALU.add).then_inc(normed, 1)
                dve.wait_ge(normed, b * 2 + 2)
                for j in range(2):
                    dve.tensor_scalar(image(j, 0, TOK), image(j, 0, TOK), ob[:, j:j + 1], None,
                                      ALU.add).then_inc(normed_bias, 1)
                dve.wait_ge(normed_bias, b * 2 + 2)
                steady(dve)

                with dve.Fori(0, GROUPS) as g:
                    it = dve.snap(b * GROUPS + g)
                    silu0 = dve.snap(it * PROJ + 1)
                    turn0 = dve.snap(it * (TURNS + NCHUNK))
                    toe0 = dve.snap(it * TOES + 1)
                    out0 = dve.snap(it * SHARES + 1)
                    for t in range(NCHUNK):
                        dve.wait_ge(silu_done, silu0 + (2 * t + 2))
                        dve.tensor_tensor(qv[:, t * CHUNK:(t + 1) * CHUNK], sq[:, t % 2, :], sv[:, t % 2, :],
                                          ALU.mult).then_inc(qv_done, 1)
                    for n in range(1, TURNS, 2):
                        dve.wait_ge(turn_ready, turn0 + (n + 1))
                        copy_turned(dve.tensor_copy, n).then_inc(turned[1], 1)
                    for n in range(1, TOES, 2):
                        dve.wait_ge(toe_ready, toe0 + (n + 1))
                        copy_toeplitz(dve.tensor_copy, n).then_inc(toe_done[1], 1)

                    def times_p(t):
                        dve.wait_ge(silu_done, silu0 + (2 * NCHUNK + t + 1))
                        dve.wait_ge(turn_ready, turn0 + (TURNS + t + 1))
                        dve.wait_ge(out_ready, out0 + max(2 * t - 2, 0))
                        dve.tensor_tensor(po[:, t % 2, :], p_back[0:HALF, t % 2, 0:CHUNK],
                                          p_all[:, t * CHUNK:(t + 1) * CHUNK], ALU.mult).then_inc(po_done, 1)

                    def add_share(t):
                        for j in range(2):
                            dve.wait_ge(out_ready, out0 + (2 * t + j + 1))
                            place = image(j, t * CHUNK, CHUNK)
                            dve.tensor_tensor(place, place, p_out[0:HALF, j, 0:CHUNK], ALU.add).then_inc(added, 1)

                    times_p(0)
                    for t in range(NCHUNK):
                        if t + 1 < NCHUNK:
                            times_p(t + 1)
                        add_share(t)


TAPS = [(1, 1), (2, 1), (1, 2), (0, 2), (0, 1), (1, 0), (2, 0)]


def conv_layer(nc, sems, tag, x_in, x_out, taps_w, consts):
    m = Pool(nc, sems, tag)
    PADDED = SIDE + 2
    with m.ctx:
        x_res = m.sb("x_res", [HALF, 2, 2, TOK])
        xn = m.sb("xn", [HALF, 2, 2, PADDED, PADDED])
        w = m.sb("w", [HALF, 2, len(TAPS), CH])
        gmean = m.sb("gmean", [HALF, HALF])
        bn = m.sb("bn", [HALF, 2, NCHUNK, 6])
        mv = m.sb("mv", [HALF, 2, 2])
        m2 = m.sb("m2", [HALF, 2])
        gs = m.sb("gs", [HALF, 4])
        gv = m.sb("gv", [HALF, 2])
        rstd = m.sb("rstd", [HALF, 2])
        shift = m.sb("shift", [HALF, 2])
        p_stat = m.ps("p_stat", [128, BANK])
        p_conv = m.ps("p_conv", [128, 4, BANK])

        passed = m.sem("passed")
        const_in = m.sem("const_in")
        w_in = m.sem("w_in")
        x_loaded = m.sem("x_loaded")
        x_stored = m.sem("x_stored")
        bordered = m.sem("bordered")
        step = m.sem("step")
        group_stats = m.sem("group_stats")
        rstd_done = m.sem("rstd_done")
        normed = m.sem("normed")
        conv_ready = m.sem("conv_ready")
        added = m.sem("added")

        OUTS = 2 * NCHUNK
        STEPS = 10

        def steady(eng):
            eng.sem_inc(passed, 1)

        def slot(t, b):
            return t[:, bass.ds(b % 2, 1)]

        block = m.ctx.enter_context(nc.Block())

        @block.sync
        def _(sp):
            sp.sem_inc(x_stored, 16)
            sp.dma_start(gmean[:], consts["gmean"][0:HALF, 0:HALF]).then_inc(const_in, 16)
            sp.dma_start(w[:], taps_w).then_inc(w_in, 16)
            with sp.Fori(0, BATCH) as b:
                sp.wait_ge(added, b * OUTS + OUTS + 1)
                sp.dma_start(x_out[bass.ds(b, 1)].rearrange("a (j p) n -> p (a j) n", p=HALF),
                             slot(x_res, b).rearrange("p a j n -> p (a j) n")).then_inc(x_stored, 16)
            sp.wait_ge(x_stored, 16 * BATCH + 16)

        @block.gpsimd
        def _(pool):
            def load(b):
                pool.dma_start(slot(x_res, b).rearrange("p a j n -> p (a j) n"),
                               x_in[bass.ds(b, 1)].rearrange("a (j p) n -> p (a j) n", p=HALF)).then_inc(x_loaded, 16)

            load(0)
            pool.memset(xn[:], 0.0).then_inc(bordered, 1)
            with pool.Fori(1, BATCH) as b:
                pool.wait_ge(normed, b * 2)
                pool.wait_ge(x_stored, b * 16)
                load(b)

        @block.tensor
        def _(pe):
            pe.wait_ge(const_in, 16)
            pe.sem_inc(conv_ready, 1)

            def stats(b):
                pe.wait_ge(step, b * STEPS + 4)
                pe.matmul(p_stat[0:HALF, 0:4], gmean[:], mv[:].rearrange("p j s -> p (j s)"),
                          start=True, stop=True).then_inc(group_stats, 1)

            def conv(b, ahead):
                added0 = pe.snap(b * OUTS)
                pe.wait_ge(normed, b * 2 + 2)
                for t in range(NCHUNK):
                    if t == 3 and ahead:
                        stats(b + 1)
                    for j in range(2):
                        n = 2 * t + j
                        pe.wait_ge(added, added0 + max(n - 3 + 1, 1))
                        k = 0
                        for i, (dy, dx) in enumerate(TAPS):
                            for half in range(2):
                                mm = pe.matmul(p_conv[0:HALF, n % 4, 0:CHUNK],
                                               w[:, half, i, j * HALF:(j + 1) * HALF],
                                               xn[:, bass.ds(b % 2, 1), half, 8 * t + dy:8 * t + dy + 8, dx:dx + SIDE]
                                               .rearrange("p a h w -> p (a h) w"),
                                               start=(k == 0), stop=(k == 2 * len(TAPS) - 1))
                                k += 1
                        mm.then_inc(conv_ready, 1)

            stats(0)
            pe.wait_ge(w_in, 16)
            with pe.Fori(0, BATCH - 1) as b:
                conv(b, True)
            conv(BATCH - 1, False)

        @block.scalar
        def _(act):
            act.wait_ge(bordered, 1)

            def norm(b):
                act.wait_ge(step, b * STEPS + 9)
                act.activation(rstd[:], gv[:], ACT.Sqrt).then_inc(rstd_done, 1)
                act.wait_ge(step, b * STEPS + STEPS)
                for j in range(2):
                    act.wait_ge(conv_ready, (b - 1) * OUTS + 1 if not isinstance(b, int) or b > 1 else 1)
                    act.activation(xn[:, bass.ds(b % 2, 1), j, 1:SIDE + 1, 1:SIDE + 1]
                                   .rearrange("p a h w -> p (a h) w"),
                                   x_res[:, bass.ds(b % 2, 1), j, :].rearrange("p a (h w) -> p (a h) w", w=SIDE),
                                   ACT.Identity, scale=rstd[:, j:j + 1], bias=shift[:, j:j + 1]).then_inc(normed, 1)

            norm(0)
            with act.Fori(1, BATCH) as b:
                norm(b)

        @block.vector
        def _(dve):
            dve.sem_inc(added, 1)

            def stats(b):
                done = [0]
                step0 = dve.snap(b * STEPS) if not isinstance(b, int) else b * STEPS

                def own(ins):
                    done[0] += 1
                    ins.then_inc(step, 1)
                    dve.wait_ge(step, step0 + done[0])

                dve.wait_ge(x_loaded, b * 16 + 16)
                for j in range(2):
                    for t in range(NCHUNK):
                        ins = dve.bn_stats(bn[:, j, t, :], x_res[:, bass.ds(b % 2, 1), j, t * CHUNK:(t + 1) * CHUNK]
                                           .rearrange("p a n -> p (a n)"))
                own(ins)
                steady(dve)
                for j in range(2):
                    ins = dve.bn_aggr(mv[:, j, :], bn[:, j, :, :].rearrange("p t s -> p (t s)"))
                own(ins)
                own(dve.tensor_tensor(m2[:], mv[:, :, 0], mv[:, :, 0], ALU.mult))
                own(dve.tensor_tensor(mv[:, :, 1], mv[:, :, 1], m2[:], ALU.add))
                dve.wait_ge(group_stats, b + 1)
                own(dve.tensor_copy(gs[:], p_stat[0:HALF, 0:4]))
                own(dve.tensor_tensor(m2[:], gs[:, 0:4:2], gs[:, 0:4:2], ALU.mult))
                own(dve.tensor_tensor(gv[:], gs[:, 1:4:2], m2[:], ALU.subtract))
                own(dve.tensor_scalar(gv[:], gv[:], GN_EPS, None, ALU.add))
                own(dve.reciprocal(gv[:], gv[:]))
                dve.wait_ge(rstd_done, b + 1)
                dve.scalar_tensor_tensor(out=shift[:], in0=gs[:, 0:4:2], scalar=-1.0, in1=rstd[:],
                                         op0=ALU.mult, op1=ALU.mult).then_inc(step, 1)
                assert done[0] + 1 == STEPS

            def add(b, ns):
                out0 = dve.snap(b * OUTS + 1) if not isinstance(b, int) else b * OUTS + 1
                dve.wait_ge(normed, b * 2 + 2)
                for n in ns:
                    t, j = n // 2, n % 2
                    dve.wait_ge(conv_ready, out0 + (n + 1))
                    place = x_res[:, bass.ds(b % 2, 1), j, t * CHUNK:(t + 1) * CHUNK].rearrange("p a n -> p (a n)")
                    dve.tensor_tensor(place, place, p_conv[0:HALF, n % 4, 0:CHUNK], ALU.add).then_inc(added, 1)

            stats(0)
            with dve.Fori(0, BATCH - 1) as b:
                add(b, range(2))
                stats(b + 1)
                add(b, range(2, OUTS))
            add(BATCH - 1, range(OUTS))


PAIRS = 4
STATES, DIRS, RANK = 16, 4, 12
LN_EPS = 1e-5
SPAN = 784
HSPAN = SPAN // 2
RING = 4
NSPAN = TOK // SPAN
PADDED = SIDE + 2
MIX = [[(0, 0), (1, 2)], [(0, 1), (2, 2)], [(3, 0), (4, 1), (5, 2)]]
V_CONV, V_CB, V_G, V_B, V_D, V_DT, V_A, V_END = 0, 9, 10, 11, 12, 16, 20, 84


def scan_layer(nc, sems, tag, x_in, x_out, ap, z_dram, consts):
    m = Pool(nc, sems, tag)
    with m.ctx:
        U_SIZE = 16128
        u = m.sb("u", [128, U_SIZE])

        def view(at, *shape, dt=F32):
            n = 1
            for s in shape:
                n *= s
            words = n if dt is F32 else n // 2
            assert at + words <= U_SIZE
            v = u[:, at:at + words]
            if dt is not F32:
                v = v.bitcast(dt)
            if len(shape) == 2:
                return v.rearrange("p (a b) -> p a b", a=shape[0])
            if len(shape) == 3:
                return v.rearrange("p (a b c) -> p a b c", a=shape[0], b=shape[1])
            return v

        xn = view(0, 3, TOK)
        pad = view(3 * TOK, PADDED, PADDED)
        sel_f = u[0:96, 0:3 * STATES * 128].rearrange("p (a b c) -> p a b c", a=3, b=STATES)
        zs = view(U_SIZE - 2 * CHUNK, 2, CHUNK)
        f = view(0, TOK)
        rest = view(TOK, TOK)
        part = [view(2 * TOK + i * TOK // 2, TOK, dt=BF16) for i in range(3)]
        t_abs, t_ln = (view(7 * TOK // 2 + 2 * CHUNK * i, 2, CHUNK) for i in range(2))
        db = view(TOK, RING, SPAN)
        hs = view(TOK + RING * SPAN, RING, SPAN)
        hc = view(TOK + 2 * RING * SPAN, RING, SPAN)
        da = view(TOK + 3 * RING * SPAN, 2, SPAN)
        cb = view(TOK + (3 * RING + 2) * SPAN, 2, SPAN)
        dev = view(0, 3, CHUNK)
        squ = view(3 * CHUNK, 3, CHUNK)
        rs = view(6 * CHUNK, 3, CHUNK)
        zc, xr, oc = (view((9 + 6 * i) * CHUNK, 6, CHUNK) for i in range(3))

        xc = m.sb("xc", [128, 3, TOK])
        y = m.sb("y", [128, 3, TOK])
        d = m.sb("d", [128, TOK])
        du = m.sb("du", [128, TOK])
        bs = m.sb("bs", [96, TOK], BF16)
        cs = m.sb("cs", [96, TOK], BF16)
        sel = m.sb("sel", [96, 3, STATES, 128], BF16)
        ln1 = m.sb("ln1", [128, 1])
        state = m.sb("state", [128, STATES])
        vec = m.sb("vec", [128, 3, V_END])
        dsum = m.sb("dsum", [128, 3])
        dtb = m.sb("dtb", [128, 3 * DIRS])
        nega = m.sb("nega", [128, 3 * DIRS * STATES])
        ident = m.sb("ident", [128, 128])
        w_ssm, w_z, w_gn, w_ln, w_out = (m.sb(n, [128, 6, 128]) for n in ("w_ssm", "w_z", "w_gn", "w_ln", "w_out"))
        w_x = m.sb("w_x", [128, 3, 128])
        w_dt = m.sb("w_dt", [128, 128])
        bn = m.sb("bn", [128, 3, NCHUNK, 6])
        mv = m.sb("mv", [128, 3, 2])
        m2 = m.sb("m2", [128, 3])
        gs = m.sb("gs", [128, 6])
        gv = m.sb("gv", [128, 3])
        rstd = m.sb("rstd", [128, 3])
        shift = m.sb("shift", [128, 3])
        ps = m.ps("ps", [128, 8, BANK])

        passed = m.sem("passed")
        const_in = m.sem("const_in")
        exp_made = m.sem("exp_made")
        made2 = m.sem("made2")
        made = m.sem("made")
        x_loaded = m.sem("x_loaded")
        step = m.sem("step")
        gn_ready = m.sem("gn_ready")
        rstd_done = m.sem("rstd_done")
        normed = m.sem("normed")
        mix_ready = m.sem("mix_ready")
        mix_out = m.sem("mix_out")
        z_stored = [m.sem(f"z_stored{i}") for i in range(2)]
        bordered = m.sem("bordered")
        tap_done = m.sem("tap_done")
        xc_done = m.sem("xc_done")
        y_init = m.sem("y_init")
        wx_in = m.sem("wx_in")
        wdt_in = m.sem("wdt_in")
        f_ready = m.sem("f_ready")
        f_out = m.sem("f_out")
        split = m.sem("split")
        gathered = m.sem("gathered")
        dt_ready = m.sem("dt_ready")
        sp_done = m.sem("sp_done")
        d_step = m.sem("d_step")
        b_ready = m.sem("b_ready")
        c_ready = m.sem("c_ready")
        c_out = m.sem("c_out")
        a_ready = m.sem("a_ready")
        b_done = m.sem("b_done")
        zeroed = m.sem("zeroed")
        scanned = m.sem("scanned")
        kept = m.sem("kept")
        hc_done = m.sem("hc_done")
        y_ready = m.sem("y_ready")
        y_added = m.sem("y_added")
        fin_in = m.sem("fin_in")
        ln_ready = m.sem("ln_ready")
        ln_step = m.sem("ln_step")
        ln_act = m.sem("ln_act")
        out_done = m.sem("out_done")
        x_stored = [m.sem(f"x_stored{i}") for i in range(2)]

        MIXES = 6 * NCHUNK
        ZUSES = (11, 10)
        OUSES = (4, 3)
        STEPS, TAPS9, SPLITS, LNS = 10, 9, 4, 8
        GATHER = 12 * 16
        TILE_N = NSPAN * STATES
        CONSTS = 8

        def steady(eng):
            eng.sem_inc(passed, 1)

        def image_view(flat, k):
            return flat.rearrange("p (h w) -> p h w", w=SIDE) if k < 2 else flat.rearrange("p (h w) -> p w h", w=SIDE)

        def scan_view(flat, k):
            g = image_view(flat, k)
            return g[:, ::-1, ::-1] if k % 2 else g

        def tile(t, i):
            return t[:, bass.ds(i, 1), :].rearrange("p a n -> p (a n)")

        def image_parts(dram, pr, place, lo=0, n=TOK):
            for e in range(2):
                row = dram[bass.ds(2 * pr + e, 1), :, lo:lo + n]
                yield place(e), row[:, 0:128, :].rearrange("a p n -> (a p) n")
                yield place(2)[64 * e:64 * e + 64, :], row[:, 128:CH, :].rearrange("a p n -> (a p) n")

        block = m.ctx.enter_context(nc.Block())

        @block.sync
        def _(sp):
            for place, src in ((sel_f, ap["c_sel"]), (ident[:], consts["ident"]), (vec[:], ap["L2_vec"]),
                               (w_ssm[:], ap["L2_ssm"]), (w_z[:], ap["L2_z"]), (w_gn[:], ap["c_mixgn"]),
                               (w_ln[:], ap["c_mixln"]), (w_out[:], ap["L2_out"])):
                sp.dma_start(place, src).then_inc(const_in, 16)
            sp.wait_ge(made, 1)
            with sp.Fori(0, PAIRS) as pr:
                sp.wait_ge(out_done, pr * NCHUNK + 1)
                for s in range(2):
                    sp.wait_ge(x_stored[s], pr * (64 * OUSES[s]) + 64)
                for place, src in image_parts(x_in, pr, lambda i: xn[:, i, :]):
                    sp.dma_start(place, src).then_inc(x_loaded, 16)
                for n in range(3 * NCHUNK):
                    i, t = n // NCHUNK, n % NCHUNK
                    sp.wait_ge(mix_out, pr * MIXES + (2 * NCHUNK * i + t + 2))
                    sp.dma_start(z_dram[bass.ds(pr, 1), :, i, t * CHUNK:(t + 1) * CHUNK]
                                 .rearrange("a p n -> (a p) n"), zs[:, n % 2, :]).then_inc(z_stored[n % 2], 16)
                for k in range(DIRS):
                    it = sp.snap(pr * DIRS + k)
                    sp.wait_ge(dt_ready, it * (3 * NCHUNK) + 1)
                    sp.dma_start(w_x[:], ap["L2_x"][k]).then_inc(wx_in, 16)
                    sp.wait_ge(split, it * SPLITS + SPLITS)
                    sp.wait_ge(y_ready, it * (3 * TILE_N) + RING)
                    for dst, row in ((bs, 32), (cs, 48)):
                        for e in range(2):
                            for i in range(3):
                                at = 48 * e + 16 * i
                                sp.dma_start(dst[at:at + 16, :],
                                             part[i][64 * e + row:64 * e + row + 16, :]).then_inc(gathered, 16)
                    with sp.Fori(0, 3) as i:
                        sp.wait_ge(dt_ready, it * (3 * NCHUNK) + i * NCHUNK + 1)
                        sp.dma_start(w_dt[:], ap["L2_dt"][k][bass.ds(i, 1), :, :].rearrange("a p n -> (a p) n"))\
                          .then_inc(wdt_in, 16)
                sp.wait_ge(y_added, pr * (DIRS * 3 * NSPAN) + DIRS * 3 * NSPAN + 1)
                for s in range(2):
                    sp.wait_ge(z_stored[s], pr * (16 * ZUSES[s]) + 16 * ZUSES[s])

                def load(t):
                    s = t % 2
                    sp.dma_start(zc[:, 3 * s:3 * s + 3, :],
                                 z_dram[bass.ds(pr, 1), :, :, t * CHUNK:(t + 1) * CHUNK]
                                 .rearrange("a p i n -> (a p) i n")).then_inc(fin_in, 16)
                    for place, src in image_parts(x_in, pr, lambda i: xr[:, 3 * s + i, :], t * CHUNK, CHUNK):
                        sp.dma_start(place, src).then_inc(fin_in, 16)

                load(0)
                for t in range(NCHUNK):
                    s = t % 2
                    if t + 1 < NCHUNK:
                        sp.wait_ge(fin_in, pr * (80 * NCHUNK) + 80 * (t + 1))
                        if t >= 1:
                            sp.wait_ge(out_done, pr * NCHUNK + t + 1)
                        load(t + 1)
                    sp.wait_ge(out_done, pr * NCHUNK + t + 2)
                    for place, dst in image_parts(x_out, pr, lambda i: oc[:, 3 * s + i, :], t * CHUNK, CHUNK):
                        sp.dma_start(dst, place).then_inc(x_stored[s], 16)
            for s in range(2):
                sp.wait_ge(x_stored[s], 64 * OUSES[s] * PAIRS + 64)

        @block.gpsimd
        def _(pool):
            pool.sem_inc(kept, STATES)
            pool.sem_inc(hc_done, RING)
            pool.wait_ge(made, 1)
            with pool.Fori(0, PAIRS) as pr:
                pool.wait_ge(out_done, pr * NCHUNK + 1)
                for s in range(2):
                    pool.wait_ge(x_stored[s], pr * (64 * OUSES[s]) + 64)
                steady(pool)
                pool.memset(pad[:], 0.0).then_inc(bordered, 1)
                with pool.Fori(0, DIRS * 3 * NSPAN) as sp_:
                    n0 = pool.snap((pr * (DIRS * 3 * NSPAN) + sp_) * STATES)
                    for n in range(STATES):
                        r = n % RING
                        pool.wait_ge(scanned, n0 + (n + 1 + RING))
                        steady(pool)
                        pool.tensor_copy(state[:, n:n + 1], hs[:, r, SPAN - 1:SPAN]).then_inc(kept, 1)
                        pool.wait_ge(c_out, n0 + (n + 1))
                        pool.wait_ge(y_ready, n0 + (n + 1))
                        pool.tensor_tensor(hc[:, r, :], hs[:, r, :], cb[:, n % 2, :], ALU.mult).then_inc(hc_done, 1)

        @block.tensor
        def _(pe):
            pe.sem_inc(dt_ready, 1)
            pe.sem_inc(y_ready, RING)
            pe.wait_ge(const_in, 16 * CONSTS)
            pe.wait_ge(made, 1)

            def mix(w, src, out_of, i):
                for q, (w_i, s_i) in enumerate(MIX[i]):
                    mm = pe.matmul(out_of, w[:, w_i, :], src(s_i), start=(q == 0), stop=(q == len(MIX[i]) - 1))
                return mm

            with pe.Fori(0, PAIRS) as pr:
                pe.wait_ge(out_done, pr * NCHUNK + 1)
                pe.wait_ge(step, pr * STEPS + 4)
                for i in range(3):
                    mm = mix(w_gn, lambda s: mv[:, s, :], ps[:, 7, 2 * i:2 * i + 2], i)
                mm.then_inc(gn_ready, 1)
                pe.wait_ge(normed, pr * 3 + 3)
                out0 = pe.snap(pr * MIXES)
                for n in range(MIXES):
                    i, q = n // (2 * NCHUNK), n % (2 * NCHUNK)
                    t = q % NCHUNK
                    if n >= 4:
                        pe.wait_ge(mix_out, out0 + (n - 4 + 2))
                    mix(w_z if q < NCHUNK else w_ssm, lambda s: xn[:, s, t * CHUNK:(t + 1) * CHUNK],
                        ps[:, n % 4, 0:CHUNK], i).then_inc(mix_ready, 1)

                for k in range(DIRS):
                    it = pe.snap(pr * DIRS + k)
                    pe.wait_ge(wx_in, it * 16 + 16)
                    pe.wait_ge(xc_done, pr * 3 + 3)
                    for t in range(NCHUNK):
                        if t >= 2:
                            pe.wait_ge(f_out, it * NCHUNK + (t - 1))
                        for i in range(3):
                            mm = pe.matmul(ps[:, t % 2, 0:CHUNK], w_x[:, i, :],
                                           scan_view(xc[:, i, :], k)[:, 8 * t:8 * t + 8, :],
                                           start=(i == 0), stop=(i == 2))
                        mm.then_inc(f_ready, 1)
                    pe.wait_ge(f_out, it * NCHUNK + NCHUNK)
                    pe.wait_ge(gathered, it * GATHER + GATHER)
                    steady(pe)
                    with pe.Fori(0, 3) as i:
                        ti = pe.snap(it * 3 + i)
                        sp0 = pe.snap(ti * (4 * NCHUNK))
                        pe.wait_ge(wdt_in, ti * 16 + 16)
                        for t in range(NCHUNK):
                            if t >= 2:
                                pe.wait_ge(sp_done, sp0 + (3 * (t - 1)))
                            pe.matmul(ps[:, t % 2, 0:CHUNK], w_dt[:], f[:, t * CHUNK:(t + 1) * CHUNK],
                                      start=True, stop=True).then_inc(dt_ready, 1)
                        pe.wait_ge(sp_done, sp0 + 3 * NCHUNK)
                        steady(pe)

                        def spread(rows, c, n, bank):
                            at = (c + n // STATES) * SPAN
                            for h in range(2):
                                mm = pe.matmul(ps[:, bank + h, 0:HSPAN],
                                               sel[:, bass.ds(i, 1), n % STATES, :].rearrange("p a m -> p (a m)"),
                                               rows[:, bass.ds(at + h * HSPAN, HSPAN)], start=True, stop=True)
                            return mm

                        def b_row(c, n, n0):
                            if n >= 2:
                                pe.wait_ge(b_done, n0 + (n - 1))
                                steady(pe)
                            spread(bs, c, n, 2 * (n % 2)).then_inc(b_ready, 1)

                        def c_row(c, n, n0):
                            if n >= 1:
                                pe.wait_ge(c_out, n0 + n)
                                steady(pe)
                            spread(cs, c, n, 4).then_inc(c_ready, 1)

                        def sum_span(c, last):
                            n0 = pe.snap((ti * NSPAN + c) * STATES)
                            ahead = 0 if last else 2

                            def share(n):
                                pe.wait_ge(hc_done, n0 + (n + 1 + RING))
                                if n == 0:
                                    pe.wait_ge(y_added, ti * NSPAN + c + 1)
                                for h in range(2):
                                    mm = pe.matmul(ps[:, 6 + h, 0:HSPAN], ident[:],
                                                   hc[:, n % RING, h * HSPAN:(h + 1) * HSPAN],
                                                   start=(n == 0), stop=(n == STATES - 1))
                                mm.then_inc(y_ready, 1)

                            for n in range(STATES):
                                if n + 2 < STATES + ahead:
                                    b_row(c, n + 2, n0)
                                if n + 1 < STATES + ahead:
                                    c_row(c, n + 1, n0)
                                if n >= 1:
                                    share(n - 1)
                            share(STATES - 1)

                        b_row(0, 0, None)
                        c_row(0, 0, None)
                        b_row(0, 1, None)
                        with pe.Fori(0, NSPAN - 1) as c:
                            sum_span(c, False)
                        sum_span(NSPAN - 1, True)
                pe.wait_ge(y_added, (pr + 1) * (DIRS * 3 * NSPAN) + 1)
                for t in range(NCHUNK):
                    lo, hi = t * CHUNK, (t + 1) * CHUNK
                    l0 = pe.snap(pr * (LNS * NCHUNK) + t * LNS)
                    if t:
                        pe.wait_ge(out_done, pr * NCHUNK + t + 1)
                    for i in range(3):
                        mm = mix(w_ln, lambda s: y[:, s, lo:hi], ps[:, i, 0:CHUNK], i)
                    mm.then_inc(ln_ready, 1)
                    pe.wait_ge(ln_act, pr * (2 * NCHUNK) + 2 * t + 1)
                    for i in range(3):
                        mm = mix(w_ln, lambda s: squ[:, s, :], ps[:, 3 + i, 0:CHUNK], i)
                    mm.then_inc(ln_ready, 1)
                    pe.wait_ge(ln_step, l0 + LNS)
                    for i in range(3):
                        mm = mix(w_out, lambda s: dev[:, s, :], ps[:, i, 0:CHUNK], i)
                    mm.then_inc(ln_ready, 1)

        @block.scalar
        def _(act):
            act.sem_inc(mix_out, 1)
            act.wait_ge(const_in, 16 * CONSTS)
            act.activation(vec[:, :, V_A:V_END], vec[:, :, V_A:V_END], ACT.Exp).then_inc(exp_made, 1)
            act.wait_ge(made2, 1)
            act.activation(ln1[:], ln1[:], ACT.Ln, bias=1.0).then_inc(exp_made, 1)
            act.wait_ge(made, 1)
            with act.Fori(0, PAIRS) as pr:
                act.wait_ge(step, pr * STEPS + 9)
                act.activation(rstd[:], gv[:], ACT.Sqrt).then_inc(rstd_done, 1)
                mix0 = act.snap(pr * MIXES)

                def silu_xc(i):
                    act.wait_ge(tap_done, pr * (3 * TAPS9) + (TAPS9 * (i + 1) + 1))
                    act.activation(xc[:, i, :], xc[:, i, :], ACT.Silu).then_inc(xc_done, 1)

                for n in range(MIXES):
                    i, q = n // (2 * NCHUNK), n % (2 * NCHUNK)
                    t = q % NCHUNK
                    if q < NCHUNK:
                        zi = NCHUNK * i + t
                        if zi >= 2:
                            act.wait_ge(z_stored[zi % 2], pr * (16 * ZUSES[zi % 2]) + 16 * (zi // 2))
                        act.wait_ge(mix_ready, mix0 + (n + 1))
                        act.activation(zs[:, zi % 2, :], ps[:, n % 4, 0:CHUNK], ACT.Silu).then_inc(mix_out, 1)
                    else:
                        if t == 0 and i:
                            silu_xc(i - 1)
                        if t == 0 and not i:
                            act.wait_ge(bordered, pr + 1)
                        act.wait_ge(mix_ready, mix0 + (n + 1))
                        act.copy(pad[:, 1 + 8 * t:9 + 8 * t, 1:1 + SIDE],
                                 ps[:, n % 4, 0:CHUNK].rearrange("p (h w) -> p h w", w=SIDE)).then_inc(mix_out, 1)
                silu_xc(2)

                for k in range(DIRS):
                    it = act.snap(pr * DIRS + k)
                    for t in range(NCHUNK):
                        act.wait_ge(f_ready, it * NCHUNK + (t + 1))
                        act.copy(f[:, t * CHUNK:(t + 1) * CHUNK], ps[:, t % 2, 0:CHUNK]).then_inc(f_out, 1)
                    with act.Fori(0, 3) as i:
                        ti = act.snap(it * 3 + i)
                        sp0 = act.snap(ti * (4 * NCHUNK))
                        sp1 = act.snap(sp0 + 3 * NCHUNK)
                        dt0 = act.snap(ti * NCHUNK + 1)
                        d0 = act.snap(ti * (5 * NCHUNK))
                        bias = dtb[:, bass.ds(i * DIRS + k, 1)]
                        act.wait_ge(gathered, it * GATHER + GATHER)
                        for t in range(NCHUNK):
                            s = t % 2
                            act.wait_ge(dt_ready, dt0 + (t + 1))
                            span = slice(t * CHUNK, (t + 1) * CHUNK)
                            if t >= 2:
                                act.wait_ge(sp_done, sp0 + (3 * (t - 1)))
                            steady(act)
                            act.activation(t_abs[:, s, :], ps[:, s, 0:CHUNK], ACT.Abs, bias=bias).then_inc(sp_done, 1)
                            act.activation(d[:, span], ps[:, s, 0:CHUNK], ACT.Relu, bias=bias).then_inc(sp_done, 1)
                            act.wait_ge(sp_done, sp0 + (3 * t + 1))
                            act.activation(du[:, span], t_abs[:, s, :], ACT.Exp, scale=-1.0).then_inc(sp_done, 1)
                        for t in range(NCHUNK):
                            s = t % 2
                            act.wait_ge(sp_done, sp0 + (3 * t + 3))
                            if t >= 2:
                                act.wait_ge(d_step, d0 + (5 * (t - 2) + 2))
                            act.activation(t_ln[:, s, :], du[:, t * CHUNK:(t + 1) * CHUNK], ACT.Ln, bias=1.0)\
                               .then_inc(sp_done, 1)
                        act.wait_ge(d_step, d0 + 5 * NCHUNK)
                        for h in range(2):
                            act.wait_ge(z_stored[h], (pr + 1) * (16 * ZUSES[h]))

                        def decay(c, n, n0):
                            act.wait_ge(scanned, n0 + (n + 3))
                            steady(act)
                            act.activation(da[:, n % 2, :], d[:, bass.ds((c + n // STATES) * SPAN, SPAN)], ACT.Exp,
                                           scale=nega[:, bass.ds(i * (DIRS * STATES) + (k * STATES + n % STATES), 1)])\
                               .then_inc(a_ready, 1)

                        def decay_span(c, last):
                            n0 = act.snap((ti * NSPAN + c) * STATES)
                            for n in range(STATES):
                                if n + 1 < STATES or not last:
                                    decay(c, n + 1, n0)
                                act.wait_ge(c_ready, n0 + (n + 1))
                                act.wait_ge(hc_done, n0 + (n + 3))
                                act.copy(cb[:, n % 2, :].rearrange("p (a n) -> p a n", a=2),
                                         ps[:, 4:6, 0:HSPAN]).then_inc(c_out, 1)

                        decay(0, 0, act.snap(ti * (NSPAN * STATES)))
                        with act.Fori(0, NSPAN - 1) as c:
                            decay_span(c, False)
                        decay_span(NSPAN - 1, True)
                for t in range(NCHUNK):
                    l0 = act.snap(pr * (LNS * NCHUNK) + t * LNS)
                    act.wait_ge(ln_step, l0 + 1)
                    act.activation(squ[:], dev[:], ACT.Square).then_inc(ln_act, 1)
                    act.wait_ge(ln_step, l0 + 3)
                    act.activation(rs[:], rs[:], ACT.Sqrt).then_inc(ln_act, 1)

        @block.vector
        def _(dve):
            dve.sem_inc(tap_done, 1)
            dve.sem_inc(scanned, RING)
            dve.sem_inc(y_added, 1)
            dve.sem_inc(out_done, 1)
            dve.sem_inc(x_stored[0], 64)
            dve.sem_inc(x_stored[1], 64)
            dve.wait_ge(const_in, 16 * CONSTS)
            dve.memset(ln1[:], 0.0).then_inc(made2, 1)
            dve.tensor_copy(sel[:], sel_f).then_inc(made2, 1)
            dve.tensor_tensor(dsum[:], vec[:, :, V_D], vec[:, :, V_D + 1], ALU.add).then_inc(made2, 1)
            for q in (2, 3):
                dve.wait_ge(made2, q + 1)
                dve.tensor_tensor(dsum[:], dsum[:], vec[:, :, V_D + q], ALU.add).then_inc(made2, 1)
            dve.tensor_tensor(dtb[:].rearrange("p (i k) -> p i k", i=3), vec[:, :, V_DT:V_A],
                              vec[:, :, V_DT:V_A], ALU.add).then_inc(made2, 1)
            dve.wait_ge(exp_made, 2)
            dve.tensor_scalar(nega[:].rearrange("p (i n) -> p i n", i=3), vec[:, :, V_A:V_END], -1.0, None,
                              ALU.mult).then_inc(made2, 1)
            dve.wait_ge(made2, 7)
            dve.sem_inc(made, 1)

            with dve.Fori(0, PAIRS) as pr:
                done = [0]
                step0 = dve.snap(pr * STEPS)

                def own(ins):
                    done[0] += 1
                    ins.then_inc(step, 1)
                    dve.wait_ge(step, step0 + done[0])

                dve.wait_ge(x_loaded, pr * 64 + 64)
                for i in range(3):
                    for t in range(NCHUNK):
                        ins = dve.bn_stats(bn[:, i, t, :], xn[:, i, t * CHUNK:(t + 1) * CHUNK])
                own(ins)
                steady(dve)
                for i in range(3):
                    ins = dve.bn_aggr(mv[:, i, :], bn[:, i, :, :].rearrange("p t s -> p (t s)"))
                own(ins)
                own(dve.tensor_tensor(m2[:], mv[:, :, 0], mv[:, :, 0], ALU.mult))
                own(dve.tensor_tensor(mv[:, :, 1], mv[:, :, 1], m2[:], ALU.add))
                dve.wait_ge(gn_ready, pr + 1)
                own(dve.tensor_copy(gs[:], ps[:, 7, 0:6]))
                own(dve.tensor_tensor(m2[:], gs[:, 0:6:2], gs[:, 0:6:2], ALU.mult))
                own(dve.tensor_tensor(gv[:], gs[:, 1:6:2], m2[:], ALU.subtract))
                own(dve.tensor_scalar(gv[:], gv[:], GN_EPS, None, ALU.add))
                own(dve.reciprocal(gv[:], gv[:]))
                dve.wait_ge(rstd_done, pr + 1)
                own(dve.scalar_tensor_tensor(out=shift[:], in0=gs[:, 0:6:2], scalar=-1.0, in1=rstd[:],
                                             op0=ALU.mult, op1=ALU.mult))
                assert done[0] == STEPS
                for i in range(3):
                    dve.tensor_scalar(xn[:, i, :], xn[:, i, :], rstd[:, i:i + 1], shift[:, i:i + 1],
                                      ALU.mult, ALU.add).then_inc(normed, 1)
                tap0 = dve.snap(pr * (3 * TAPS9) + 1)
                for i in range(3):
                    dve.wait_ge(mix_out, pr * MIXES + (2 * NCHUNK * (i + 1) + 1))
                    acc = xc[:, i, :].rearrange("p (h w) -> p h w", w=SIDE)
                    for q in range(TAPS9):
                        src = pad[:, q // 3:q // 3 + SIDE, q % 3:q % 3 + SIDE]
                        w = vec[:, i, V_CONV + q:V_CONV + q + 1]
                        if q == 0:
                            dve.tensor_scalar(acc, src, w, vec[:, i, V_CB:V_CB + 1], ALU.mult, ALU.add)\
                               .then_inc(tap_done, 1)
                        else:
                            dve.wait_ge(tap_done, tap0 + (TAPS9 * i + q))
                            dve.scalar_tensor_tensor(out=acc, in0=src, scalar=w, in1=acc, op0=ALU.mult,
                                                     op1=ALU.add).then_inc(tap_done, 1)
                for i in range(3):
                    dve.wait_ge(xc_done, pr * 3 + (i + 1))
                    dve.tensor_scalar(y[:, i, :], xc[:, i, :], dsum[:, i:i + 1], None, ALU.mult).then_inc(y_init, 1)

                for k in range(DIRS):
                    it = dve.snap(pr * DIRS + k)
                    split0 = dve.snap(it * SPLITS)
                    dve.wait_ge(f_out, it * NCHUNK + NCHUNK)
                    dve.tensor_copy(part[0], f).then_inc(split, 1)
                    dve.wait_ge(split, split0 + 1)
                    dve.tensor_tensor(rest, f, part[0], ALU.subtract).then_inc(split, 1)
                    dve.wait_ge(split, split0 + 2)
                    dve.tensor_copy(part[1], rest).then_inc(split, 1)
                    dve.wait_ge(split, split0 + 3)
                    dve.tensor_tensor(part[2], rest, part[1], ALU.subtract).then_inc(split, 1)
                    dve.wait_ge(y_init, pr * 3 + 3)
                    steady(dve)
                    with dve.Fori(0, 3) as i:
                        ti = dve.snap(it * 3 + i)
                        sp0 = dve.snap(ti * (4 * NCHUNK))
                        d0 = dve.snap(ti * (5 * NCHUNK))
                        u_k = image_view(tile(xc, i), k)
                        for t in range(NCHUNK):
                            s = t % 2
                            span = slice(t * CHUNK, (t + 1) * CHUNK)

                            def own5(q):
                                dve.wait_ge(d_step, d0 + (5 * t + q))

                            dve.wait_ge(sp_done, sp0 + (3 * NCHUNK + t + 1))
                            dve.tensor_scalar(t_abs[:, s, :], du[:, span], 1.0, -1.0, ALU.add, ALU.add)\
                               .then_inc(d_step, 1)
                            dve.scalar_tensor_tensor(out=d[:, span], in0=t_ln[:, s, :], scalar=ln1[:],
                                                     in1=d[:, span], op0=ALU.subtract, op1=ALU.add)\
                               .then_inc(d_step, 1)
                            own5(1)
                            dve.tensor_tensor(t_abs[:, s, :], du[:, span], t_abs[:, s, :], ALU.subtract)\
                               .then_inc(d_step, 1)
                            own5(3)
                            dve.tensor_tensor(d[:, span], t_abs[:, s, :], d[:, span], ALU.add).then_inc(d_step, 1)
                            own5(4)
                            du_t, d_t = (v[:, span].rearrange("p (a b) -> p a b", b=SIDE) for v in (du, d))
                            row = 8 * t
                            if k % 2:
                                du_t, d_t, row = du_t[:, ::-1, ::-1], d_t[:, ::-1, ::-1], SIDE - 8 - 8 * t
                            dve.tensor_tensor(du_t, d_t, u_k[:, row:row + 8, :], ALU.mult).then_inc(d_step, 1)
                        dve.wait_ge(d_step, d0 + 5 * NCHUNK)
                        dve.wait_ge(kept, ti * TILE_N + STATES)
                        steady(dve)
                        dve.memset(state[:], 0.0).then_inc(zeroed, 1)
                        dve.wait_ge(zeroed, ti + 1)
                        steady(dve)

                        def times_b(c, n, n0):
                            dve.wait_ge(b_ready, n0 + (n + 1))
                            dve.wait_ge(scanned, n0 + (n + 1))
                            b = 2 * (n % 2)
                            dve.tensor_tensor(db[:, n % RING, :].rearrange("p (a n) -> p a n", a=2),
                                              ps[:, b:b + 2, 0:HSPAN],
                                              du[:, bass.ds((c + n // STATES) * SPAN, SPAN)]
                                              .rearrange("p (a n) -> p a n", a=2), ALU.mult).then_inc(b_done, 1)

                        def add_y(c):
                            dve.wait_ge(y_ready, ti * TILE_N + (c * STATES + (STATES + RING)))
                            rows = SPAN // SIDE
                            total = ps[:, 6:8, 0:HSPAN].rearrange("p a (r w) -> p a r w", w=SIDE)
                            row = c * rows
                            if k % 2:
                                total, row = total[:, ::-1, ::-1, ::-1], c * -rows + (SIDE - rows)
                            place = image_view(tile(y, i), k)[:, bass.ds(row, rows), :]\
                                .rearrange("p (a r) w -> p a r w", a=2)
                            dve.tensor_tensor(place, place, total, ALU.add).then_inc(y_added, 1)

                        def scan_span(c, first, last):
                            n0 = dve.snap((ti * NSPAN + c) * STATES)
                            for n in range(STATES):
                                if n + 1 < STATES or not last:
                                    times_b(c, n + 1, n0)
                                dve.wait_ge(a_ready, n0 + (n + 1))
                                dve.wait_ge(b_done, n0 + (n + 1))
                                dve.wait_ge(kept, n0 + (n + 1))
                                dve.wait_ge(hc_done, n0 + (n + 1))
                                dve.tensor_tensor_scan(hs[:, n % RING, :], da[:, n % 2, :], db[:, n % RING, :],
                                                       state[:, n:n + 1], ALU.mult, ALU.add).then_inc(scanned, 1)
                                if n == 1 and not first:
                                    add_y(c - 1)

                        times_b(0, 0, dve.snap(ti * TILE_N))
                        scan_span(0, True, False)
                        with dve.Fori(1, NSPAN - 1) as c:
                            scan_span(c, False, False)
                        scan_span(NSPAN - 1, False, True)
                        add_y(NSPAN - 1)
                dve.wait_ge(y_added, (pr + 1) * (DIRS * 3 * NSPAN) + 1)
                for t in range(NCHUNK):
                    s = t % 2
                    l0 = dve.snap(pr * (LNS * NCHUNK) + t * LNS)
                    ready0 = dve.snap(pr * (3 * NCHUNK) + 3 * t)
                    chunk = y[:, :, t * CHUNK:(t + 1) * CHUNK]
                    dve.wait_ge(ln_ready, ready0 + 1)
                    dve.tensor_tensor(dev[:], chunk, ps[:, 0:3, 0:CHUNK], ALU.subtract).then_inc(ln_step, 1)
                    dve.wait_ge(ln_ready, ready0 + 2)
                    dve.tensor_scalar(rs[:], ps[:, 3:6, 0:CHUNK], LN_EPS, None, ALU.add).then_inc(ln_step, 1)
                    dve.wait_ge(ln_step, l0 + 2)
                    dve.reciprocal(rs[:], rs[:]).then_inc(ln_step, 1)
                    dve.wait_ge(ln_act, pr * (2 * NCHUNK) + 2 * t + 2)
                    dve.tensor_tensor(dev[:], dev[:], rs[:], ALU.mult).then_inc(ln_step, 1)
                    dve.wait_ge(ln_step, l0 + 4)
                    for i in range(3):
                        dve.tensor_scalar(dev[:, i, :], dev[:, i, :], vec[:, i, V_G:V_G + 1], vec[:, i, V_B:V_B + 1],
                                          ALU.mult, ALU.add).then_inc(ln_step, 1)
                    dve.wait_ge(ln_step, l0 + 7)
                    dve.wait_ge(fin_in, pr * (80 * NCHUNK) + 80 * (t + 1))
                    dve.tensor_tensor(dev[:], dev[:], zc[:, 3 * s:3 * s + 3, :], ALU.mult).then_inc(ln_step, 1)
                    dve.wait_ge(ln_ready, ready0 + 3)
                    dve.wait_ge(x_stored[s], pr * (64 * OUSES[s]) + (64 * (t // 2) + 64))
                    dve.tensor_tensor(oc[:, 3 * s:3 * s + 3, :], xr[:, 3 * s:3 * s + 3, :], ps[:, 0:3, 0:CHUNK],
                                      ALU.add).then_inc(out_done, 1)


def host_layout(arrays):
    import numpy as np

    f = {k: np.asarray(v) for k, v in arrays.items()}
    out = {"x": np.ascontiguousarray(f["x"].reshape(8, TOK, CH).transpose(0, 2, 1))}
    for tag in ("L0", "L1"):
        a = lambda n: f[f"{tag}_conv_{n}"]
        w = np.zeros((GROUPS, HALF, WCOLS + 3), np.float32)
        for kind, n in enumerate("qvp"):
            v = a(f"{n}_w").reshape(GROUPS, HALF, 2, HALF).transpose(0, 3, 2, 1)
            for j in range(2):
                w[:, :, (3 * j + kind) * HALF:(3 * j + kind + 1) * HALF] = v[:, :, j, :]
            w[:, :, BIAS + kind] = a(f"{n}_b").reshape(GROUPS, HALF)
        out[f"{tag}_w"] = w
        out[f"{tag}_ow"] = np.ascontiguousarray(a("o_w").T.reshape(GROUPS, HALF, CH))
        out[f"{tag}_ob"] = np.ascontiguousarray(a("o_b").reshape(2, HALF).T)
        out[f"{tag}_slope"] = np.ascontiguousarray(a("slope").reshape(GROUPS, HALF).T)
        for k in (1, 2):
            h = np.zeros((32, 96 + D1 + 4), np.float32)
            for i in range(3):
                h[:, 32 * i:32 * i + 32] = a(f"t{k}_ws")[i].T
                h[:, 96 + D1 + 1 + i] = a(f"t{k}_bs")[i]
            h[:, 96:96 + D1] = a(f"t{k}_wo").T
            h[:, 96 + D1] = a(f"t{k}_b0")
            out[f"{tag}_t{k}_hid"] = h
            out[f"{tag}_t{k}_w0"] = np.ascontiguousarray(a(f"t{k}_w0").T)
            out[f"{tag}_t{k}_bo"] = np.ascontiguousarray(a(f"t{k}_bo").reshape(GROUPS, HALF).T)
    nei = np.array([[2, 1], [1, 2], [0, 2], [0, 1], [1, 0], [2, 0]])
    k, s = np.arange(12) % 6, np.arange(12) // 6
    sign = np.where(s == 0, 1, -1)
    act = (k[:, None] + sign[:, None] * np.arange(6)[None, :]) % 6
    mult = (k[:, None] + sign[:, None] * k[None, :]) % 6 + 6 * (s[:, None] ^ s[None, :])
    ke = np.zeros((3, 3, 12, 16, 12, 16), np.float32)
    kern = f["L3_conv_kernel"]
    for g in range(12):
        for t in range(7):
            yy, xx = (1, 1) if t == 0 else nei[act[g, t - 1]]
            for h in range(12):
                ke[yy, xx, mult[g, h], :, g, :] = kern[t, h]
    ke = ke.reshape(3, 3, CH, CH)
    out["L3_w"] = np.ascontiguousarray(
        np.stack([ke[dy, dx].reshape(2, HALF, CH) for dy, dx in TAPS]).transpose(2, 1, 0, 3))
    a = lambda n: f[f"L2_conv_{n}"]

    def mixed(w):
        o = np.zeros((128, 6, 128), np.float32)
        o[:, 0] = w[:128, :128]
        o[:64, 1] = o[64:, 2] = w[128:, :128]
        o[:, 3, :64] = o[:, 4, 64:] = w[:128, 128:]
        o[:64, 5, :64] = o[64:, 5, 64:] = w[128:, 128:]
        return o

    def tiled(v):
        return np.stack([v[:128], v[:128], np.concatenate([v[128:], v[128:]])], 1)

    out["L2_ssm"], out["L2_z"] = mixed(a("in_proj_w")[:, :CH]), mixed(a("in_proj_w")[:, CH:])
    out["L2_out"] = mixed(a("out_w"))
    c = np.arange(CH)
    out["c_mixgn"] = mixed(((c[:, None] // 6 == c[None] // 6) / 6.0).astype(np.float32))
    out["c_mixln"] = mixed(np.full((CH, CH), 1.0 / CH, np.float32))
    out["L2_vec"] = np.ascontiguousarray(tiled(np.concatenate(
        [a("conv_w").reshape(CH, 9), a("conv_b")[:, None], a("ln_g")[:, None], a("ln_b")[:, None], a("Ds").T,
         a("dt_b").T, a("A_logs").transpose(1, 0, 2).reshape(CH, DIRS * STATES)], 1)))
    wx = np.zeros((DIRS, 128, 3, 128), np.float32)
    wdt = np.zeros((DIRS, 3, 128, 128), np.float32)
    for k in range(DIRS):
        w = np.zeros((CH, 64), np.float32)
        w[:, :RANK], w[:, 32:64] = a("x_proj_w")[k][:, :RANK], a("x_proj_w")[k][:, RANK:]
        wx[k, :, 0, :64] = wx[k, :, 1, 64:] = w[:128]
        wx[k, :64, 2, :64] = wx[k, 64:, 2, 64:] = w[128:]
        dt = a("dt_w")[k]
        wdt[k, 0, :RANK] = wdt[k, 1, 64:64 + RANK] = dt[:, :128]
        wdt[k, 2, :RANK, :64] = wdt[k, 2, 64:64 + RANK, 64:] = dt[:, 128:]
    out["L2_x"], out["L2_dt"] = wx, wdt
    sel = np.zeros((2, 3, STATES, 3, STATES, 128), np.float32)
    for n in range(STATES):
        sel[0, :, n, 0, n, :] = sel[1, :, n, 1, n, :] = 1.0
        sel[0, :, n, 2, n, :64] = sel[1, :, n, 2, n, 64:] = 1.0
    out["c_sel"] = sel.reshape(96, 3, STATES, 128)
    lag = np.arange(LAGS) - (SIDE - 1)
    out["c_pos"] = np.where(lag == SIDE, 0, np.where(lag >= 0, lag, -(SIDE + lag))).astype(np.float32)[None]
    out["c_expo"] = np.tile(np.where(lag == SIDE, 0, np.abs(lag)).astype(np.float32), (HALF, 1))
    out["c_ident"] = np.eye(128, dtype=np.float32)
    c = np.arange(HALF)
    out["c_gmean"] = ((c[:, None] // 6 == c[None] // 6) / 6.0).astype(np.float32)
    return out


def tno_program(nc, sems, ap, tag, x_out, x_in=None):
    consts = {k: ap[f"c_{k}"] for k in ("pos", "expo", "ident", "gmean")}
    lag = [nc.dram_tensor(f"{tag}_lag{k}", (D1, LAGS), F32).ap() for k in range(2)]
    table = [nc.dram_tensor(f"{tag}_table{k}", (SIDE, D1, SIDE), F32).ap() for k in range(2)]
    mlp = [{n: ap[f"{tag}_t{k}_{n}"] for n in ("w0", "hid", "bo")} for k in (1, 2)]
    toeplitz_tables(nc, sems, tag + "t", mlp, ap[f"{tag}_slope"], consts["pos"], consts, lag, table)
    tno_layer(nc, sems, tag, ap["x"] if x_in is None else x_in, x_out, ap[f"{tag}_w"], ap[f"{tag}_ow"],
              ap[f"{tag}_ob"], table, consts)


def network(nc, ap, out):
    consts = {k: ap[f"c_{k}"] for k in ("pos", "expo", "ident", "gmean")}
    x1, x2, x3 = (nc.dram_tensor(n, (BATCH, CH, TOK), F32).ap() for n in ("x1", "x2", "x3"))
    z = nc.dram_tensor("z", (PAIRS, 128, 3, TOK), F32).ap()
    with ExitStack() as sems:
        tno_program(nc, sems, ap, "L0", x1)
        tno_program(nc, sems, ap, "L1", x2, x1)
        scan_layer(nc, sems, "L2", x2, x3, ap, z, consts)
        conv_layer(nc, sems, "L3", x3, out, ap["L3_w"], consts)


def kernel(**inputs):
    import numpy as np
    import concourse.bacc as bacc
    from concourse.bass_utils import run_bass_kernel_spmd

    arrays = host_layout(inputs)
    nc = bacc.Bacc("TRN2", target_bir_lowering=False, num_devices=1)
    ap = {n: nc.dram_tensor(n, a.shape, F32, kind="ExternalInput").ap() for n, a in arrays.items()}
    out = nc.dram_tensor("out", (BATCH, CH, TOK), F32, kind="ExternalOutput").ap()
    network(nc, ap, out)
    r = run_bass_kernel_spmd(nc, [arrays], core_ids=[0])
    y = np.asarray(r.results[0]["out"]).reshape(BATCH, CH, TOK)
    return np.ascontiguousarray(y.transpose(0, 2, 1)).reshape(BATCH, SIDE, SIDE, CH)
```

```python
from contextlib import ExitStack

import concourse.bass as bass
from concourse import mybir

F32 = mybir.dt.float32
F32R = mybir.dt.float32r
BF16 = mybir.dt.bfloat16
ALU = mybir.AluOpType
ACT = mybir.ActivationFunctionType

BATCH, SIDE, CH = 8, 56, 192
TOK = SIDE * SIDE
HALF = CH // 2
D1 = 3 * CH
GROUPS = D1 // HALF
CHUNK = 8 * SIDE
NCHUNK = TOK // CHUNK
LAGS = 2 * SIDE
GN_EPS = 1e-5
BANK = 512

WCOLS = 2 * 3 * HALF
BIAS = WCOLS


class Pool:

    def __init__(self, nc, sems, tag):
        self.nc, self.sems, self.tag, self.ctx = nc, sems, tag, ExitStack()

    def sb(self, name, shape, dt=F32):
        return self.ctx.enter_context(self.nc.sbuf_tensor(f"{self.tag}.{name}", shape, dt))

    def ps(self, name, shape, dt=F32):
        return self.ctx.enter_context(self.nc.psum_tensor(f"{self.tag}.{name}", shape, dt))

    def sem(self, name):
        return self.sems.enter_context(self.nc.semaphore(f"{self.tag}.{name}"))


def toeplitz_tables(nc, sems, tag, mlp, slope, rpe, consts, lag_dram, table_dram):
    m = Pool(nc, sems, tag)
    with m.ctx:
        pos = m.sb("pos", [1, LAGS])
        expo = m.sb("expo", [HALF, LAGS])
        w0 = m.sb("w0", [1, 2, 32])
        hid = m.sb("hid", [32, 2, 3 * 32 + D1 + 4])
        bo = m.sb("bo", [HALF, 2, GROUPS])
        sl = m.sb("sl", [HALF, GROUPS])
        lnsl = m.sb("lnsl", [HALF, GROUPS])
        decay = m.sb("decay", [HALF, GROUPS, LAGS])
        h = m.sb("h", [32, 2, 4, LAGS])
        taps = m.sb("taps", [HALF, 2, GROUPS, LAGS])
        ph = m.ps("ph", [32, 2, BANK])
        pa = m.ps("pa", [HALF, 2, BANK])

        loaded = m.sem("loaded")
        hidden = m.sem("hidden")
        relu = m.sem("relu")
        clipped = m.sem("clipped")
        logged = m.sem("logged")
        decayed = m.sem("decayed")
        tap_ready = m.sem("tap_ready")
        tap_done = m.sem("tap_done")
        stored = m.sem("stored")
        skewed = m.sem("skewed")

        block = m.ctx.enter_context(nc.Block())

        @block.sync
        def _(sp):
            sp.dma_start(pos[:], rpe).then_inc(loaded, 16)
            sp.dma_start(expo[:], consts["expo"]).then_inc(loaded, 16)
            sp.dma_start(sl[:], slope).then_inc(loaded, 16)
            for k in range(2):
                sp.dma_start(w0[:, k, :], mlp[k]["w0"]).then_inc(loaded, 16)
                sp.dma_start(hid[:, k, :], mlp[k]["hid"]).then_inc(loaded, 16)
                sp.dma_start(bo[:, k, :], mlp[k]["bo"]).then_inc(loaded, 16)
            for k in range(2):
                sp.wait_ge(tap_done, GROUPS * (k + 1))
                sp.dma_start(lag_dram[k].rearrange("(g p) l -> p g l", p=HALF), taps[:, k, :, :]).then_inc(stored, 16)
                sp.wait_ge(stored, 16 * (k + 1))
                with sp.Fori(0, SIDE) as w:
                    sp.dma_start(table_dram[k][bass.ds(w, 1), :, :],
                                 lag_dram[k].unsqueeze(0)[:, :, bass.ds(SIDE - 1 - w, SIDE)]).then_inc(skewed, 16)
            sp.wait_ge(skewed, 16 * SIDE * 2)

        @block.tensor
        def _(pe):
            pe.wait_ge(loaded, 9 * 16)
            for k in range(2):
                for layer in range(4):
                    if k or layer:
                        pe.wait_ge(relu, 4 * k + layer)
                    if layer == 0:
                        pe.matmul(ph[:, k, 0:LAGS], w0[:, k, :], pos[:], start=True, stop=True).then_inc(hidden, 1)
                    else:
                        pe.matmul(ph[:, k, 0:LAGS], hid[:, k, 32 * (layer - 1):32 * layer], h[:, k, layer - 1, :],
                                  start=True, stop=True).then_inc(hidden, 1)
                pe.wait_ge(relu, 4 * k + 4)
                for g in range(GROUPS):
                    n = GROUPS * k + g
                    if n >= 2:
                        pe.wait_ge(tap_done, n - 1)
                    pe.matmul(pa[:, n % 2, 0:LAGS], hid[:, k, 96 + HALF * g:96 + HALF * (g + 1)], h[:, k, 3, :],
                              start=True, stop=True).then_inc(tap_ready, 1)

        @block.scalar
        def _(act):
            for k in range(2):
                for layer in range(4):
                    act.wait_ge(hidden, 4 * k + layer + 1)
                    act.activation(h[:, k, layer, :], ph[:, k, 0:LAGS], ACT.Relu,
                                   bias=hid[:, k, 96 + D1 + layer:97 + D1 + layer]).then_inc(relu, 1)
                if k == 0:
                    act.wait_ge(clipped, 2)
                    act.activation(lnsl[:], sl[:], ACT.Ln).then_inc(logged, 1)
                    act.wait_ge(logged, 1)
                    for g in range(GROUPS):
                        act.activation(decay[:, g, :], expo[:], ACT.Exp, scale=lnsl[:, g:g + 1]).then_inc(decayed, 1)

        @block.vector
        def _(dve):
            dve.wait_ge(loaded, 9 * 16)
            dve.tensor_scalar(sl[:], sl[:], 0.0, 1.0, ALU.max, ALU.min).then_inc(clipped, 1)
            dve.wait_ge(clipped, 1)
            dve.tensor_scalar(sl[:], sl[:], 1.0 - 0.95, 0.95, ALU.mult, ALU.add).then_inc(clipped, 1)
            dve.wait_ge(decayed, GROUPS)
            for k in range(2):
                for g in range(GROUPS):
                    n = GROUPS * k + g
                    dve.wait_ge(tap_ready, n + 1)
                    dve.scalar_tensor_tensor(out=taps[:, k, g, :], in0=pa[:, n % 2, 0:LAGS], scalar=bo[:, k, g:g + 1],
                                             in1=decay[:, g, :], op0=ALU.add, op1=ALU.mult).then_inc(tap_done, 1)


def tno_layer(nc, sems, tag, x_in, x_out, weights, out_w, out_b, tables, consts):
    m = Pool(nc, sems, tag)
    with m.ctx:
        x_res = m.sb("x_res", [HALF, 2, 2, TOK])
        x_hi = m.sb("x_hi", [HALF, 2, TOK], F32R)
        x_lo = m.sb("x_lo", [HALF, 2, TOK], F32R)
        p_all = m.sb("p_all", [HALF, TOK])
        qv = m.sb("qv", [HALF, TOK])
        sq = m.sb("sq", [HALF, 2, CHUNK])
        sv = m.sb("sv", [HALF, 2, CHUNK])
        left = m.sb("left", [128, HALF, SIDE])
        right = m.sb("right", [128, HALF, SIDE])
        t_w = left[0:SIDE, :, :]
        xh = left[64:64 + SIDE, :, :]
        xw = right[0:SIDE, :, :]
        t_h = right[64:64 + SIDE, :, :]
        wg = m.sb("wg", [HALF, WCOLS + 3])
        w_hi = m.sb("w_hi", [HALF, WCOLS], F32R)
        w_lo = m.sb("w_lo", [HALF, WCOLS], F32R)
        bias = m.sb("bias", [HALF, 3])
        wo = m.sb("wo", [HALF, CH])
        po = m.sb("po", [HALF, 2, CHUNK])
        ident = m.sb("ident", [HALF, HALF])
        gmean = m.sb("gmean", [HALF, HALF])
        ob = m.sb("ob", [HALF, 2])
        bn = m.sb("bn", [HALF, 2, NCHUNK, 6])
        mv = m.sb("mv", [HALF, 2, 2])
        m2 = m.sb("m2", [HALF, 2])
        gs = m.sb("gs", [HALF, 4])
        gv = m.sb("gv", [HALF, 2])
        rstd = m.sb("rstd", [HALF, 2])
        shift = m.sb("shift", [HALF, 2])

        p_proj = m.ps("p_proj", [128, 2, BANK])
        p_turn = m.ps("p_turn", [128, 4, BANK])
        p_back, p_toe = p_turn[:, 0:2, :], p_turn[:, 2:4, :]
        p_out = m.ps("p_out", [128, 2, BANK])

        const_in = m.sem("const_in")
        gap_zero = m.sem("gap_zero")
        x_loaded = m.sem("x_loaded")
        w_in = m.sem("w_in")
        w_taken = m.sem("w_taken")
        wo_in = m.sem("wo_in")
        t_in = m.sem("t_in")
        x_stored = m.sem("x_stored")
        passed = m.sem("passed")
        step = m.sem("step")
        group_stats = m.sem("group_stats")
        rstd_done = m.sem("rstd_done")
        scaled = m.sem("scaled")
        normed = m.sem("normed")
        normed_bias = m.sem("normed_bias")
        proj_ready = m.sem("proj_ready")
        silu_done = m.sem("silu_done")
        qv_done = m.sem("qv_done")
        turn_ready = m.sem("turn_ready")
        turned = [m.sem(f"turned{s}") for s in range(2)]
        toe_ready = m.sem("toe_ready")
        toe_done = [m.sem(f"toe_done{s}") for s in range(2)]
        po_done = m.sem("po_done")
        out_ready = m.sem("out_ready")
        added = m.sem("added")

        PROJ = 3 * NCHUNK
        TURNS = 28
        HTURNS = TURNS // 2
        TOES = HALF // 8
        HTOES = TOES // 2
        SHARES = 2 * NCHUNK
        STEPS = 10
        PIECES = ((0, 2), (2, 5), (5, NCHUNK))
        NORMS = 4 * len(PIECES)
        P_FIRST, P_TURNED, P_SUMMED = (0, 1), (2, 3), (4, 5, 6)

        def copy_turned(copy, n):
            k = 4 * (n % HTURNS)
            squares = p_turn[0:SIDE, n % 4, 0:4 * HALF].rearrange("p (e c) -> p e c", e=4)
            return copy((xw if n < HTURNS else xh)[:, :, k:k + 4].rearrange("p c e -> p e c"), squares)

        def copy_toeplitz(copy, n):
            return copy(xw[:, 8 * n:8 * n + 8, :],
                        p_toe[0:SIDE, n % 2, 0:CHUNK].rearrange("p (c h) -> p c h", c=8))

        def steady(eng):
            eng.sem_inc(passed, 1)

        block = m.ctx.enter_context(nc.Block())

        @block.sync
        def _(sp):
            sp.sem_inc(x_stored, 16)
            sp.dma_start(ident[:], consts["ident"][0:HALF, 0:HALF]).then_inc(const_in, 16)
            sp.dma_start(gmean[:], consts["gmean"][0:HALF, 0:HALF]).then_inc(const_in, 16)
            sp.dma_start(ob[:], out_b).then_inc(const_in, 16)
            sp.wait_ge(gap_zero, 2)
            sp.dma_start(wg[:], weights[0]).then_inc(w_in, 16)
            with sp.Fori(0, BATCH) as b:
                with sp.Fori(0, GROUPS) as g:
                    it = sp.snap(b * GROUPS + g)
                    sp.wait_ge(w_taken, it * 3 + 3)
                    sp.dma_start(wg[:], weights[bass.ds((g + 1) % GROUPS, 1), :, :]
                                 .rearrange("a p n -> (a p) n")).then_inc(w_in, 16)
                    sp.wait_ge(toe_ready, it * TOES + 1)
                    sp.dma_start(t_w, tables[0][:, bass.ds(g * HALF, HALF), :]).then_inc(t_in, 16)
                    sp.dma_start(t_h, tables[1][:, bass.ds(g * HALF, HALF), :]).then_inc(t_in, 16)
                    sp.wait_ge(out_ready, it * SHARES + 1)
                    sp.dma_start(wo[:], out_w[bass.ds(g, 1), :, :].rearrange("a p n -> (a p) n")).then_inc(wo_in, 16)
                sp.wait_ge(added, b * (GROUPS * SHARES) + GROUPS * SHARES + 1)
                sp.dma_start(x_out[bass.ds(b, 1)].rearrange("a (j p) n -> p (a j) n", p=HALF),
                             x_res[:, bass.ds(b % 2, 1), :, :].rearrange("p a j n -> p (a j) n")).then_inc(x_stored, 16)
            sp.wait_ge(x_stored, 16 * BATCH + 16)
            sp.wait_ge(w_in, 16 * (BATCH * GROUPS + 1))

        @block.gpsimd
        def _(pool):
            def load(b):
                pool.dma_start(x_res[:, bass.ds(b % 2, 1), :, :].rearrange("p a j n -> p (a j) n"),
                               x_in[bass.ds(b, 1)].rearrange("a (j p) n -> p (a j) n", p=HALF)).then_inc(x_loaded, 16)

            load(0)
            with pool.Fori(1, BATCH) as b:
                pool.wait_ge(normed, b * NORMS)
                pool.wait_ge(x_stored, b * 16)
                load(b)

        @block.tensor
        def _(pe):
            pe.wait_ge(const_in, 48)
            pe.wait_ge(gap_zero, 2)
            pe.sem_inc(toe_ready, 1)
            pe.sem_inc(out_ready, 1)
            with pe.Fori(0, BATCH) as b:
                pe.wait_ge(step, b * STEPS + 4)
                pe.wait_ge(added, b * (GROUPS * SHARES) + 1)
                pe.matmul(p_out[0:HALF, 0, 0:4], gmean[:], mv[:].rearrange("p j s -> p (j s)"),
                          start=True, stop=True).then_inc(group_stats, 1)
                with pe.Fori(0, GROUPS) as g:
                    it = pe.snap(b * GROUPS + g)
                    silu0 = pe.snap(it * PROJ + 1)
                    po0 = pe.snap(it * NCHUNK + 1)
                    added0 = pe.snap(it * SHARES + 1)
                    turned0 = pe.snap(it * HTURNS)
                    toe0 = pe.snap(it * HTOES)
                    pe.wait_ge(w_taken, it * 3 + 3)

                    def project(kind, t, s, before):
                        pe.wait_ge(silu_done, silu0 + before)
                        for j in range(2):
                            cols, span = slice((3 * j + kind) * HALF, (3 * j + kind + 1) * HALF), slice(t * CHUNK, (t + 1) * CHUNK)
                            for q, (w, x) in enumerate(((w_hi, x_hi), (w_hi, x_lo), (w_lo, x_hi))):
                                mm = pe.matmul(p_proj[0:HALF, s, 0:CHUNK], w[:, cols], x[:, j, span],
                                               start=(j == 0 and q == 0), stop=(j == 1 and q == 2))
                        mm.then_inc(proj_ready, 1)

                    for t in range(NCHUNK):
                        for q, (lo, hi) in enumerate(PIECES):
                            if t == lo:
                                pe.wait_ge(normed, b * NORMS + 4 * (q + 1))
                        project(0, t, 0, max(2 * t - 1, 0))
                        project(1, t, 1, max(2 * t, 0))
                    for t in P_FIRST:
                        project(2, t, t % 2, 2 * NCHUNK - 1 + t)
                    pe.wait_ge(qv_done, it * NCHUNK + NCHUNK)
                    rows = qv[:].rearrange("p (h w) -> p h w", w=SIDE)
                    cols = qv[:].rearrange("p (h w) -> p w h", w=SIDE)
                    for n in range(TURNS):
                        s = n % 2
                        if n == 0:
                            pe.wait_ge(po_done, po0)
                        elif n >= 4:
                            pe.wait_ge(turned[s], turned0 + (n // 2 - 1))
                        if n == 0 or n >= 4:
                            steady(pe)
                        src = rows if n < HTURNS else cols
                        for e in range(4):
                            mm = pe.transpose(p_turn[0:SIDE, n % 4, e * HALF:(e + 1) * HALF],
                                              src[:, 4 * (n % HTURNS) + e, :], ident[:])
                        mm.then_inc(turn_ready, 1)
                    for t in P_TURNED:
                        project(2, t, t % 2, 2 * NCHUNK - 1 + t)
                    for s in range(2):
                        pe.wait_ge(turned[s], turned0 + HTURNS)
                    pe.wait_ge(t_in, it * 32 + 32)
                    for n in range(TOES):
                        s = n % 2
                        if n >= 2:
                            pe.wait_ge(toe_done[s], toe0 + n // 2)
                        steady(pe)
                        for e in range(8):
                            c = 8 * n + e
                            mm = pe.matmul(p_toe[0:SIDE, s, e * SIDE:(e + 1) * SIDE], left[0:64 + SIDE, c, :],
                                           right[0:64 + SIDE, c, :], start=True, stop=True)
                        mm.then_inc(toe_ready, 1)
                    for t in P_SUMMED:
                        project(2, t, t % 2, 2 * NCHUNK - 1 + t)
                    for s in range(2):
                        pe.wait_ge(toe_done[s], toe0 + HTOES)
                    pe.wait_ge(wo_in, it * 16 + 16)

                    def turn_back(t):
                        if t >= 2:
                            pe.wait_ge(po_done, po0 + (t - 1))
                        steady(pe)
                        for e in range(8):
                            mm = pe.transpose(p_back[0:HALF, t % 2, e * SIDE:(e + 1) * SIDE],
                                              xw[:, :, 8 * t + e], ident[0:SIDE, 0:SIDE])
                        mm.then_inc(turn_ready, 1)

                    def share(t):
                        pe.wait_ge(po_done, po0 + (t + 1))
                        for j in range(2):
                            pe.wait_ge(added, added0 + (2 * t + j - 1 if t else 0))
                            pe.matmul(p_out[0:HALF, j, 0:CHUNK], wo[:, j * HALF:(j + 1) * HALF], po[:, t % 2, :],
                                      start=True, stop=True).then_inc(out_ready, 1)

                    turn_back(0)
                    for t in range(NCHUNK):
                        if t + 1 < NCHUNK:
                            turn_back(t + 1)
                        share(t)

        @block.scalar
        def _(act):
            act.sem_inc(silu_done, 1)
            act.wait_ge(gap_zero, 2)
            with act.Fori(0, BATCH) as b:
                act.wait_ge(step, b * STEPS + 9)
                act.activation(rstd[:], gv[:], ACT.Sqrt).then_inc(rstd_done, 1)
                act.wait_ge(step, b * STEPS + STEPS)
                act.wait_ge(po_done, b * (GROUPS * NCHUNK) + 1)
                for lo, hi in PIECES:
                    for j in range(2):
                        span = slice(lo * CHUNK, hi * CHUNK)
                        act.activation((p_all, qv)[j][:, span],
                                       x_res[:, bass.ds(b % 2, 1), j, span].rearrange("p a n -> p (a n)"),
                                       ACT.Identity, scale=rstd[:, j:j + 1], bias=shift[:, j:j + 1]).then_inc(scaled, 1)
                with act.Fori(0, GROUPS) as g:
                    it = act.snap(b * GROUPS + g)
                    proj0 = act.snap(it * PROJ)
                    qv0 = act.snap(it * NCHUNK)
                    turn0 = act.snap(it * (TURNS + NCHUNK))
                    toe0 = act.snap(it * TOES + 1)
                    act.wait_ge(w_taken, it * 3 + 3)
                    for t in range(NCHUNK):
                        if t >= 2:
                            act.wait_ge(qv_done, qv0 + (t - 1))
                        for kind, out in ((0, sq), (1, sv)):
                            act.wait_ge(proj_ready, proj0 + (2 * t + kind + 1))
                            act.activation(out[:, t % 2, :], p_proj[0:HALF, kind, 0:CHUNK], ACT.Silu,
                                           bias=bias[:, kind:kind + 1]).then_inc(silu_done, 1)

                    def silu_p(t):
                        act.wait_ge(proj_ready, proj0 + (2 * NCHUNK + t + 1))
                        act.activation(p_all[:, t * CHUNK:(t + 1) * CHUNK], p_proj[0:HALF, t % 2, 0:CHUNK], ACT.Silu,
                                       bias=bias[:, 2:3]).then_inc(silu_done, 1)

                    for t in P_FIRST:
                        silu_p(t)
                    for n in range(0, TURNS, 2):
                        act.wait_ge(turn_ready, turn0 + (n + 1))
                        copy_turned(act.copy, n).then_inc(turned[0], 1)
                    for t in P_TURNED:
                        silu_p(t)
                    for n in range(0, TOES, 2):
                        act.wait_ge(toe_ready, toe0 + (n + 1))
                        copy_toeplitz(act.copy, n).then_inc(toe_done[0], 1)
                    for t in P_SUMMED:
                        silu_p(t)

        @block.vector
        def _(dve):
            dve.sem_inc(po_done, 1)
            dve.sem_inc(added, 1)
            dve.memset(left[32:64, :, :], 0.0).then_inc(gap_zero, 1)
            dve.memset(right[32:64, :, :], 0.0).then_inc(gap_zero, 1)
            dve.wait_ge(gap_zero, 2)
            dve.wait_ge(const_in, 48)

            def take_weights(it):
                dve.wait_ge(w_in, it * 16 + 16)
                dve.wait_ge(silu_done, it * PROJ + 1)
                steady(dve)
                dve.tensor_copy(bias[:], wg[:, BIAS:BIAS + 3]).then_inc(w_taken, 1)
                dve.tensor_copy(w_hi[:], wg[:, 0:WCOLS]).then_inc(w_taken, 1)
                dve.wait_ge(w_taken, it * 3 + 2)
                dve.tensor_tensor(w_lo[:], wg[:, 0:WCOLS], w_hi[:].bitcast(F32), ALU.subtract).then_inc(w_taken, 1)

            take_weights(0)
            with dve.Fori(0, BATCH) as b:
                done = [0]
                step0 = dve.snap(b * STEPS)

                def own(ins):
                    done[0] += 1
                    ins.then_inc(step, 1)
                    dve.wait_ge(step, step0 + done[0])

                def image(j, lo, n):
                    return x_res[:, bass.ds(b % 2, 1), j, lo:lo + n].rearrange("p a n -> p (a n)")

                dve.wait_ge(x_loaded, b * 16 + 16)
                for j in range(2):
                    for t in range(NCHUNK):
                        ins = dve.bn_stats(bn[:, j, t, :], image(j, t * CHUNK, CHUNK))
                own(ins)
                steady(dve)
                for j in range(2):
                    ins = dve.bn_aggr(mv[:, j, :], bn[:, j, :, :].rearrange("p t s -> p (t s)"))
                own(ins)
                own(dve.tensor_tensor(m2[:], mv[:, :, 0], mv[:, :, 0], ALU.mult))
                own(dve.tensor_tensor(mv[:, :, 1], mv[:, :, 1], m2[:], ALU.add))
                dve.wait_ge(group_stats, b + 1)
                own(dve.tensor_copy(gs[:], p_out[0:HALF, 0, 0:4]))
                own(dve.tensor_tensor(m2[:], gs[:, 0:4:2], gs[:, 0:4:2], ALU.mult))
                own(dve.tensor_tensor(gv[:], gs[:, 1:4:2], m2[:], ALU.subtract))
                own(dve.tensor_scalar(gv[:], gv[:], GN_EPS, None, ALU.add))
                own(dve.reciprocal(gv[:], gv[:]))
                dve.wait_ge(rstd_done, b + 1)
                own(dve.scalar_tensor_tensor(out=shift[:], in0=gs[:, 0:4:2], scalar=-1.0, in1=rstd[:],
                                             op0=ALU.mult, op1=ALU.mult))
                assert done[0] == STEPS
                norm0 = dve.snap(b * NORMS)
                for q, (lo, hi) in enumerate(PIECES):
                    for j in range(2):
                        span = slice(lo * CHUNK, hi * CHUNK)
                        whole = (p_all, qv)[j][:, span]
                        dve.wait_ge(scaled, b * (2 * len(PIECES)) + (2 * q + j + 1))
                        dve.tensor_copy(x_hi[:, j, span], whole).then_inc(normed, 1)
                        dve.wait_ge(normed, norm0 + (4 * q + 2 * j + 1))
                        dve.tensor_tensor(x_lo[:, j, span], whole, x_hi[:, j, span].bitcast(F32),
                                          ALU.subtract).then_inc(normed, 1)
                for j in range(2):
                    dve.tensor_scalar(image(j, 0, TOK), image(j, 0, TOK), ob[:, j:j + 1], None,
                                      ALU.add).then_inc(normed_bias, 1)
                dve.wait_ge(normed, norm0 + NORMS)
                dve.wait_ge(normed_bias, b * 2 + 2)
                steady(dve)

                with dve.Fori(0, GROUPS) as g:
                    it = dve.snap(b * GROUPS + g)
                    silu0 = dve.snap(it * PROJ + 1)
                    turn0 = dve.snap(it * (TURNS + NCHUNK))
                    toe0 = dve.snap(it * TOES + 1)
                    out0 = dve.snap(it * SHARES + 1)
                    for t in range(NCHUNK):
                        dve.wait_ge(silu_done, silu0 + (2 * t + 2))
                        dve.tensor_tensor(qv[:, t * CHUNK:(t + 1) * CHUNK], sq[:, t % 2, :], sv[:, t % 2, :],
                                          ALU.mult).then_inc(qv_done, 1)
                    for n in range(1, TURNS, 2):
                        dve.wait_ge(turn_ready, turn0 + (n + 1))
                        copy_turned(dve.tensor_copy, n).then_inc(turned[1], 1)
                    for n in range(1, TOES, 2):
                        dve.wait_ge(toe_ready, toe0 + (n + 1))
                        copy_toeplitz(dve.tensor_copy, n).then_inc(toe_done[1], 1)

                    def times_p(t):
                        dve.wait_ge(silu_done, silu0 + (2 * NCHUNK + t + 1))
                        dve.wait_ge(turn_ready, turn0 + (TURNS + t + 1))
                        dve.wait_ge(out_ready, out0 + max(2 * t - 2, 0))
                        dve.tensor_tensor(po[:, t % 2, :], p_back[0:HALF, t % 2, 0:CHUNK],
                                          p_all[:, t * CHUNK:(t + 1) * CHUNK], ALU.mult).then_inc(po_done, 1)

                    def add_share(t):
                        for j in range(2):
                            dve.wait_ge(out_ready, out0 + (2 * t + j + 1))
                            place = image(j, t * CHUNK, CHUNK)
                            dve.tensor_tensor(place, place, p_out[0:HALF, j, 0:CHUNK], ALU.add).then_inc(added, 1)

                    times_p(0)
                    for t in range(NCHUNK):
                        if t + 1 < NCHUNK:
                            times_p(t + 1)
                        if t == 1:
                            take_weights(it + 1)
                        add_share(t)


TAPS = [(1, 1), (2, 1), (1, 2), (0, 2), (0, 1), (1, 0), (2, 0)]


def conv_layer(nc, sems, tag, x_in, x_out, taps_w, consts):
    m = Pool(nc, sems, tag)
    PADDED = SIDE + 2
    with m.ctx:
        x_res = m.sb("x_res", [HALF, 2, 2, TOK])
        x_hi = m.sb("x_hi", [HALF, 2, 2, PADDED, PADDED], F32R)
        x_lo = m.sb("x_lo", [HALF, 2, 2, PADDED, PADDED], F32R)
        whole = m.sb("whole", [HALF, TOK])
        W_SIZE = 2 * len(TAPS) * CH
        w_hi = m.sb("w_hi", [HALF, 2, len(TAPS), CH], F32R)
        w_lo = m.sb("w_lo", [HALF, 2, len(TAPS), CH], F32R)
        gmean = m.sb("gmean", [HALF, HALF])
        bn = m.sb("bn", [HALF, 2, NCHUNK, 6])
        mv = m.sb("mv", [HALF, 2, 2])
        m2 = m.sb("m2", [HALF, 2])
        gs = m.sb("gs", [HALF, 4])
        gv = m.sb("gv", [HALF, 2])
        rstd = m.sb("rstd", [HALF, 2])
        shift = m.sb("shift", [HALF, 2])
        p_stat = m.ps("p_stat", [128, BANK])
        p_conv = m.ps("p_conv", [128, 4, BANK])

        passed = m.sem("passed")
        const_in = m.sem("const_in")
        w_in = m.sem("w_in")
        x_loaded = m.sem("x_loaded")
        x_stored = m.sem("x_stored")
        bordered = m.sem("bordered")
        step = m.sem("step")
        group_stats = m.sem("group_stats")
        rstd_done = m.sem("rstd_done")
        scaled = m.sem("scaled")
        normed = m.sem("normed")
        w_split = m.sem("w_split")
        conv_ready = m.sem("conv_ready")
        added = m.sem("added")

        OUTS = 2 * NCHUNK
        NORMS = 4
        STEPS = 10

        def steady(eng):
            eng.sem_inc(passed, 1)

        def slot(t, b):
            return t[:, bass.ds(b % 2, 1)]

        block = m.ctx.enter_context(nc.Block())

        @block.sync
        def _(sp):
            sp.sem_inc(x_stored, 16)
            sp.dma_start(gmean[:], consts["gmean"][0:HALF, 0:HALF]).then_inc(const_in, 16)
            sp.dma_start(whole[:, 0:W_SIZE], taps_w.rearrange("p a i c -> p (a i c)")).then_inc(w_in, 16)
            with sp.Fori(0, BATCH) as b:
                sp.wait_ge(added, b * OUTS + OUTS + 1)
                sp.dma_start(x_out[bass.ds(b, 1)].rearrange("a (j p) n -> p (a j) n", p=HALF),
                             slot(x_res, b).rearrange("p a j n -> p (a j) n")).then_inc(x_stored, 16)
            sp.wait_ge(x_stored, 16 * BATCH + 16)

        @block.gpsimd
        def _(pool):
            def load(b):
                pool.dma_start(slot(x_res, b).rearrange("p a j n -> p (a j) n"),
                               x_in[bass.ds(b, 1)].rearrange("a (j p) n -> p (a j) n", p=HALF)).then_inc(x_loaded, 16)

            load(0)
            pool.memset(x_hi[:].bitcast(F32), 0.0).then_inc(bordered, 1)
            pool.memset(x_lo[:].bitcast(F32), 0.0).then_inc(bordered, 1)
            with pool.Fori(1, BATCH) as b:
                pool.wait_ge(normed, b * NORMS)
                pool.wait_ge(x_stored, b * 16)
                load(b)

        @block.tensor
        def _(pe):
            pe.wait_ge(const_in, 16)
            pe.sem_inc(conv_ready, 1)

            def stats(b):
                pe.wait_ge(step, b * STEPS + 4)
                pe.matmul(p_stat[0:HALF, 0:4], gmean[:], mv[:].rearrange("p j s -> p (j s)"),
                          start=True, stop=True).then_inc(group_stats, 1)

            def conv(b, ahead):
                added0 = pe.snap(b * OUTS)
                pe.wait_ge(normed, b * NORMS + NORMS)
                for t in range(NCHUNK):
                    if t == 3 and ahead:
                        stats(b + 1)
                    for j in range(2):
                        n = 2 * t + j
                        pe.wait_ge(added, added0 + max(n - 3 + 1, 1))
                        k = 0
                        for i, (dy, dx) in enumerate(TAPS):
                            for half in range(2):
                                for w, x in ((w_hi, x_hi), (w_hi, x_lo), (w_lo, x_hi)):
                                    mm = pe.matmul(p_conv[0:HALF, n % 4, 0:CHUNK],
                                                   w[:, half, i, j * HALF:(j + 1) * HALF],
                                                   x[:, bass.ds(b % 2, 1), half, 8 * t + dy:8 * t + dy + 8, dx:dx + SIDE]
                                                   .rearrange("p a h w -> p (a h) w"),
                                                   start=(k == 0), stop=(k == 6 * len(TAPS) - 1))
                                    k += 1
                        mm.then_inc(conv_ready, 1)

            stats(0)
            pe.wait_ge(w_split, 2)
            with pe.Fori(0, BATCH - 1) as b:
                conv(b, True)
            conv(BATCH - 1, False)

        @block.scalar
        def _(act):
            act.wait_ge(w_split, 2)

            def norm(b):
                act.wait_ge(step, b * STEPS + 9)
                act.activation(rstd[:], gv[:], ACT.Sqrt).then_inc(rstd_done, 1)
                act.wait_ge(step, b * STEPS + STEPS)
                for j in range(2):
                    if not (isinstance(b, int) and b == 0 and j == 0):
                        act.wait_ge(normed, b * NORMS + 2 * j)
                    act.activation(whole[:], x_res[:, bass.ds(b % 2, 1), j, :].rearrange("p a n -> p (a n)"),
                                   ACT.Identity, scale=rstd[:, j:j + 1], bias=shift[:, j:j + 1]).then_inc(scaled, 1)

            norm(0)
            with act.Fori(1, BATCH) as b:
                norm(b)

        @block.vector
        def _(dve):
            dve.sem_inc(added, 1)

            def stats(b):
                done = [0]
                step0 = dve.snap(b * STEPS) if not isinstance(b, int) else b * STEPS

                def own(ins):
                    done[0] += 1
                    ins.then_inc(step, 1)
                    dve.wait_ge(step, step0 + done[0])

                dve.wait_ge(x_loaded, b * 16 + 16)
                for j in range(2):
                    for t in range(NCHUNK):
                        ins = dve.bn_stats(bn[:, j, t, :], x_res[:, bass.ds(b % 2, 1), j, t * CHUNK:(t + 1) * CHUNK]
                                           .rearrange("p a n -> p (a n)"))
                own(ins)
                steady(dve)
                for j in range(2):
                    ins = dve.bn_aggr(mv[:, j, :], bn[:, j, :, :].rearrange("p t s -> p (t s)"))
                own(ins)
                own(dve.tensor_tensor(m2[:], mv[:, :, 0], mv[:, :, 0], ALU.mult))
                own(dve.tensor_tensor(mv[:, :, 1], mv[:, :, 1], m2[:], ALU.add))
                dve.wait_ge(group_stats, b + 1)
                own(dve.tensor_copy(gs[:], p_stat[0:HALF, 0:4]))
                own(dve.tensor_tensor(m2[:], gs[:, 0:4:2], gs[:, 0:4:2], ALU.mult))
                own(dve.tensor_tensor(gv[:], gs[:, 1:4:2], m2[:], ALU.subtract))
                own(dve.tensor_scalar(gv[:], gv[:], GN_EPS, None, ALU.add))
                own(dve.reciprocal(gv[:], gv[:]))
                dve.wait_ge(rstd_done, b + 1)
                dve.scalar_tensor_tensor(out=shift[:], in0=gs[:, 0:4:2], scalar=-1.0, in1=rstd[:],
                                         op0=ALU.mult, op1=ALU.mult).then_inc(step, 1)
                assert done[0] + 1 == STEPS

            def add(b, ns):
                out0 = dve.snap(b * OUTS + 1) if not isinstance(b, int) else b * OUTS + 1
                dve.wait_ge(normed, b * NORMS + NORMS)
                for n in ns:
                    t, j = n // 2, n % 2
                    dve.wait_ge(conv_ready, out0 + (n + 1))
                    place = x_res[:, bass.ds(b % 2, 1), j, t * CHUNK:(t + 1) * CHUNK].rearrange("p a n -> p (a n)")
                    dve.tensor_tensor(place, place, p_conv[0:HALF, n % 4, 0:CHUNK], ALU.add).then_inc(added, 1)

            def split(b, j):
                image = whole[:].rearrange("p (h w) -> p h w", w=SIDE)
                hi, lo = (x[:, bass.ds(b % 2, 1), j, 1:SIDE + 1, 1:SIDE + 1].rearrange("p a h w -> p (a h) w")
                          for x in (x_hi, x_lo))
                dve.wait_ge(scaled, b * 2 + j + 1)
                steady(dve)
                dve.tensor_copy(hi, image).then_inc(normed, 1)
                dve.wait_ge(normed, b * NORMS + 2 * j + 1)
                steady(dve)
                dve.tensor_tensor(lo, image, hi.bitcast(F32), ALU.subtract).then_inc(normed, 1)

            dve.wait_ge(w_in, 16)
            flat = [w[:].rearrange("p a i c -> p (a i c)") for w in (w_hi, w_lo)]
            dve.tensor_copy(flat[0], whole[:, 0:W_SIZE]).then_inc(w_split, 1)
            dve.wait_ge(w_split, 1)
            dve.tensor_tensor(flat[1], whole[:, 0:W_SIZE], flat[0].bitcast(F32), ALU.subtract).then_inc(w_split, 1)
            dve.wait_ge(bordered, 2)
            stats(0)
            for j in range(2):
                split(0, j)
            with dve.Fori(0, BATCH - 1) as b:
                add(b, range(2))
                stats(b + 1)
                add(b, range(2, 5))
                split(b + 1, 0)
                add(b, range(5, 8))
                split(b + 1, 1)
                add(b, range(8, OUTS))
            add(BATCH - 1, range(OUTS))


PAIRS = 4
STATES, DIRS, RANK = 16, 4, 12
LN_EPS = 1e-5
SPAN = 784
HSPAN = SPAN // 2
RING = 4
NSPAN = TOK // SPAN
PADDED = SIDE + 2
MIX = [[(0, 0), (1, 2)], [(0, 1), (2, 2)], [(3, 0), (4, 1), (5, 2)]]
V_CONV, V_CB, V_G, V_B, V_D, V_DT, V_A, V_END = 0, 9, 10, 11, 12, 16, 20, 84


def scan_layer(nc, sems, tag, x_in, x_out, ap, z_dram, consts):
    m = Pool(nc, sems, tag)
    with m.ctx:
        U_SIZE = 16128
        u = m.sb("u", [128, U_SIZE])

        def view(at, *shape, dt=F32):
            n = 1
            for s in shape:
                n *= s
            words = n if dt is F32 else n // 2
            assert at + words <= U_SIZE
            v = u[:, at:at + words]
            if dt is not F32:
                v = v.bitcast(dt)
            if len(shape) == 2:
                return v.rearrange("p (a b) -> p a b", a=shape[0])
            if len(shape) == 3:
                return v.rearrange("p (a b c) -> p a b c", a=shape[0], b=shape[1])
            return v

        xn = view(0, 3, TOK)
        pad = view(3 * TOK, PADDED, PADDED)
        sel_f = u[0:96, 0:3 * STATES * 128].rearrange("p (a b c) -> p a b c", a=3, b=STATES)
        zs = view(U_SIZE - 2 * CHUNK, 2, CHUNK)
        f = view(0, TOK)
        rest = view(TOK, TOK)
        part = [view(2 * TOK + i * TOK // 2, TOK, dt=BF16) for i in range(3)]
        one_e = view(7 * TOK // 2, TOK)
        t_abs, t_e = (view(9 * TOK // 2 + 2 * CHUNK * i, 2, CHUNK) for i in range(2))
        t_ln = t_abs
        db = view(TOK, RING, SPAN)
        hs = view(TOK + RING * SPAN, RING, SPAN)
        hc = view(TOK + 2 * RING * SPAN, RING, SPAN)
        da = view(TOK + 3 * RING * SPAN, 2, SPAN)
        cb = view(TOK + (3 * RING + 2) * SPAN, 2, SPAN)
        dev = view(0, 6, CHUNK)
        squ = view(6 * CHUNK, 3, CHUNK)
        rs = view(9 * CHUNK, 6, CHUNK)
        zc, xr, oc = (view((15 + 6 * i) * CHUNK, 6, CHUNK) for i in range(3))

        xc = m.sb("xc", [128, 3, TOK])
        y = m.sb("y", [128, 3, TOK])
        d = m.sb("d", [128, TOK])
        du = m.sb("du", [128, TOK])
        bs = m.sb("bs", [96, TOK], BF16)
        cs = m.sb("cs", [96, TOK], BF16)
        sel = m.sb("sel", [96, 3, STATES, 128], BF16)
        ln1 = m.sb("ln1", [128, 1])
        state = m.sb("state", [128, STATES])
        vec = m.sb("vec", [128, 3, V_END])
        dsum = m.sb("dsum", [128, 3])
        dtb = m.sb("dtb", [128, 3 * DIRS])
        nega = m.sb("nega", [128, 3 * DIRS * STATES])
        ident = m.sb("ident", [128, 128])
        w_ssm, w_z, w_gn, w_ln, w_out = (m.sb(n, [128, 6, 128]) for n in ("w_ssm", "w_z", "w_gn", "w_ln", "w_out"))
        w_x = m.sb("w_x", [128, 3, 128])
        w_dt = m.sb("w_dt", [128, 128])
        bn = m.sb("bn", [128, 3, NCHUNK, 6])
        mv = m.sb("mv", [128, 3, 2])
        m2 = m.sb("m2", [128, 3])
        gs = m.sb("gs", [128, 6])
        gv = m.sb("gv", [128, 3])
        rstd = m.sb("rstd", [128, 3])
        shift = m.sb("shift", [128, 3])
        ps = m.ps("ps", [128, 8, BANK])

        passed = m.sem("passed")
        const_in = m.sem("const_in")
        exp_made = m.sem("exp_made")
        made2 = m.sem("made2")
        made = m.sem("made")
        x_loaded = m.sem("x_loaded")
        step = m.sem("step")
        gn_ready = m.sem("gn_ready")
        rstd_done = m.sem("rstd_done")
        normed = m.sem("normed")
        mix_ready = m.sem("mix_ready")
        mix_out = m.sem("mix_out")
        z_stored = [m.sem(f"z_stored{i}") for i in range(2)]
        bordered = m.sem("bordered")
        tap_done = m.sem("tap_done")
        xc_done = m.sem("xc_done")
        y_init = m.sem("y_init")
        wx_in = m.sem("wx_in")
        wdt_in = m.sem("wdt_in")
        f_ready = m.sem("f_ready")
        f_out = m.sem("f_out")
        split = m.sem("split")
        gathered = m.sem("gathered")
        dt_ready = m.sem("dt_ready")
        sp_done = m.sem("sp_done")
        d_step = m.sem("d_step")
        b_ready = m.sem("b_ready")
        c_ready = m.sem("c_ready")
        c_out = m.sem("c_out")
        a_ready = m.sem("a_ready")
        b_done = m.sem("b_done")
        zeroed = m.sem("zeroed")
        scanned = m.sem("scanned")
        kept = m.sem("kept")
        hc_done = m.sem("hc_done")
        y_ready = m.sem("y_ready")
        y_added = m.sem("y_added")
        fin_in = m.sem("fin_in")
        mean_ready = m.sem("mean_ready")
        var_ready = m.sem("var_ready")
        share_ready = m.sem("share_ready")
        dev_done = m.sem("dev_done")
        inv_step = m.sem("inv_step")
        gate_step = m.sem("gate_step")
        squared = m.sem("squared")
        rooted = m.sem("rooted")
        out_done = m.sem("out_done")
        x_stored = [m.sem(f"x_stored{i}") for i in range(2)]

        MIXES = 6 * NCHUNK
        ZUSES = (11, 10)
        OUSES = (4, 3)
        STEPS, TAPS9, SPLITS, GATES = 10, 9, 8, 5
        GATHER = 12 * 16
        TILE_N = NSPAN * STATES
        CONSTS = 8

        def steady(eng):
            eng.sem_inc(passed, 1)

        def image_view(flat, k):
            return flat.rearrange("p (h w) -> p h w", w=SIDE) if k < 2 else flat.rearrange("p (h w) -> p w h", w=SIDE)

        def scan_view(flat, k):
            g = image_view(flat, k)
            return g[:, ::-1, ::-1] if k % 2 else g

        def tile(t, i):
            return t[:, bass.ds(i, 1), :].rearrange("p a n -> p (a n)")

        def image_parts(dram, pr, place, lo=0, n=TOK):
            for e in range(2):
                row = dram[bass.ds(2 * pr + e, 1), :, lo:lo + n]
                yield place(e), row[:, 0:128, :].rearrange("a p n -> (a p) n")
                yield place(2)[64 * e:64 * e + 64, :], row[:, 128:CH, :].rearrange("a p n -> (a p) n")

        block = m.ctx.enter_context(nc.Block())

        @block.sync
        def _(sp):
            for place, src in ((sel_f, ap["c_sel"]), (ident[:], consts["ident"]), (vec[:], ap["L2_vec"]),
                               (w_ssm[:], ap["L2_ssm"]), (w_z[:], ap["L2_z"]), (w_gn[:], ap["c_mixgn"]),
                               (w_ln[:], ap["c_mixln"]), (w_out[:], ap["L2_out"])):
                sp.dma_start(place, src).then_inc(const_in, 16)
            sp.wait_ge(made, 1)
            with sp.Fori(0, PAIRS) as pr:
                sp.wait_ge(out_done, pr * NCHUNK + 1)
                for s in range(2):
                    sp.wait_ge(x_stored[s], pr * (64 * OUSES[s]) + 64)
                for place, src in image_parts(x_in, pr, lambda i: xn[:, i, :]):
                    sp.dma_start(place, src).then_inc(x_loaded, 16)
                for n in range(3 * NCHUNK):
                    i, t = n // NCHUNK, n % NCHUNK
                    sp.wait_ge(mix_out, pr * MIXES + (2 * NCHUNK * i + NCHUNK + t + 2))
                    sp.dma_start(z_dram[bass.ds(pr, 1), :, i, t * CHUNK:(t + 1) * CHUNK]
                                 .rearrange("a p n -> (a p) n"), zs[:, n % 2, :]).then_inc(z_stored[n % 2], 16)
                for k in range(DIRS):
                    it = sp.snap(pr * DIRS + k)
                    sp.wait_ge(dt_ready, it * (3 * NCHUNK) + 1)
                    sp.dma_start(w_x[:], ap["L2_x"][k]).then_inc(wx_in, 16)

                    def load_dt(i):
                        sp.wait_ge(dt_ready, it * (3 * NCHUNK) + i * NCHUNK + 1)
                        sp.dma_start(w_dt[:], ap["L2_dt"][k][bass.ds(i, 1), :, :].rearrange("a p n -> (a p) n"))\
                          .then_inc(wdt_in, 16)

                    load_dt(0)
                    sp.wait_ge(split, it * SPLITS + SPLITS)
                    sp.wait_ge(y_ready, it * (3 * TILE_N) + RING)
                    for dst, row in ((bs, 32), (cs, 48)):
                        for e in range(2):
                            for i in range(3):
                                at = 48 * e + 16 * i
                                sp.dma_start(dst[at:at + 16, :],
                                             part[i][64 * e + row:64 * e + row + 16, :]).then_inc(gathered, 16)
                    with sp.Fori(1, 3) as i:
                        load_dt(i)
                sp.wait_ge(y_added, pr * (DIRS * 3 * NSPAN) + DIRS * 3 * NSPAN + 1)
                for s in range(2):
                    sp.wait_ge(z_stored[s], pr * (16 * ZUSES[s]) + 16 * ZUSES[s])

                def load(t):
                    s = t % 2
                    sp.dma_start(zc[:, 3 * s:3 * s + 3, :],
                                 z_dram[bass.ds(pr, 1), :, :, t * CHUNK:(t + 1) * CHUNK]
                                 .rearrange("a p i n -> (a p) i n")).then_inc(fin_in, 16)
                    for place, src in image_parts(x_in, pr, lambda i: xr[:, 3 * s + i, :], t * CHUNK, CHUNK):
                        sp.dma_start(place, src).then_inc(fin_in, 16)

                load(0)
                for t in range(NCHUNK):
                    s = t % 2
                    if t + 1 < NCHUNK:
                        sp.wait_ge(fin_in, pr * (80 * NCHUNK) + 80 * (t + 1))
                        if t >= 1:
                            sp.wait_ge(out_done, pr * NCHUNK + t + 1)
                        load(t + 1)
                    sp.wait_ge(out_done, pr * NCHUNK + t + 2)
                    for place, dst in image_parts(x_out, pr, lambda i: oc[:, 3 * s + i, :], t * CHUNK, CHUNK):
                        sp.dma_start(dst, place).then_inc(x_stored[s], 16)
            for s in range(2):
                sp.wait_ge(x_stored[s], 64 * OUSES[s] * PAIRS + 64)

        @block.gpsimd
        def _(pool):
            pool.sem_inc(kept, STATES)
            pool.sem_inc(hc_done, RING)
            pool.wait_ge(made, 1)
            with pool.Fori(0, PAIRS) as pr:
                pool.wait_ge(out_done, pr * NCHUNK + 1)
                for s in range(2):
                    pool.wait_ge(x_stored[s], pr * (64 * OUSES[s]) + 64)
                steady(pool)
                pool.memset(pad[:], 0.0).then_inc(bordered, 1)
                with pool.Fori(0, DIRS) as k:
                    it = pool.snap(pr * DIRS + k)
                    split0 = pool.snap(it * SPLITS)
                    for q, (lo, hi) in enumerate(((0, 3), (3, NCHUNK))):
                        span = slice(lo * CHUNK, hi * CHUNK)
                        pool.wait_ge(f_out, it * NCHUNK + hi)
                        steady(pool)
                        pool.tensor_copy(part[0][:, span], f[:, span]).then_inc(split, 1)
                        pool.wait_ge(split, split0 + (4 * q + 1))
                        pool.tensor_tensor(rest[:, span], f[:, span], part[0][:, span], ALU.subtract).then_inc(split, 1)
                        pool.wait_ge(split, split0 + (4 * q + 2))
                        steady(pool)
                        pool.tensor_copy(part[1][:, span], rest[:, span]).then_inc(split, 1)
                        pool.wait_ge(split, split0 + (4 * q + 3))
                        pool.tensor_tensor(part[2][:, span], rest[:, span], part[1][:, span], ALU.subtract)\
                            .then_inc(split, 1)
                    with pool.Fori(0, 3 * NSPAN) as c:
                        n0 = pool.snap((it * (3 * NSPAN) + c) * STATES)
                        for n in range(STATES):
                            r = n % RING
                            pool.wait_ge(scanned, n0 + (n + 1 + RING))
                            steady(pool)
                            pool.tensor_copy(state[:, n:n + 1], hs[:, r, SPAN - 1:SPAN]).then_inc(kept, 1)
                            pool.wait_ge(c_out, n0 + (n + 1))
                            pool.wait_ge(y_ready, n0 + (n + 1))
                            pool.tensor_tensor(hc[:, r, :], hs[:, r, :], cb[:, n % 2, :], ALU.mult)\
                                .then_inc(hc_done, 1)

        @block.tensor
        def _(pe):
            pe.sem_inc(dt_ready, 1)
            pe.sem_inc(y_ready, RING)
            pe.wait_ge(const_in, 16 * CONSTS)
            pe.wait_ge(made, 1)

            def mix(w, src, out_of, i):
                for q, (w_i, s_i) in enumerate(MIX[i]):
                    mm = pe.matmul(out_of, w[:, w_i, :], src(s_i), start=(q == 0), stop=(q == len(MIX[i]) - 1))
                return mm

            with pe.Fori(0, PAIRS) as pr:
                pe.wait_ge(out_done, pr * NCHUNK + 1)
                pe.wait_ge(step, pr * STEPS + 4)
                for i in range(3):
                    mm = mix(w_gn, lambda s: mv[:, s, :], ps[:, 7, 2 * i:2 * i + 2], i)
                mm.then_inc(gn_ready, 1)
                pe.wait_ge(normed, pr * 3 + 3)
                out0 = pe.snap(pr * MIXES)
                for n in range(MIXES):
                    i, q = n // (2 * NCHUNK), n % (2 * NCHUNK)
                    t = q % NCHUNK
                    if n >= 4:
                        pe.wait_ge(mix_out, out0 + (n - 4 + 2))
                    mix(w_ssm if q < NCHUNK else w_z, lambda s: xn[:, s, t * CHUNK:(t + 1) * CHUNK],
                        ps[:, n % 4, 0:CHUNK], i).then_inc(mix_ready, 1)

                for k in range(DIRS):
                    it = pe.snap(pr * DIRS + k)
                    pe.wait_ge(wx_in, it * 16 + 16)
                    pe.wait_ge(xc_done, pr * 3 + 3)
                    for t in range(NCHUNK):
                        if t >= 2:
                            pe.wait_ge(f_out, it * NCHUNK + (t - 1))
                        for i in range(3):
                            mm = pe.matmul(ps[:, t % 2, 0:CHUNK], w_x[:, i, :],
                                           scan_view(xc[:, i, :], k)[:, 8 * t:8 * t + 8, :],
                                           start=(i == 0), stop=(i == 2))
                        mm.then_inc(f_ready, 1)
                    pe.wait_ge(f_out, it * NCHUNK + NCHUNK)
                    steady(pe)
                    with pe.Fori(0, 3) as i:
                        ti = pe.snap(it * 3 + i)
                        sp0 = pe.snap(ti * (4 * NCHUNK))
                        pe.wait_ge(wdt_in, ti * 16 + 16)
                        for t in range(NCHUNK):
                            if t >= 2:
                                pe.wait_ge(sp_done, sp0 + (3 * (t - 1)))
                            pe.matmul(ps[:, t % 2, 0:CHUNK], w_dt[:], f[:, t * CHUNK:(t + 1) * CHUNK],
                                      start=True, stop=True).then_inc(dt_ready, 1)
                        pe.wait_ge(sp_done, sp0 + 3 * NCHUNK)
                        pe.wait_ge(gathered, it * GATHER + GATHER)
                        steady(pe)

                        def spread(rows, c, n, bank):
                            at = (c + n // STATES) * SPAN
                            for h in range(2):
                                mm = pe.matmul(ps[:, bank + h, 0:HSPAN],
                                               sel[:, bass.ds(i, 1), n % STATES, :].rearrange("p a m -> p (a m)"),
                                               rows[:, bass.ds(at + h * HSPAN, HSPAN)], start=True, stop=True)
                            return mm

                        def b_row(c, n, n0):
                            if n >= 2:
                                pe.wait_ge(b_done, n0 + (n - 1))
                                steady(pe)
                            spread(bs, c, n, 2 * (n % 2)).then_inc(b_ready, 1)

                        def c_row(c, n, n0):
                            if n >= 1:
                                pe.wait_ge(c_out, n0 + n)
                                steady(pe)
                            spread(cs, c, n, 4).then_inc(c_ready, 1)

                        def sum_span(c, last):
                            n0 = pe.snap((ti * NSPAN + c) * STATES)

                            def share(n):
                                pe.wait_ge(hc_done, n0 + (n + 1 + RING))
                                if n == 0:
                                    pe.wait_ge(y_added, ti * NSPAN + c + 1)
                                for h in range(2):
                                    mm = pe.matmul(ps[:, 6 + h, 0:HSPAN], ident[:],
                                                   hc[:, n % RING, h * HSPAN:(h + 1) * HSPAN],
                                                   start=(n == 0), stop=(n == STATES - 1))
                                mm.then_inc(y_ready, 1)

                            for n in range(STATES):
                                if n + 3 < STATES or not last:
                                    b_row(c, n + 3, n0)
                                if n + 2 < STATES or not last:
                                    c_row(c, n + 2, n0)
                                share(n)

                        first = pe.snap(ti * TILE_N)
                        b_row(0, 0, first)
                        c_row(0, 0, first)
                        b_row(0, 1, first)
                        b_row(0, 2, first)
                        c_row(0, 1, first)
                        with pe.Fori(0, NSPAN - 1) as c:
                            sum_span(c, False)
                        sum_span(NSPAN - 1, True)
                pe.wait_ge(y_added, (pr + 1) * (DIRS * 3 * NSPAN) + 1)
                c0 = pe.snap(pr * NCHUNK)

                def moments(t):
                    if t == 1:
                        pe.wait_ge(dev_done, c0 + 1)
                    elif t >= 2:
                        pe.wait_ge(out_done, c0 + t)
                    for i in range(3):
                        mm = mix(w_ln, lambda s: y[:, s, t * CHUNK:(t + 1) * CHUNK], ps[:, i, 0:CHUNK], i)
                    mm.then_inc(mean_ready, 1)
                    pe.wait_ge(squared, c0 + (t + 1))
                    if t >= 1:
                        pe.wait_ge(inv_step, pr * (2 * NCHUNK) + (2 * t - 1))
                    for i in range(3):
                        mm = mix(w_ln, lambda s: squ[:, s, :], ps[:, 3 + i, 0:CHUNK], i)
                    mm.then_inc(var_ready, 1)

                moments(0)
                for t in range(NCHUNK):
                    if t + 1 < NCHUNK:
                        moments(t + 1)
                        pe.wait_ge(dev_done, c0 + (t + 2))
                    pe.wait_ge(gate_step, pr * (GATES * NCHUNK) + GATES * (t + 1))
                    for i in range(3):
                        mm = mix(w_out, lambda s: dev[:, 3 * (t % 2) + s, :], ps[:, i, 0:CHUNK], i)
                    mm.then_inc(share_ready, 1)

        @block.scalar
        def _(act):
            act.sem_inc(mix_out, 1)
            act.wait_ge(const_in, 16 * CONSTS)
            act.activation(vec[:, :, V_A:V_END], vec[:, :, V_A:V_END], ACT.Exp).then_inc(exp_made, 1)
            act.wait_ge(made2, 1)
            act.activation(ln1[:], ln1[:], ACT.Ln).then_inc(exp_made, 1)
            act.wait_ge(made, 1)
            with act.Fori(0, PAIRS) as pr:
                act.wait_ge(step, pr * STEPS + 9)
                act.activation(rstd[:], gv[:], ACT.Sqrt).then_inc(rstd_done, 1)
                mix0 = act.snap(pr * MIXES)

                def silu_xc(i):
                    act.wait_ge(tap_done, pr * (3 * TAPS9) + (TAPS9 * (i + 1) + 1))
                    act.activation(xc[:, i, :], xc[:, i, :], ACT.Silu).then_inc(xc_done, 1)

                for n in range(MIXES):
                    i, q = n // (2 * NCHUNK), n % (2 * NCHUNK)
                    t = q % NCHUNK
                    if q >= NCHUNK:
                        zi = NCHUNK * i + t
                        if zi >= 2:
                            act.wait_ge(z_stored[zi % 2], pr * (16 * ZUSES[zi % 2]) + 16 * (zi // 2))
                        act.wait_ge(mix_ready, mix0 + (n + 1))
                        act.activation(zs[:, zi % 2, :], ps[:, n % 4, 0:CHUNK], ACT.Silu).then_inc(mix_out, 1)
                    else:
                        if t == 0 and i:
                            silu_xc(i - 1)
                        if t == 0 and not i:
                            act.wait_ge(bordered, pr + 1)
                        act.wait_ge(mix_ready, mix0 + (n + 1))
                        act.copy(pad[:, 1 + 8 * t:9 + 8 * t, 1:1 + SIDE],
                                 ps[:, n % 4, 0:CHUNK].rearrange("p (h w) -> p h w", w=SIDE)).then_inc(mix_out, 1)
                silu_xc(2)

                for k in range(DIRS):
                    it = act.snap(pr * DIRS + k)
                    for t in range(NCHUNK):
                        act.wait_ge(f_ready, it * NCHUNK + (t + 1))
                        act.copy(f[:, t * CHUNK:(t + 1) * CHUNK], ps[:, t % 2, 0:CHUNK]).then_inc(f_out, 1)
                    with act.Fori(0, 3) as i:
                        ti = act.snap(it * 3 + i)
                        sp0 = act.snap(ti * (4 * NCHUNK))
                        sp1 = act.snap(sp0 + 3 * NCHUNK)
                        dt0 = act.snap(ti * NCHUNK + 1)
                        d0 = act.snap(ti * (5 * NCHUNK))
                        bias = dtb[:, bass.ds(i * DIRS + k, 1)]
                        for h in range(2):
                            act.wait_ge(z_stored[h], (pr + 1) * (16 * ZUSES[h]))
                        steady(act)
                        for t in range(NCHUNK):
                            s = t % 2
                            act.wait_ge(dt_ready, dt0 + (t + 1))
                            span = slice(t * CHUNK, (t + 1) * CHUNK)
                            if t >= 2:
                                act.wait_ge(sp_done, sp0 + (3 * (t - 1)))
                            steady(act)
                            act.activation(t_abs[:, s, :], ps[:, s, 0:CHUNK], ACT.Abs, bias=bias).then_inc(sp_done, 1)
                            act.activation(d[:, span], ps[:, s, 0:CHUNK], ACT.Relu, bias=bias).then_inc(sp_done, 1)
                            act.wait_ge(sp_done, sp0 + (3 * t + 1))
                            if t >= 2:
                                act.wait_ge(d_step, d0 + (3 * (t - 2) + 3))
                            act.activation(t_e[:, s, :], t_abs[:, s, :], ACT.Exp, scale=-1.0).then_inc(sp_done, 1)
                        for t in range(NCHUNK):
                            s = t % 2
                            act.wait_ge(d_step, d0 + (3 * t + 1))
                            if t >= 2:
                                act.wait_ge(d_step, d0 + (3 * NCHUNK + 2 * (t - 2) + 1))
                            else:
                                act.wait_ge(sp_done, sp0 + 3 * NCHUNK)
                            act.activation(t_ln[:, s, :], one_e[:, t * CHUNK:(t + 1) * CHUNK], ACT.Ln)\
                               .then_inc(sp_done, 1)
                        act.wait_ge(d_step, d0 + 5 * NCHUNK)

                        def decay(c, n, n0):
                            act.wait_ge(scanned, n0 + (n + 3))
                            steady(act)
                            act.activation(da[:, n % 2, :], d[:, bass.ds((c + n // STATES) * SPAN, SPAN)], ACT.Exp,
                                           scale=nega[:, bass.ds(i * (DIRS * STATES) + (k * STATES + n % STATES), 1)])\
                               .then_inc(a_ready, 1)

                        def decay_span(c, last):
                            n0 = act.snap((ti * NSPAN + c) * STATES)
                            for n in range(STATES):
                                if n + 1 < STATES or not last:
                                    decay(c, n + 1, n0)
                                act.wait_ge(c_ready, n0 + (n + 1))
                                act.wait_ge(hc_done, n0 + (n + 3))
                                act.copy(cb[:, n % 2, :].rearrange("p (a n) -> p a n", a=2),
                                         ps[:, 4:6, 0:HSPAN]).then_inc(c_out, 1)

                        decay(0, 0, act.snap(ti * (NSPAN * STATES)))
                        for c in range(NSPAN):
                            decay_span(c, c == NSPAN - 1)
                c0 = act.snap(pr * NCHUNK)
                for t in range(NCHUNK):
                    part_of = slice(3 * (t % 2), 3 * (t % 2) + 3)
                    act.wait_ge(dev_done, c0 + (t + 1))
                    if t >= 1:
                        act.wait_ge(var_ready, c0 + t)
                    act.activation(squ[:], dev[:, part_of, :], ACT.Square).then_inc(squared, 1)
                    act.wait_ge(inv_step, pr * (2 * NCHUNK) + (2 * t + 2))
                    act.activation(rs[:, part_of, :], rs[:, part_of, :], ACT.Sqrt).then_inc(rooted, 1)

        @block.vector
        def _(dve):
            dve.sem_inc(tap_done, 1)
            dve.sem_inc(scanned, RING)
            dve.sem_inc(y_added, 1)
            dve.sem_inc(out_done, 1)
            dve.sem_inc(x_stored[0], 64)
            dve.sem_inc(x_stored[1], 64)
            dve.wait_ge(const_in, 16 * CONSTS)
            dve.memset(ln1[:], 1.0).then_inc(made2, 1)
            dve.tensor_copy(sel[:], sel_f).then_inc(made2, 1)
            dve.tensor_tensor(dsum[:], vec[:, :, V_D], vec[:, :, V_D + 1], ALU.add).then_inc(made2, 1)
            for q in (2, 3):
                dve.wait_ge(made2, q + 1)
                dve.tensor_tensor(dsum[:], dsum[:], vec[:, :, V_D + q], ALU.add).then_inc(made2, 1)
            dve.tensor_tensor(dtb[:].rearrange("p (i k) -> p i k", i=3), vec[:, :, V_DT:V_A],
                              vec[:, :, V_DT:V_A], ALU.add).then_inc(made2, 1)
            dve.wait_ge(exp_made, 2)
            dve.tensor_scalar(nega[:].rearrange("p (i n) -> p i n", i=3), vec[:, :, V_A:V_END], -1.0, None,
                              ALU.mult).then_inc(made2, 1)
            dve.wait_ge(made2, 7)
            dve.sem_inc(made, 1)

            with dve.Fori(0, PAIRS) as pr:
                done = [0]
                step0 = dve.snap(pr * STEPS)

                def own(ins):
                    done[0] += 1
                    ins.then_inc(step, 1)
                    dve.wait_ge(step, step0 + done[0])

                dve.wait_ge(x_loaded, pr * 64 + 64)
                for i in range(3):
                    for t in range(NCHUNK):
                        ins = dve.bn_stats(bn[:, i, t, :], xn[:, i, t * CHUNK:(t + 1) * CHUNK])
                own(ins)
                steady(dve)
                for i in range(3):
                    ins = dve.bn_aggr(mv[:, i, :], bn[:, i, :, :].rearrange("p t s -> p (t s)"))
                own(ins)
                own(dve.tensor_tensor(m2[:], mv[:, :, 0], mv[:, :, 0], ALU.mult))
                own(dve.tensor_tensor(mv[:, :, 1], mv[:, :, 1], m2[:], ALU.add))
                dve.wait_ge(gn_ready, pr + 1)
                own(dve.tensor_copy(gs[:], ps[:, 7, 0:6]))
                own(dve.tensor_tensor(m2[:], gs[:, 0:6:2], gs[:, 0:6:2], ALU.mult))
                own(dve.tensor_tensor(gv[:], gs[:, 1:6:2], m2[:], ALU.subtract))
                own(dve.tensor_scalar(gv[:], gv[:], GN_EPS, None, ALU.add))
                own(dve.reciprocal(gv[:], gv[:]))
                dve.wait_ge(rstd_done, pr + 1)
                own(dve.scalar_tensor_tensor(out=shift[:], in0=gs[:, 0:6:2], scalar=-1.0, in1=rstd[:],
                                             op0=ALU.mult, op1=ALU.mult))
                assert done[0] == STEPS
                for i in range(3):
                    dve.tensor_scalar(xn[:, i, :], xn[:, i, :], rstd[:, i:i + 1], shift[:, i:i + 1],
                                      ALU.mult, ALU.add).then_inc(normed, 1)
                tap0 = dve.snap(pr * (3 * TAPS9) + 1)
                for i in range(3):
                    dve.wait_ge(mix_out, pr * MIXES + (2 * NCHUNK * i + NCHUNK + 1))
                    acc = xc[:, i, :].rearrange("p (h w) -> p h w", w=SIDE)
                    for q in range(TAPS9):
                        src = pad[:, q // 3:q // 3 + SIDE, q % 3:q % 3 + SIDE]
                        w = vec[:, i, V_CONV + q:V_CONV + q + 1]
                        if q == 0:
                            dve.tensor_scalar(acc, src, w, vec[:, i, V_CB:V_CB + 1], ALU.mult, ALU.add)\
                               .then_inc(tap_done, 1)
                        else:
                            dve.wait_ge(tap_done, tap0 + (TAPS9 * i + q))
                            dve.scalar_tensor_tensor(out=acc, in0=src, scalar=w, in1=acc, op0=ALU.mult,
                                                     op1=ALU.add).then_inc(tap_done, 1)
                for i in range(3):
                    dve.wait_ge(xc_done, pr * 3 + (i + 1))
                    dve.tensor_scalar(y[:, i, :], xc[:, i, :], dsum[:, i:i + 1], None, ALU.mult).then_inc(y_init, 1)

                for k in range(DIRS):
                    it = dve.snap(pr * DIRS + k)
                    dve.wait_ge(y_init, pr * 3 + 3)
                    steady(dve)
                    with dve.Fori(0, 3) as i:
                        ti = dve.snap(it * 3 + i)
                        sp0 = dve.snap(ti * (4 * NCHUNK))
                        d0 = dve.snap(ti * (5 * NCHUNK))
                        u_k = image_view(tile(xc, i), k)
                        for t in range(NCHUNK):
                            s = t % 2
                            span = slice(t * CHUNK, (t + 1) * CHUNK)
                            dve.wait_ge(sp_done, sp0 + (3 * t + 3))
                            dve.tensor_scalar(one_e[:, span], t_e[:, s, :], 1.0, None, ALU.add).then_inc(d_step, 1)
                            dve.wait_ge(d_step, d0 + (3 * t + 1))
                            dve.scalar_tensor_tensor(out=t_e[:, s, :], in0=one_e[:, span], scalar=-1.0,
                                                     in1=t_e[:, s, :], op0=ALU.add, op1=ALU.subtract)\
                               .then_inc(d_step, 1)
                            dve.wait_ge(d_step, d0 + (3 * t + 2))
                            dve.tensor_tensor(d[:, span], d[:, span], t_e[:, s, :], ALU.subtract).then_inc(d_step, 1)
                        for t in range(NCHUNK):
                            s = t % 2
                            span = slice(t * CHUNK, (t + 1) * CHUNK)
                            dve.wait_ge(sp_done, sp0 + (3 * NCHUNK + t + 1))
                            dve.wait_ge(d_step, d0 + (3 * t + 3))
                            dve.scalar_tensor_tensor(out=d[:, span], in0=t_ln[:, s, :], scalar=ln1[:],
                                                     in1=d[:, span], op0=ALU.subtract, op1=ALU.add)\
                               .then_inc(d_step, 1)
                            dve.wait_ge(d_step, d0 + (3 * NCHUNK + 2 * t + 1))
                            du_t, d_t = (v[:, span].rearrange("p (a b) -> p a b", b=SIDE) for v in (du, d))
                            row = 8 * t
                            if k % 2:
                                du_t, d_t, row = du_t[:, ::-1, ::-1], d_t[:, ::-1, ::-1], SIDE - 8 - 8 * t
                            dve.tensor_tensor(du_t, d_t, u_k[:, row:row + 8, :], ALU.mult).then_inc(d_step, 1)
                        dve.wait_ge(d_step, d0 + 5 * NCHUNK)
                        dve.wait_ge(kept, ti * TILE_N + STATES)
                        steady(dve)
                        dve.memset(state[:], 0.0).then_inc(zeroed, 1)
                        dve.wait_ge(zeroed, ti + 1)
                        steady(dve)

                        def times_b(c, n, n0):
                            dve.wait_ge(b_ready, n0 + (n + 1))
                            dve.wait_ge(scanned, n0 + (n + 1))
                            b = 2 * (n % 2)
                            dve.tensor_tensor(db[:, n % RING, :].rearrange("p (a n) -> p a n", a=2),
                                              ps[:, b:b + 2, 0:HSPAN],
                                              du[:, bass.ds((c + n // STATES) * SPAN, SPAN)]
                                              .rearrange("p (a n) -> p a n", a=2), ALU.mult).then_inc(b_done, 1)

                        def add_y(c):
                            dve.wait_ge(y_ready, ti * TILE_N + (c * STATES + (STATES + RING)))
                            rows = SPAN // SIDE
                            total = ps[:, 6:8, 0:HSPAN].rearrange("p a (r w) -> p a r w", w=SIDE)
                            row = c * rows
                            if k % 2:
                                total, row = total[:, ::-1, ::-1, ::-1], c * -rows + (SIDE - rows)
                            place = image_view(tile(y, i), k)[:, bass.ds(row, rows), :]\
                                .rearrange("p (a r) w -> p a r w", a=2)
                            dve.tensor_tensor(place, place, total, ALU.add).then_inc(y_added, 1)

                        def scan_span(c, first, last):
                            n0 = dve.snap((ti * NSPAN + c) * STATES)
                            for n in range(STATES):
                                if n + 1 < STATES or not last:
                                    times_b(c, n + 1, n0)
                                dve.wait_ge(a_ready, n0 + (n + 1))
                                dve.wait_ge(b_done, n0 + (n + 1))
                                dve.wait_ge(kept, n0 + (n + 1))
                                dve.wait_ge(hc_done, n0 + (n + 1))
                                dve.tensor_tensor_scan(hs[:, n % RING, :], da[:, n % 2, :], db[:, n % RING, :],
                                                       state[:, n:n + 1], ALU.mult, ALU.add).then_inc(scanned, 1)
                                if n == 1 and not first:
                                    add_y(c - 1)

                        times_b(0, 0, dve.snap(ti * TILE_N))
                        scan_span(0, True, False)
                        with dve.Fori(1, NSPAN - 1) as c:
                            scan_span(c, False, False)
                        scan_span(NSPAN - 1, False, True)
                        add_y(NSPAN - 1)
                dve.wait_ge(y_added, (pr + 1) * (DIRS * 3 * NSPAN) + 1)
                c0 = dve.snap(pr * NCHUNK)
                inv0 = dve.snap(pr * (2 * NCHUNK))
                gate0 = dve.snap(pr * (GATES * NCHUNK))

                def half(t):
                    return slice(3 * (t % 2), 3 * (t % 2) + 3)

                def deviate(t):
                    dve.wait_ge(mean_ready, c0 + (t + 1))
                    dve.tensor_tensor(dev[:, half(t), :], y[:, :, t * CHUNK:(t + 1) * CHUNK], ps[:, 0:3, 0:CHUNK],
                                      ALU.subtract).then_inc(dev_done, 1)

                def invert(t):
                    dve.wait_ge(var_ready, c0 + (t + 1))
                    dve.tensor_scalar(rs[:, half(t), :], ps[:, 3:6, 0:CHUNK], LN_EPS, None, ALU.add)\
                       .then_inc(inv_step, 1)
                    dve.wait_ge(inv_step, inv0 + (2 * t + 1))
                    dve.reciprocal(rs[:, half(t), :], rs[:, half(t), :]).then_inc(inv_step, 1)

                deviate(0)
                invert(0)
                for t in range(NCHUNK):
                    dv = dev[:, half(t), :]
                    if t + 1 < NCHUNK:
                        deviate(t + 1)
                    dve.wait_ge(rooted, c0 + (t + 1))
                    dve.tensor_tensor(dv, dv, rs[:, half(t), :], ALU.mult).then_inc(gate_step, 1)
                    dve.wait_ge(gate_step, gate0 + (GATES * t + 1))
                    for i in range(3):
                        dve.tensor_scalar(dv[:, i, :], dv[:, i, :], vec[:, i, V_G:V_G + 1], vec[:, i, V_B:V_B + 1],
                                          ALU.mult, ALU.add).then_inc(gate_step, 1)
                    dve.wait_ge(gate_step, gate0 + (GATES * t + 4))
                    dve.wait_ge(fin_in, pr * (80 * NCHUNK) + 80 * (t + 1))
                    dve.tensor_tensor(dv, dv, zc[:, half(t), :], ALU.mult).then_inc(gate_step, 1)
                    if t + 1 < NCHUNK:
                        invert(t + 1)
                    dve.wait_ge(share_ready, c0 + (t + 1))
                    dve.wait_ge(x_stored[t % 2], pr * (64 * OUSES[t % 2]) + (64 * (t // 2) + 64))
                    dve.tensor_tensor(oc[:, half(t), :], xr[:, half(t), :], ps[:, 0:3, 0:CHUNK],
                                      ALU.add).then_inc(out_done, 1)


def host_layout(arrays):
    import numpy as np

    f = {k: np.asarray(v) for k, v in arrays.items()}
    out = {"x": np.ascontiguousarray(f["x"].reshape(8, TOK, CH).transpose(0, 2, 1))}
    for tag in ("L0", "L1"):
        a = lambda n: f[f"{tag}_conv_{n}"]
        w = np.zeros((GROUPS, HALF, WCOLS + 3), np.float32)
        for kind, n in enumerate("qvp"):
            v = a(f"{n}_w").reshape(GROUPS, HALF, 2, HALF).transpose(0, 3, 2, 1)
            for j in range(2):
                w[:, :, (3 * j + kind) * HALF:(3 * j + kind + 1) * HALF] = v[:, :, j, :]
            w[:, :, BIAS + kind] = a(f"{n}_b").reshape(GROUPS, HALF)
        out[f"{tag}_w"] = w
        out[f"{tag}_ow"] = np.ascontiguousarray(a("o_w").T.reshape(GROUPS, HALF, CH))
        out[f"{tag}_ob"] = np.ascontiguousarray(a("o_b").reshape(2, HALF).T)
        out[f"{tag}_slope"] = np.ascontiguousarray(a("slope").reshape(GROUPS, HALF).T)
        for k in (1, 2):
            h = np.zeros((32, 96 + D1 + 4), np.float32)
            for i in range(3):
                h[:, 32 * i:32 * i + 32] = a(f"t{k}_ws")[i].T
                h[:, 96 + D1 + 1 + i] = a(f"t{k}_bs")[i]
            h[:, 96:96 + D1] = a(f"t{k}_wo").T
            h[:, 96 + D1] = a(f"t{k}_b0")
            out[f"{tag}_t{k}_hid"] = h
            out[f"{tag}_t{k}_w0"] = np.ascontiguousarray(a(f"t{k}_w0").T)
            out[f"{tag}_t{k}_bo"] = np.ascontiguousarray(a(f"t{k}_bo").reshape(GROUPS, HALF).T)
    nei = np.array([[2, 1], [1, 2], [0, 2], [0, 1], [1, 0], [2, 0]])
    k, s = np.arange(12) % 6, np.arange(12) // 6
    sign = np.where(s == 0, 1, -1)
    act = (k[:, None] + sign[:, None] * np.arange(6)[None, :]) % 6
    mult = (k[:, None] + sign[:, None] * k[None, :]) % 6 + 6 * (s[:, None] ^ s[None, :])
    ke = np.zeros((3, 3, 12, 16, 12, 16), np.float32)
    kern = f["L3_conv_kernel"]
    for g in range(12):
        for t in range(7):
            yy, xx = (1, 1) if t == 0 else nei[act[g, t - 1]]
            for h in range(12):
                ke[yy, xx, mult[g, h], :, g, :] = kern[t, h]
    ke = ke.reshape(3, 3, CH, CH)
    out["L3_w"] = np.ascontiguousarray(
        np.stack([ke[dy, dx].reshape(2, HALF, CH) for dy, dx in TAPS]).transpose(2, 1, 0, 3))
    a = lambda n: f[f"L2_conv_{n}"]

    def mixed(w):
        o = np.zeros((128, 6, 128), np.float32)
        o[:, 0] = w[:128, :128]
        o[:64, 1] = o[64:, 2] = w[128:, :128]
        o[:, 3, :64] = o[:, 4, 64:] = w[:128, 128:]
        o[:64, 5, :64] = o[64:, 5, 64:] = w[128:, 128:]
        return o

    def tiled(v):
        return np.stack([v[:128], v[:128], np.concatenate([v[128:], v[128:]])], 1)

    out["L2_ssm"], out["L2_z"] = mixed(a("in_proj_w")[:, :CH]), mixed(a("in_proj_w")[:, CH:])
    out["L2_out"] = mixed(a("out_w"))
    c = np.arange(CH)
    out["c_mixgn"] = mixed(((c[:, None] // 6 == c[None] // 6) / 6.0).astype(np.float32))
    out["c_mixln"] = mixed(np.full((CH, CH), 1.0 / CH, np.float32))
    out["L2_vec"] = np.ascontiguousarray(tiled(np.concatenate(
        [a("conv_w").reshape(CH, 9), a("conv_b")[:, None], a("ln_g")[:, None], a("ln_b")[:, None], a("Ds").T,
         a("dt_b").T, a("A_logs").transpose(1, 0, 2).reshape(CH, DIRS * STATES)], 1)))
    wx = np.zeros((DIRS, 128, 3, 128), np.float32)
    wdt = np.zeros((DIRS, 3, 128, 128), np.float32)
    for k in range(DIRS):
        w = np.zeros((CH, 64), np.float32)
        w[:, :RANK], w[:, 32:64] = a("x_proj_w")[k][:, :RANK], a("x_proj_w")[k][:, RANK:]
        wx[k, :, 0, :64] = wx[k, :, 1, 64:] = w[:128]
        wx[k, :64, 2, :64] = wx[k, 64:, 2, 64:] = w[128:]
        dt = a("dt_w")[k]
        wdt[k, 0, :RANK] = wdt[k, 1, 64:64 + RANK] = dt[:, :128]
        wdt[k, 2, :RANK, :64] = wdt[k, 2, 64:64 + RANK, 64:] = dt[:, 128:]
    out["L2_x"], out["L2_dt"] = wx, wdt
    sel = np.zeros((2, 3, STATES, 3, STATES, 128), np.float32)
    for n in range(STATES):
        sel[0, :, n, 0, n, :] = sel[1, :, n, 1, n, :] = 1.0
        sel[0, :, n, 2, n, :64] = sel[1, :, n, 2, n, 64:] = 1.0
    out["c_sel"] = sel.reshape(96, 3, STATES, 128)
    lag = np.arange(LAGS) - (SIDE - 1)
    out["c_pos"] = np.where(lag == SIDE, 0, np.where(lag >= 0, lag, -(SIDE + lag))).astype(np.float32)[None]
    out["c_expo"] = np.tile(np.where(lag == SIDE, 0, np.abs(lag)).astype(np.float32), (HALF, 1))
    out["c_ident"] = np.eye(128, dtype=np.float32)
    c = np.arange(HALF)
    out["c_gmean"] = ((c[:, None] // 6 == c[None] // 6) / 6.0).astype(np.float32)
    return out


def tno_program(nc, sems, ap, tag, x_out, x_in=None):
    consts = {k: ap[f"c_{k}"] for k in ("pos", "expo", "ident", "gmean")}
    lag = [nc.dram_tensor(f"{tag}_lag{k}", (D1, LAGS), F32).ap() for k in range(2)]
    table = [nc.dram_tensor(f"{tag}_table{k}", (SIDE, D1, SIDE), F32).ap() for k in range(2)]
    mlp = [{n: ap[f"{tag}_t{k}_{n}"] for n in ("w0", "hid", "bo")} for k in (1, 2)]
    toeplitz_tables(nc, sems, tag + "t", mlp, ap[f"{tag}_slope"], consts["pos"], consts, lag, table)
    tno_layer(nc, sems, tag, ap["x"] if x_in is None else x_in, x_out, ap[f"{tag}_w"], ap[f"{tag}_ow"],
              ap[f"{tag}_ob"], table, consts)


def network(nc, ap, out):
    consts = {k: ap[f"c_{k}"] for k in ("pos", "expo", "ident", "gmean")}
    x1, x2, x3 = (nc.dram_tensor(n, (BATCH, CH, TOK), F32).ap() for n in ("x1", "x2", "x3"))
    z = nc.dram_tensor("z", (PAIRS, 128, 3, TOK), F32).ap()
    with ExitStack() as sems:
        tno_program(nc, sems, ap, "L0", x1)
        tno_program(nc, sems, ap, "L1", x2, x1)
        scan_layer(nc, sems, "L2", x2, x3, ap, z, consts)
        conv_layer(nc, sems, "L3", x3, out, ap["L3_w"], consts)


def kernel(**inputs):
    import numpy as np
    import concourse.bacc as bacc
    from concourse.bass_utils import run_bass_kernel_spmd

    arrays = host_layout(inputs)
    nc = bacc.Bacc("TRN2", target_bir_lowering=False, num_devices=1)
    ap = {n: nc.dram_tensor(n, a.shape, F32, kind="ExternalInput").ap() for n, a in arrays.items()}
    out = nc.dram_tensor("out", (BATCH, CH, TOK), F32, kind="ExternalOutput").ap()
    network(nc, ap, out)
    r = run_bass_kernel_spmd(nc, [arrays], core_ids=[0])
    y = np.asarray(r.results[0]["out"]).reshape(BATCH, CH, TOK)
    return np.ascontiguousarray(y.transpose(0, 2, 1)).reshape(BATCH, SIDE, SIDE, CH)
```

```python
from contextlib import ExitStack

import concourse.bass as bass
from concourse import mybir

F32 = mybir.dt.float32
F32R = mybir.dt.float32r
BF16 = mybir.dt.bfloat16
ALU = mybir.AluOpType
ACT = mybir.ActivationFunctionType

BATCH, SIDE, CH = 8, 56, 192
TOK = SIDE * SIDE
HALF = CH // 2
D1 = 3 * CH
GROUPS = D1 // HALF
CHUNK = 8 * SIDE
NCHUNK = TOK // CHUNK
LAGS = 2 * SIDE
GN_EPS = 1e-5
BANK = 512

REST = 128 - HALF
XTILES = 3
WCOLS = XTILES * 3 * HALF
BIAS = WCOLS


class Pool:

    def __init__(self, nc, sems, tag):
        self.nc, self.sems, self.tag, self.ctx = nc, sems, tag, ExitStack()

    def sb(self, name, shape, dt=F32):
        return self.ctx.enter_context(self.nc.sbuf_tensor(f"{self.tag}.{name}", shape, dt))

    def ps(self, name, shape, dt=F32):
        return self.ctx.enter_context(self.nc.psum_tensor(f"{self.tag}.{name}", shape, dt))

    def sem(self, name):
        return self.sems.enter_context(self.nc.semaphore(f"{self.tag}.{name}"))


def skew(eng, g, taps, tables, done):
    for k in range(2):
        window = bass.AP(tensor=taps[k].tensor, offset=g * HALF * LAGS + SIDE - 1,
                         ap=[[LAGS, HALF], [-1, SIDE], [1, SIDE]])
        eng.dma_start(tables[k][:, g * HALF:(g + 1) * HALF, :].rearrange("w c v -> c w v"), window).then_inc(done, 16)


def toeplitz_taps(nc, sems, tag, mlp, slope, rpe, consts, taps_dram):
    m = Pool(nc, sems, tag)
    with m.ctx:
        pos = m.sb("pos", [1, LAGS])
        expo = m.sb("expo", [HALF, LAGS])
        w0 = m.sb("w0", [1, 2, 32])
        hid = m.sb("hid", [32, 2, 3 * 32 + D1 + 4])
        bo = m.sb("bo", [HALF, 2, GROUPS])
        sl = m.sb("sl", [HALF, GROUPS])
        lnsl = m.sb("lnsl", [HALF, GROUPS])
        decay = m.sb("decay", [HALF, GROUPS, LAGS])
        h = m.sb("h", [32, 2, 4, LAGS])
        taps = m.sb("taps", [HALF, 2, GROUPS, LAGS])
        ph = m.ps("ph", [32, 2, BANK])
        pa = m.ps("pa", [HALF, 2, BANK])

        loaded = m.sem("loaded")
        hidden = m.sem("hidden")
        relu = m.sem("relu")
        clipped = m.sem("clipped")
        logged = m.sem("logged")
        decayed = m.sem("decayed")
        tap_ready = m.sem("tap_ready")
        tap_done = m.sem("tap_done")
        stored = m.sem("stored")

        block = m.ctx.enter_context(nc.Block())

        @block.sync
        def _(sp):
            sp.dma_start(pos[:], rpe).then_inc(loaded, 16)
            sp.dma_start(expo[:], consts["expo"]).then_inc(loaded, 16)
            sp.dma_start(sl[:], slope).then_inc(loaded, 16)
            for k in range(2):
                sp.dma_start(w0[:, k, :], mlp[k]["w0"]).then_inc(loaded, 16)
                sp.dma_start(hid[:, k, :], mlp[k]["hid"]).then_inc(loaded, 16)
                sp.dma_start(bo[:, k, :], mlp[k]["bo"]).then_inc(loaded, 16)
            for k in range(2):
                sp.wait_ge(tap_done, GROUPS * (k + 1))
                sp.dma_start(taps_dram[k].rearrange("(g p) l -> p g l", p=HALF), taps[:, k, :, :]).then_inc(stored, 16)
            sp.wait_ge(stored, 16 * 2)

        @block.tensor
        def _(pe):
            pe.wait_ge(loaded, 9 * 16)
            for k in range(2):
                for layer in range(4):
                    if k or layer:
                        pe.wait_ge(relu, 4 * k + layer)
                    if layer == 0:
                        pe.matmul(ph[:, k, 0:LAGS], w0[:, k, :], pos[:], start=True, stop=True).then_inc(hidden, 1)
                    else:
                        pe.matmul(ph[:, k, 0:LAGS], hid[:, k, 32 * (layer - 1):32 * layer], h[:, k, layer - 1, :],
                                  start=True, stop=True).then_inc(hidden, 1)
                pe.wait_ge(relu, 4 * k + 4)
                for g in range(GROUPS):
                    n = GROUPS * k + g
                    if n >= 2:
                        pe.wait_ge(tap_done, n - 1)
                    pe.matmul(pa[:, n % 2, 0:LAGS], hid[:, k, 96 + HALF * g:96 + HALF * (g + 1)], h[:, k, 3, :],
                              start=True, stop=True).then_inc(tap_ready, 1)

        @block.scalar
        def _(act):
            for k in range(2):
                for layer in range(4):
                    act.wait_ge(hidden, 4 * k + layer + 1)
                    act.activation(h[:, k, layer, :], ph[:, k, 0:LAGS], ACT.Relu,
                                   bias=hid[:, k, 96 + D1 + layer:97 + D1 + layer]).then_inc(relu, 1)
                if k == 0:
                    act.wait_ge(clipped, 2)
                    act.activation(lnsl[:], sl[:], ACT.Ln).then_inc(logged, 1)
                    act.wait_ge(logged, 1)
                    for g in range(GROUPS):
                        act.activation(decay[:, g, :], expo[:], ACT.Exp, scale=lnsl[:, g:g + 1]).then_inc(decayed, 1)

        @block.vector
        def _(dve):
            dve.wait_ge(loaded, 9 * 16)
            dve.tensor_scalar(sl[:], sl[:], 0.0, 1.0, ALU.max, ALU.min).then_inc(clipped, 1)
            dve.wait_ge(clipped, 1)
            dve.tensor_scalar(sl[:], sl[:], 1.0 - 0.95, 0.95, ALU.mult, ALU.add).then_inc(clipped, 1)
            dve.wait_ge(decayed, GROUPS)
            for k in range(2):
                for g in range(GROUPS):
                    n = GROUPS * k + g
                    dve.wait_ge(tap_ready, n + 1)
                    dve.scalar_tensor_tensor(out=taps[:, k, g, :], in0=pa[:, n % 2, 0:LAGS], scalar=bo[:, k, g:g + 1],
                                             in1=decay[:, g, :], op0=ALU.add, op1=ALU.mult).then_inc(tap_done, 1)


def tno_layer(nc, sems, tag, x_in, x_out, weights, out_w, out_b, tables, consts, taps=None, later=None):
    m = Pool(nc, sems, tag)
    with m.ctx:
        x_res = m.sb("x_res", [HALF, 2, 2, TOK])
        xt = m.sb("xt", [128, XTILES, TOK], F32R)
        p_all = m.sb("p_all", [HALF, TOK])
        qv = m.sb("qv", [HALF, TOK])
        sq = m.sb("sq", [HALF, 2, CHUNK])
        sv = m.sb("sv", [HALF, 2, CHUNK])
        left = m.sb("left", [128, HALF, SIDE])
        right = m.sb("right", [128, HALF, SIDE])
        t_w = left[0:SIDE, :, :]
        xh = left[64:64 + SIDE, :, :]
        xw = right[0:SIDE, :, :]
        t_h = right[64:64 + SIDE, :, :]
        wg = m.sb("wg", [128, WCOLS + 3])
        w_hi = m.sb("w_hi", [128, WCOLS], F32R)
        w_lo = m.sb("w_lo", [HALF, 2 * 3 * HALF], F32R)
        bias = m.sb("bias", [HALF, 3])
        wo = m.sb("wo", [HALF, CH])
        po = m.sb("po", [HALF, 2, CHUNK])
        ident = m.sb("ident", [HALF, HALF])
        gmean = m.sb("gmean", [HALF, HALF])
        ob = m.sb("ob", [HALF, 2])
        bn = m.sb("bn", [HALF, 2, NCHUNK, 6])
        mv = m.sb("mv", [HALF, 2, 2])
        m2 = m.sb("m2", [HALF, 2])
        gs = m.sb("gs", [HALF, 4])
        gv = m.sb("gv", [HALF, 2])
        rstd = m.sb("rstd", [HALF, 2])
        shift = m.sb("shift", [HALF, 2])

        p_proj = m.ps("p_proj", [128, 2, BANK])
        p_turn = m.ps("p_turn", [128, 4, BANK])
        p_back, p_toe = p_turn[:, 0:2, :], p_turn[:, 2:4, :]
        p_out = m.ps("p_out", [128, 2, BANK])

        const_in = m.sem("const_in")
        skewed = m.sem("skewed")
        tables_made = m.sem("tables_made")
        gap_zero = m.sem("gap_zero")
        x_loaded = m.sem("x_loaded")
        w_in = m.sem("w_in")
        w_taken = m.sem("w_taken")
        wo_in = m.sem("wo_in")
        t_in = m.sem("t_in")
        x_stored = m.sem("x_stored")
        passed = m.sem("passed")
        step = m.sem("step")
        group_stats = m.sem("group_stats")
        rstd_done = m.sem("rstd_done")
        scaled = m.sem("scaled")
        normed = m.sem("normed")
        biased = m.sem("biased")
        proj_ready = m.sem("proj_ready")
        silu_done = m.sem("silu_done")
        qv_done = m.sem("qv_done")
        turn_ready = m.sem("turn_ready")
        turned = [m.sem(f"turned{s}") for s in range(2)]
        toe_ready = m.sem("toe_ready")
        toe_done = [m.sem(f"toe_done{s}") for s in range(2)]
        po_done = m.sem("po_done")
        out_ready = m.sem("out_ready")
        added = m.sem("added")

        PROJ = 3 * NCHUNK
        TURNS = 28
        HTURNS = TURNS // 2
        TOES = HALF // 8
        HTOES = TOES // 2
        SHARES = 2 * NCHUNK
        STEPS = 10
        PIECES = ((0, 2), (2, 5), (5, NCHUNK))
        NSTEPS = 6
        NORMS = NSTEPS * len(PIECES)
        P_FIRST, P_TURNED, P_SUMMED = (0, 1), (2, 3), (4, 5, 6)

        def copy_turned(copy, n):
            k = 4 * (n % HTURNS)
            squares = p_turn[0:SIDE, n % 4, 0:4 * HALF].rearrange("p (e c) -> p e c", e=4)
            return copy((xw if n < HTURNS else xh)[:, :, k:k + 4].rearrange("p c e -> p e c"), squares)

        def copy_toeplitz(copy, n):
            return copy(xw[:, 8 * n:8 * n + 8, :],
                        p_toe[0:SIDE, n % 2, 0:CHUNK].rearrange("p (c h) -> p c h", c=8))

        def steady(eng):
            eng.sem_inc(passed, 1)

        block = m.ctx.enter_context(nc.Block())

        @block.sync
        def _(sp):
            sp.sem_inc(x_stored, 16)
            sp.dma_start(ident[:], consts["ident"][0:HALF, 0:HALF]).then_inc(const_in, 16)
            sp.dma_start(gmean[:], consts["gmean"][0:HALF, 0:HALF]).then_inc(const_in, 16)
            sp.dma_start(ob[:], out_b).then_inc(const_in, 16)
            sp.wait_ge(gap_zero, 2)
            sp.dma_start(wg[:], weights[0]).then_inc(w_in, 16)
            with sp.Fori(0, BATCH) as b:
                with sp.Fori(0, GROUPS) as g:
                    it = sp.snap(b * GROUPS + g)
                    sp.wait_ge(w_taken, it * 3 + 3)
                    sp.dma_start(wg[:], weights[bass.ds((g + 1) % GROUPS, 1), :, :]
                                 .rearrange("a p n -> (a p) n")).then_inc(w_in, 16)
                    sp.wait_ge(toe_ready, it * TOES + 1)
                    sp.wait_ge(tables_made, g + 1)
                    sp.dma_start(t_w, tables[0][:, bass.ds(g * HALF, HALF), :]).then_inc(t_in, 16)
                    sp.dma_start(t_h, tables[1][:, bass.ds(g * HALF, HALF), :]).then_inc(t_in, 16)
                    sp.wait_ge(out_ready, it * SHARES + 1)
                    sp.dma_start(wo[:], out_w[bass.ds(g, 1), :, :].rearrange("a p n -> (a p) n")).then_inc(wo_in, 16)
                sp.wait_ge(added, b * (GROUPS * SHARES) + GROUPS * SHARES + 1)
                sp.dma_start(x_out[bass.ds(b, 1)].rearrange("a (j p) n -> p (a j) n", p=HALF),
                             x_res[:, bass.ds(b % 2, 1), :, :].rearrange("p a j n -> p (a j) n")).then_inc(x_stored, 16)
            sp.wait_ge(x_stored, 16 * BATCH + 16)
            sp.wait_ge(w_in, 16 * (BATCH * GROUPS + 1))

        @block.gpsimd
        def _(pool):
            def load(b):
                pool.dma_start(x_res[:, bass.ds(b % 2, 1), :, :].rearrange("p a j n -> p (a j) n"),
                               x_in[bass.ds(b, 1)].rearrange("a (j p) n -> p (a j) n", p=HALF)).then_inc(x_loaded, 16)

            def add_bias(b):
                pool.wait_ge(scaled, b * (2 * len(PIECES)) + 2 * len(PIECES))
                steady(pool)
                for j in range(2):
                    image = x_res[:, bass.ds(b % 2, 1), j, :].rearrange("p a n -> p (a n)")
                    pool.tensor_tensor(image, image, ob[:, j:j + 1].to_broadcast([HALF, TOK]), ALU.add)\
                        .then_inc(biased, 1)

            def make_tables(gs):
                for g in gs:
                    if taps is not None:
                        skew(pool, g, taps, tables, skewed)
                        pool.wait_ge(skewed, 32 * (g + 1))
                    pool.sem_inc(tables_made, 1)

            load(0)
            make_tables(range(1))
            pool.wait_ge(const_in, 48)
            add_bias(0)
            make_tables(range(1, GROUPS))
            load(1)
            if later is not None:
                for g in range(GROUPS):
                    skew(pool, g, *later, skewed)
            with pool.Fori(1, BATCH - 1) as b:
                add_bias(b)
                pool.wait_ge(x_stored, b * 16 + 16)
                load(b + 1)
            add_bias(BATCH - 1)
            if later is not None:
                pool.wait_ge(skewed, 2 * 32 * GROUPS)

        @block.tensor
        def _(pe):
            pe.wait_ge(const_in, 48)
            pe.wait_ge(gap_zero, 2)
            pe.sem_inc(toe_ready, 1)
            pe.sem_inc(out_ready, 1)
            with pe.Fori(0, BATCH) as b:
                pe.wait_ge(step, b * STEPS + 4)
                pe.wait_ge(added, b * (GROUPS * SHARES) + 1)
                pe.matmul(p_out[0:HALF, 0, 0:4], gmean[:], mv[:].rearrange("p j s -> p (j s)"),
                          start=True, stop=True).then_inc(group_stats, 1)
                with pe.Fori(0, GROUPS) as g:
                    it = pe.snap(b * GROUPS + g)
                    silu0 = pe.snap(it * PROJ + 1)
                    po0 = pe.snap(it * NCHUNK + 1)
                    added0 = pe.snap(it * SHARES + 1)
                    turned0 = pe.snap(it * HTURNS)
                    toe0 = pe.snap(it * HTOES)
                    pe.wait_ge(w_taken, it * 3 + 3)

                    def project(kind, t, s, before):
                        pe.wait_ge(silu_done, silu0 + before)
                        span = slice(t * CHUNK, (t + 1) * CHUNK)
                        passes = [(w_hi, 128, j) for j in range(XTILES)] + [(w_lo, HALF, j) for j in range(2)]
                        for q, (w, k, j) in enumerate(passes):
                            mm = pe.matmul(p_proj[0:HALF, s, 0:CHUNK],
                                           w[0:k, (3 * j + kind) * HALF:(3 * j + kind + 1) * HALF], xt[0:k, j, span],
                                           start=(q == 0), stop=(q == len(passes) - 1))
                        mm.then_inc(proj_ready, 1)

                    for t in range(NCHUNK):
                        for q, (lo, hi) in enumerate(PIECES):
                            if t == lo:
                                pe.wait_ge(normed, b * NORMS + NSTEPS * (q + 1))
                        project(0, t, 0, max(2 * t - 1, 0))
                        project(1, t, 1, max(2 * t, 0))
                    for t in P_FIRST:
                        project(2, t, t % 2, 2 * NCHUNK - 1 + t)
                    pe.wait_ge(qv_done, it * NCHUNK + NCHUNK)
                    rows = qv[:].rearrange("p (h w) -> p h w", w=SIDE)
                    cols = qv[:].rearrange("p (h w) -> p w h", w=SIDE)
                    for n in range(TURNS):
                        s = n % 2
                        if n == 0:
                            pe.wait_ge(po_done, po0)
                        elif n >= 4:
                            pe.wait_ge(turned[s], turned0 + (n // 2 - 1))
                        if n == 0 or n >= 4:
                            steady(pe)
                        src = rows if n < HTURNS else cols
                        for e in range(4):
                            mm = pe.transpose(p_turn[0:SIDE, n % 4, e * HALF:(e + 1) * HALF],
                                              src[:, 4 * (n % HTURNS) + e, :], ident[:])
                        mm.then_inc(turn_ready, 1)
                    for t in P_TURNED:
                        project(2, t, t % 2, 2 * NCHUNK - 1 + t)
                    for s in range(2):
                        pe.wait_ge(turned[s], turned0 + HTURNS)
                    pe.wait_ge(t_in, it * 32 + 32)
                    for n in range(TOES):
                        s = n % 2
                        if n >= 2:
                            pe.wait_ge(toe_done[s], toe0 + n // 2)
                        steady(pe)
                        for e in range(8):
                            c = 8 * n + e
                            mm = pe.matmul(p_toe[0:SIDE, s, e * SIDE:(e + 1) * SIDE], left[0:64 + SIDE, c, :],
                                           right[0:64 + SIDE, c, :], start=True, stop=True)
                        mm.then_inc(toe_ready, 1)
                    for t in P_SUMMED:
                        project(2, t, t % 2, 2 * NCHUNK - 1 + t)
                    for s in range(2):
                        pe.wait_ge(toe_done[s], toe0 + HTOES)
                    pe.wait_ge(wo_in, it * 16 + 16)

                    def turn_back(t):
                        if t >= 2:
                            pe.wait_ge(po_done, po0 + (t - 1))
                        steady(pe)
                        for e in range(8):
                            mm = pe.transpose(p_back[0:HALF, t % 2, e * SIDE:(e + 1) * SIDE],
                                              xw[:, :, 8 * t + e], ident[0:SIDE, 0:SIDE])
                        mm.then_inc(turn_ready, 1)

                    def share(t):
                        pe.wait_ge(po_done, po0 + (t + 1))
                        for j in range(2):
                            pe.wait_ge(added, added0 + (2 * t + j - 1 if t else 0))
                            pe.matmul(p_out[0:HALF, j, 0:CHUNK], wo[:, j * HALF:(j + 1) * HALF], po[:, t % 2, :],
                                      start=True, stop=True).then_inc(out_ready, 1)

                    turn_back(0)
                    for t in range(NCHUNK):
                        if t + 1 < NCHUNK:
                            turn_back(t + 1)
                        share(t)

        @block.scalar
        def _(act):
            act.sem_inc(silu_done, 1)
            act.wait_ge(gap_zero, 2)
            with act.Fori(0, BATCH) as b:
                act.wait_ge(step, b * STEPS + 9)
                act.activation(rstd[:], gv[:], ACT.Sqrt).then_inc(rstd_done, 1)
                act.wait_ge(step, b * STEPS + STEPS)
                act.wait_ge(po_done, b * (GROUPS * NCHUNK) + 1)
                for lo, hi in PIECES:
                    for j in range(2):
                        span = slice(lo * CHUNK, hi * CHUNK)
                        act.activation((p_all, qv)[j][:, span],
                                       x_res[:, bass.ds(b % 2, 1), j, span].rearrange("p a n -> p (a n)"),
                                       ACT.Identity, scale=rstd[:, j:j + 1], bias=shift[:, j:j + 1]).then_inc(scaled, 1)
                with act.Fori(0, GROUPS) as g:
                    it = act.snap(b * GROUPS + g)
                    proj0 = act.snap(it * PROJ)
                    qv0 = act.snap(it * NCHUNK)
                    turn0 = act.snap(it * (TURNS + NCHUNK))
                    toe0 = act.snap(it * TOES + 1)
                    act.wait_ge(w_taken, it * 3 + 3)
                    for t in range(NCHUNK):
                        if t >= 2:
                            act.wait_ge(qv_done, qv0 + (t - 1))
                        for kind, out in ((0, sq), (1, sv)):
                            act.wait_ge(proj_ready, proj0 + (2 * t + kind + 1))
                            act.activation(out[:, t % 2, :], p_proj[0:HALF, kind, 0:CHUNK], ACT.Silu,
                                           bias=bias[:, kind:kind + 1]).then_inc(silu_done, 1)

                    def silu_p(t):
                        act.wait_ge(proj_ready, proj0 + (2 * NCHUNK + t + 1))
                        act.activation(p_all[:, t * CHUNK:(t + 1) * CHUNK], p_proj[0:HALF, t % 2, 0:CHUNK], ACT.Silu,
                                       bias=bias[:, 2:3]).then_inc(silu_done, 1)

                    for t in P_FIRST:
                        silu_p(t)
                    for n in range(0, TURNS, 2):
                        act.wait_ge(turn_ready, turn0 + (n + 1))
                        copy_turned(act.copy, n).then_inc(turned[0], 1)
                    for t in P_TURNED:
                        silu_p(t)
                    for n in range(0, TOES, 2):
                        act.wait_ge(toe_ready, toe0 + (n + 1))
                        copy_toeplitz(act.copy, n).then_inc(toe_done[0], 1)
                    for t in P_SUMMED:
                        silu_p(t)

        @block.vector
        def _(dve):
            dve.sem_inc(po_done, 1)
            dve.sem_inc(added, 1)
            dve.memset(left[32:64, :, :], 0.0).then_inc(gap_zero, 1)
            dve.memset(right[32:64, :, :], 0.0).then_inc(gap_zero, 1)
            dve.wait_ge(gap_zero, 2)
            dve.wait_ge(const_in, 48)

            def take_weights(it):
                dve.wait_ge(w_in, it * 16 + 16)
                dve.wait_ge(silu_done, it * PROJ + 1)
                steady(dve)
                dve.tensor_copy(bias[:], wg[0:HALF, BIAS:BIAS + 3]).then_inc(w_taken, 1)
                dve.tensor_copy(w_hi[:], wg[:, 0:WCOLS]).then_inc(w_taken, 1)
                dve.wait_ge(w_taken, it * 3 + 2)
                dve.tensor_tensor(w_lo[:], wg[0:HALF, 0:2 * 3 * HALF], w_hi[0:HALF, 0:2 * 3 * HALF].bitcast(F32),
                                  ALU.subtract).then_inc(w_taken, 1)

            take_weights(0)
            with dve.Fori(0, BATCH) as b:
                done = [0]
                step0 = dve.snap(b * STEPS)

                def own(ins):
                    done[0] += 1
                    ins.then_inc(step, 1)
                    dve.wait_ge(step, step0 + done[0])

                def image(j, lo, n):
                    return x_res[:, bass.ds(b % 2, 1), j, lo:lo + n].rearrange("p a n -> p (a n)")

                dve.wait_ge(x_loaded, b * 16 + 16)
                for j in range(2):
                    for t in range(NCHUNK):
                        ins = dve.bn_stats(bn[:, j, t, :], image(j, t * CHUNK, CHUNK))
                own(ins)
                steady(dve)
                for j in range(2):
                    ins = dve.bn_aggr(mv[:, j, :], bn[:, j, :, :].rearrange("p t s -> p (t s)"))
                own(ins)
                own(dve.tensor_tensor(m2[:], mv[:, :, 0], mv[:, :, 0], ALU.mult))
                own(dve.tensor_tensor(mv[:, :, 1], mv[:, :, 1], m2[:], ALU.add))
                dve.wait_ge(group_stats, b + 1)
                own(dve.tensor_copy(gs[:], p_out[0:HALF, 0, 0:4]))
                own(dve.tensor_tensor(m2[:], gs[:, 0:4:2], gs[:, 0:4:2], ALU.mult))
                own(dve.tensor_tensor(gv[:], gs[:, 1:4:2], m2[:], ALU.subtract))
                own(dve.tensor_scalar(gv[:], gv[:], GN_EPS, None, ALU.add))
                own(dve.reciprocal(gv[:], gv[:]))
                dve.wait_ge(rstd_done, b + 1)
                own(dve.scalar_tensor_tensor(out=shift[:], in0=gs[:, 0:4:2], scalar=-1.0, in1=rstd[:],
                                             op0=ALU.mult, op1=ALU.mult))
                assert done[0] == STEPS
                norm0 = dve.snap(b * NORMS)
                for q, (lo, hi) in enumerate(PIECES):
                    span = slice(lo * CHUNK, hi * CHUNK)
                    for j in range(2):
                        dve.wait_ge(scaled, b * (2 * len(PIECES)) + (2 * q + j + 1))
                        dve.tensor_copy(xt[0:HALF, j, span], (p_all, qv)[j][:, span]).then_inc(normed, 1)
                    dve.wait_ge(normed, norm0 + (NSTEPS * q + 2))
                    dve.tensor_tensor(xt[0:HALF, 2, span], qv[:, span], xt[0:HALF, 1, span].bitcast(F32),
                                      ALU.subtract).then_inc(normed, 1)
                    for i in range(XTILES):
                        rows = slice(REST * i, REST * (i + 1))
                        dve.tensor_tensor(xt[HALF:128, i, span], p_all[rows, span], xt[rows, 0, span].bitcast(F32),
                                          ALU.subtract).then_inc(normed, 1)
                dve.wait_ge(normed, norm0 + NORMS)
                steady(dve)

                with dve.Fori(0, GROUPS) as g:
                    it = dve.snap(b * GROUPS + g)
                    silu0 = dve.snap(it * PROJ + 1)
                    turn0 = dve.snap(it * (TURNS + NCHUNK))
                    toe0 = dve.snap(it * TOES + 1)
                    out0 = dve.snap(it * SHARES + 1)
                    for t in range(NCHUNK):
                        dve.wait_ge(silu_done, silu0 + (2 * t + 2))
                        dve.tensor_tensor(qv[:, t * CHUNK:(t + 1) * CHUNK], sq[:, t % 2, :], sv[:, t % 2, :],
                                          ALU.mult).then_inc(qv_done, 1)
                    for n in range(1, TURNS, 2):
                        dve.wait_ge(turn_ready, turn0 + (n + 1))
                        copy_turned(dve.tensor_copy, n).then_inc(turned[1], 1)
                    for n in range(1, TOES, 2):
                        dve.wait_ge(toe_ready, toe0 + (n + 1))
                        copy_toeplitz(dve.tensor_copy, n).then_inc(toe_done[1], 1)

                    def times_p(t):
                        dve.wait_ge(silu_done, silu0 + (2 * NCHUNK + t + 1))
                        dve.wait_ge(turn_ready, turn0 + (TURNS + t + 1))
                        dve.wait_ge(out_ready, out0 + max(2 * t - 2, 0))
                        dve.tensor_tensor(po[:, t % 2, :], p_back[0:HALF, t % 2, 0:CHUNK],
                                          p_all[:, t * CHUNK:(t + 1) * CHUNK], ALU.mult).then_inc(po_done, 1)

                    def add_share(t):
                        for j in range(2):
                            dve.wait_ge(out_ready, out0 + (2 * t + j + 1))
                            place = image(j, t * CHUNK, CHUNK)
                            dve.tensor_tensor(place, place, p_out[0:HALF, j, 0:CHUNK], ALU.add).then_inc(added, 1)

                    times_p(0)
                    dve.wait_ge(biased, b * 2 + 2)
                    for t in range(NCHUNK):
                        if t + 1 < NCHUNK:
                            times_p(t + 1)
                        if t == 1:
                            take_weights(it + 1)
                        add_share(t)


TAPS = [(1, 1), (2, 1), (1, 2), (0, 2), (0, 1), (1, 0), (2, 0)]


def conv_layer(nc, sems, tag, x_in, x_out, taps_w, consts):
    m = Pool(nc, sems, tag)
    PADDED = SIDE + 2
    with m.ctx:
        x_res = m.sb("x_res", [HALF, 2, 2, TOK])
        xt = m.sb("xt", [128, 2, XTILES, PADDED, PADDED], F32R)
        whole = m.sb("whole", [128, TOK])
        W_SIZE = len(TAPS) * CH
        w_hi = m.sb("w_hi", [128, XTILES, len(TAPS), CH], F32R)
        w_lo = m.sb("w_lo", [HALF, 2, len(TAPS), CH], F32R)
        gmean = m.sb("gmean", [HALF, HALF])
        bn = m.sb("bn", [HALF, 2, NCHUNK, 6])
        mv = m.sb("mv", [HALF, 2, 2])
        m2 = m.sb("m2", [HALF, 2])
        gs = m.sb("gs", [HALF, 4])
        gv = m.sb("gv", [HALF, 2])
        rstd = m.sb("rstd", [HALF, 2])
        shift = m.sb("shift", [HALF, 2])
        p_stat = m.ps("p_stat", [128, BANK])
        p_conv = m.ps("p_conv", [128, 4, BANK])

        passed = m.sem("passed")
        const_in = m.sem("const_in")
        w_in = m.sem("w_in")
        x_loaded = m.sem("x_loaded")
        x_stored = m.sem("x_stored")
        bordered = m.sem("bordered")
        step = m.sem("step")
        group_stats = m.sem("group_stats")
        rstd_done = m.sem("rstd_done")
        scaled = m.sem("scaled")
        normed = m.sem("normed")
        w_split = m.sem("w_split")
        conv_ready = m.sem("conv_ready")
        added = m.sem("added")

        OUTS = 2 * NCHUNK
        NORMS = 6
        STEPS = 10

        def steady(eng):
            eng.sem_inc(passed, 1)

        def slot(t, b):
            return t[:, bass.ds(b % 2, 1)]

        block = m.ctx.enter_context(nc.Block())

        @block.sync
        def _(sp):
            sp.sem_inc(x_stored, 16)
            sp.dma_start(gmean[:], consts["gmean"][0:HALF, 0:HALF]).then_inc(const_in, 16)
            for j in range(XTILES):
                if j:
                    sp.wait_ge(w_split, min(2 * j, 4))
                sp.dma_start(whole[:, 0:W_SIZE], taps_w[j]).then_inc(w_in, 16)
            with sp.Fori(0, BATCH) as b:
                sp.wait_ge(added, b * OUTS + OUTS + 1)
                sp.dma_start(x_out[bass.ds(b, 1)].rearrange("a (j p) n -> p (a j) n", p=HALF),
                             slot(x_res, b).rearrange("p a j n -> p (a j) n")).then_inc(x_stored, 16)
            sp.wait_ge(x_stored, 16 * BATCH + 16)

        @block.gpsimd
        def _(pool):
            def load(b):
                pool.dma_start(slot(x_res, b).rearrange("p a j n -> p (a j) n"),
                               x_in[bass.ds(b, 1)].rearrange("a (j p) n -> p (a j) n", p=HALF)).then_inc(x_loaded, 16)

            load(0)
            pool.memset(xt[:].bitcast(F32), 0.0).then_inc(bordered, 1)
            with pool.Fori(1, BATCH) as b:
                pool.wait_ge(normed, b * NORMS)
                pool.wait_ge(x_stored, b * 16)
                load(b)

        @block.tensor
        def _(pe):
            pe.wait_ge(const_in, 16)
            pe.sem_inc(conv_ready, 1)

            def stats(b):
                pe.wait_ge(step, b * STEPS + 4)
                pe.matmul(p_stat[0:HALF, 0:4], gmean[:], mv[:].rearrange("p j s -> p (j s)"),
                          start=True, stop=True).then_inc(group_stats, 1)

            def conv(b, ahead):
                added0 = pe.snap(b * OUTS)
                pe.wait_ge(normed, b * NORMS + NORMS)
                for t in range(NCHUNK):
                    if t == 3 and ahead:
                        stats(b + 1)
                    for j in range(2):
                        n = 2 * t + j
                        pe.wait_ge(added, added0 + max(n - 3 + 1, 1))
                        k = 0
                        for i, (dy, dx) in enumerate(TAPS):
                            for w, rows, q in ([(w_hi, 128, q) for q in range(XTILES)]
                                               + [(w_lo, HALF, q) for q in range(2)]):
                                mm = pe.matmul(p_conv[0:HALF, n % 4, 0:CHUNK],
                                               w[0:rows, q, i, j * HALF:(j + 1) * HALF],
                                               xt[0:rows, bass.ds(b % 2, 1), q, 8 * t + dy:8 * t + dy + 8, dx:dx + SIDE]
                                               .rearrange("p a h w -> p (a h) w"),
                                               start=(k == 0), stop=(k == 5 * len(TAPS) - 1))
                                k += 1
                        mm.then_inc(conv_ready, 1)

            stats(0)
            pe.wait_ge(w_split, 5)
            with pe.Fori(0, BATCH - 1) as b:
                conv(b, True)
            conv(BATCH - 1, False)

        @block.scalar
        def _(act):
            act.wait_ge(w_split, 5)

            def norm(b):
                act.wait_ge(step, b * STEPS + 9)
                act.activation(rstd[:], gv[:], ACT.Sqrt).then_inc(rstd_done, 1)
                act.wait_ge(step, b * STEPS + STEPS)
                for j in range(2):
                    if not (isinstance(b, int) and b == 0 and j == 0):
                        act.wait_ge(normed, b * NORMS + 4 * j)
                    act.activation(whole[0:HALF, :], x_res[:, bass.ds(b % 2, 1), j, :].rearrange("p a n -> p (a n)"),
                                   ACT.Identity, scale=rstd[:, j:j + 1], bias=shift[:, j:j + 1]).then_inc(scaled, 1)

            norm(0)
            with act.Fori(1, BATCH) as b:
                norm(b)

        @block.vector
        def _(dve):
            dve.sem_inc(added, 1)

            def stats(b):
                done = [0]
                step0 = dve.snap(b * STEPS) if not isinstance(b, int) else b * STEPS

                def own(ins):
                    done[0] += 1
                    ins.then_inc(step, 1)
                    dve.wait_ge(step, step0 + done[0])

                dve.wait_ge(x_loaded, b * 16 + 16)
                for j in range(2):
                    for t in range(NCHUNK):
                        ins = dve.bn_stats(bn[:, j, t, :], x_res[:, bass.ds(b % 2, 1), j, t * CHUNK:(t + 1) * CHUNK]
                                           .rearrange("p a n -> p (a n)"))
                own(ins)
                steady(dve)
                for j in range(2):
                    ins = dve.bn_aggr(mv[:, j, :], bn[:, j, :, :].rearrange("p t s -> p (t s)"))
                own(ins)
                own(dve.tensor_tensor(m2[:], mv[:, :, 0], mv[:, :, 0], ALU.mult))
                own(dve.tensor_tensor(mv[:, :, 1], mv[:, :, 1], m2[:], ALU.add))
                dve.wait_ge(group_stats, b + 1)
                own(dve.tensor_copy(gs[:], p_stat[0:HALF, 0:4]))
                own(dve.tensor_tensor(m2[:], gs[:, 0:4:2], gs[:, 0:4:2], ALU.mult))
                own(dve.tensor_tensor(gv[:], gs[:, 1:4:2], m2[:], ALU.subtract))
                own(dve.tensor_scalar(gv[:], gv[:], GN_EPS, None, ALU.add))
                own(dve.reciprocal(gv[:], gv[:]))
                dve.wait_ge(rstd_done, b + 1)
                dve.scalar_tensor_tensor(out=shift[:], in0=gs[:, 0:4:2], scalar=-1.0, in1=rstd[:],
                                         op0=ALU.mult, op1=ALU.mult).then_inc(step, 1)
                assert done[0] + 1 == STEPS

            def add(b, ns):
                out0 = dve.snap(b * OUTS + 1) if not isinstance(b, int) else b * OUTS + 1
                dve.wait_ge(normed, b * NORMS + NORMS)
                for n in ns:
                    t, j = n // 2, n % 2
                    dve.wait_ge(conv_ready, out0 + (n + 1))
                    place = x_res[:, bass.ds(b % 2, 1), j, t * CHUNK:(t + 1) * CHUNK].rearrange("p a n -> p (a n)")
                    dve.tensor_tensor(place, place, p_conv[0:HALF, n % 4, 0:CHUNK], ALU.add).then_inc(added, 1)

            def split(b, j):
                image = whole[:].rearrange("p (h w) -> p h w", w=SIDE)

                def inner(rows, q):
                    return xt[rows, bass.ds(b % 2, 1), q, 1:SIDE + 1, 1:SIDE + 1].rearrange("p a h w -> p (a h) w")

                half = slice(0, HALF)
                dve.wait_ge(scaled, b * 2 + j + 1)
                steady(dve)
                dve.tensor_copy(inner(half, j), image[half]).then_inc(normed, 1)
                dve.wait_ge(normed, b * NORMS + 4 * j + 1)
                steady(dve)
                if j == 0:
                    for i in range(XTILES):
                        rows = slice(REST * i, REST * (i + 1))
                        dve.tensor_tensor(inner(slice(HALF, 128), i), image[rows], inner(rows, 0).bitcast(F32),
                                          ALU.subtract).then_inc(normed, 1)
                else:
                    dve.tensor_tensor(inner(half, 2), image[half], inner(half, 1).bitcast(F32),
                                      ALU.subtract).then_inc(normed, 1)

            for j in range(XTILES):
                dve.wait_ge(w_in, 16 * (j + 1))
                hi = w_hi[:, j].rearrange("p i c -> p (i c)")
                dve.tensor_copy(hi, whole[:, 0:W_SIZE]).then_inc(w_split, 1)
                if j < 2:
                    dve.wait_ge(w_split, 2 * j + 1)
                    dve.tensor_tensor(w_lo[:, j].rearrange("p i c -> p (i c)"), whole[0:HALF, 0:W_SIZE],
                                      hi[0:HALF].bitcast(F32), ALU.subtract).then_inc(w_split, 1)
            dve.wait_ge(bordered, 1)
            stats(0)
            for j in range(2):
                split(0, j)
            with dve.Fori(0, BATCH - 1) as b:
                add(b, range(2))
                stats(b + 1)
                add(b, range(2, 5))
                split(b + 1, 0)
                add(b, range(5, 8))
                split(b + 1, 1)
                add(b, range(8, OUTS))
            add(BATCH - 1, range(OUTS))


PAIRS = 4
STATES, DIRS, RANK = 16, 4, 12
LN_EPS = 1e-5
SPAN = 784
HSPAN = SPAN // 2
RING = 4
NSPAN = TOK // SPAN
PADDED = SIDE + 2
MIX = [[(0, 0), (1, 2)], [(0, 1), (2, 2)], [(3, 0), (4, 1), (5, 2)]]
V_CONV, V_CB, V_G, V_B, V_D, V_DT, V_A, V_END = 0, 9, 10, 11, 12, 16, 20, 84


def scan_layer(nc, sems, tag, x_in, x_out, ap, z_dram, consts):
    m = Pool(nc, sems, tag)
    with m.ctx:
        U_SIZE = 16128
        u = m.sb("u", [128, U_SIZE])

        def view(at, *shape, dt=F32):
            n = 1
            for s in shape:
                n *= s
            words = n if dt is F32 else n // 2
            assert at + words <= U_SIZE
            v = u[:, at:at + words]
            if dt is not F32:
                v = v.bitcast(dt)
            if len(shape) == 2:
                return v.rearrange("p (a b) -> p a b", a=shape[0])
            if len(shape) == 3:
                return v.rearrange("p (a b c) -> p a b c", a=shape[0], b=shape[1])
            return v

        xn = view(0, 3, TOK)
        pad = view(3 * TOK, PADDED, PADDED)
        sel_f = u[0:96, 0:3 * STATES * 128].rearrange("p (a b c) -> p a b c", a=3, b=STATES)
        zs = view(U_SIZE - 2 * CHUNK, 2, CHUNK)
        f = view(0, TOK)
        rest = view(TOK, TOK)
        part = [view(2 * TOK + i * TOK // 2, TOK, dt=BF16) for i in range(3)]
        one_e = view(7 * TOK // 2, TOK)
        t_ln = view(9 * TOK // 2, 2, 2 * CHUNK)
        db = view(TOK, RING, SPAN)
        hs = view(TOK + RING * SPAN, RING, SPAN)
        hc = view(TOK + 2 * RING * SPAN, RING, SPAN)
        da = view(TOK + 3 * RING * SPAN, 2, SPAN)
        cb = view(TOK + (3 * RING + 2) * SPAN, 2, SPAN)
        dev = view(0, 6, CHUNK)
        squ = view(6 * CHUNK, 3, CHUNK)
        rs = view(9 * CHUNK, 2, CHUNK)
        zc, xr, oc = (view((15 + 6 * i) * CHUNK, 6, CHUNK) for i in range(3))

        xc = m.sb("xc", [128, 3, TOK])
        y = m.sb("y", [128, 3, TOK])
        d = m.sb("d", [128, TOK])
        du = m.sb("du", [128, TOK])
        bs = m.sb("bs", [96, TOK], BF16)
        cs = m.sb("cs", [96, TOK], BF16)
        sel = m.sb("sel", [96, 3, STATES, 128], BF16)
        ln1 = m.sb("ln1", [128, 1])
        state = m.sb("state", [128, STATES])
        vec = m.sb("vec", [128, 3, V_END])
        dsum = m.sb("dsum", [128, 3])
        dtb = m.sb("dtb", [128, 3 * DIRS])
        nega = m.sb("nega", [128, 3 * DIRS * STATES])
        ident = m.sb("ident", [128, 128])
        w_ssm, w_z, w_gn, w_ln, w_out = (m.sb(n, [128, 6, 128]) for n in ("w_ssm", "w_z", "w_gn", "w_ln", "w_out"))
        w_x = m.sb("w_x", [128, 3, 128])
        w_spread = m.sb("w_spread", [128, 3, 128])
        w_dt = m.sb("w_dt", [128, 128])
        bn = m.sb("bn", [128, 3, NCHUNK, 6])
        mv = m.sb("mv", [128, 3, 2])
        m2 = m.sb("m2", [128, 3])
        gs = m.sb("gs", [128, 6])
        gv = m.sb("gv", [128, 3])
        rstd = m.sb("rstd", [128, 3])
        shift = m.sb("shift", [128, 3])
        ps = m.ps("ps", [128, 8, BANK])

        passed = m.sem("passed")
        const_in = m.sem("const_in")
        exp_made = m.sem("exp_made")
        made2 = m.sem("made2")
        made = m.sem("made")
        x_loaded = m.sem("x_loaded")
        step = m.sem("step")
        gn_ready = m.sem("gn_ready")
        rstd_done = m.sem("rstd_done")
        normed = m.sem("normed")
        mix_ready = m.sem("mix_ready")
        mix_out = m.sem("mix_out")
        z_stored = [m.sem(f"z_stored{i}") for i in range(2)]
        bordered = m.sem("bordered")
        tap_done = m.sem("tap_done")
        xc_done = m.sem("xc_done")
        y_init = m.sem("y_init")
        wx_in = m.sem("wx_in")
        wdt_in = m.sem("wdt_in")
        f_ready = m.sem("f_ready")
        f_out = m.sem("f_out")
        split = m.sem("split")
        gathered = m.sem("gathered")
        dt_ready = m.sem("dt_ready")
        sp_done = m.sem("sp_done")
        d_step = m.sem("d_step")
        b_ready = m.sem("b_ready")
        c_ready = m.sem("c_ready")
        c_out = m.sem("c_out")
        a_ready = m.sem("a_ready")
        b_done = m.sem("b_done")
        zeroed = m.sem("zeroed")
        scanned = m.sem("scanned")
        kept = m.sem("kept")
        hc_done = m.sem("hc_done")
        y_ready = m.sem("y_ready")
        y_added = m.sem("y_added")
        fin_in = m.sem("fin_in")
        mean_ready = m.sem("mean_ready")
        var_ready = m.sem("var_ready")
        inv_ready = m.sem("inv_ready")
        share_ready = m.sem("share_ready")
        dev_done = m.sem("dev_done")
        inv_step = m.sem("inv_step")
        gate_step = m.sem("gate_step")
        squared = m.sem("squared")
        rooted = m.sem("rooted")
        out_done = m.sem("out_done")
        x_stored = [m.sem(f"x_stored{i}") for i in range(2)]

        MIXES = 6 * NCHUNK
        ZUSES = (11, 10)
        OUSES = (4, 3)
        STEPS, TAPS9, SPLITS, GATES = 10, 9, 8, 5
        GATHER = 12 * 16
        TILE_N = NSPAN * STATES
        CONSTS = 9
        DPIECES = [(lo, min(lo + 2, NCHUNK)) for lo in range(0, NCHUNK, 2)]
        ND = len(DPIECES)
        assert SPAN <= 2 * CHUNK

        def steady(eng):
            eng.sem_inc(passed, 1)

        def image_view(flat, k):
            return flat.rearrange("p (h w) -> p h w", w=SIDE) if k < 2 else flat.rearrange("p (h w) -> p w h", w=SIDE)

        def scan_view(flat, k):
            g = image_view(flat, k)
            return g[:, ::-1, ::-1] if k % 2 else g

        def tile(t, i):
            return t[:, bass.ds(i, 1), :].rearrange("p a n -> p (a n)")

        def image_parts(dram, pr, place, lo=0, n=TOK):
            for e in range(2):
                row = dram[bass.ds(2 * pr + e, 1), :, lo:lo + n]
                yield place(e), row[:, 0:128, :].rearrange("a p n -> (a p) n")
                yield place(2)[64 * e:64 * e + 64, :], row[:, 128:CH, :].rearrange("a p n -> (a p) n")

        block = m.ctx.enter_context(nc.Block())

        @block.sync
        def _(sp):
            for place, src in ((sel_f, ap["c_sel"]), (ident[:], consts["ident"]), (vec[:], ap["L2_vec"]),
                               (w_ssm[:], ap["L2_ssm"]), (w_z[:], ap["L2_z"]), (w_gn[:], ap["c_mixgn"]),
                               (w_ln[:], ap["c_mixln"]), (w_out[:], ap["L2_out"]), (w_spread[:], ap["c_spread"])):
                sp.dma_start(place, src).then_inc(const_in, 16)
            sp.wait_ge(made, 1)
            with sp.Fori(0, PAIRS) as pr:
                sp.wait_ge(out_done, pr * NCHUNK + 1)
                for s in range(2):
                    sp.wait_ge(x_stored[s], pr * (64 * OUSES[s]) + 64)
                for place, src in image_parts(x_in, pr, lambda i: xn[:, i, :]):
                    sp.dma_start(place, src).then_inc(x_loaded, 16)
                for n in range(3 * NCHUNK):
                    i, t = n // NCHUNK, n % NCHUNK
                    sp.wait_ge(mix_out, pr * MIXES + (2 * NCHUNK * i + NCHUNK + t + 2))
                    sp.dma_start(z_dram[bass.ds(pr, 1), :, i, t * CHUNK:(t + 1) * CHUNK]
                                 .rearrange("a p n -> (a p) n"), zs[:, n % 2, :]).then_inc(z_stored[n % 2], 16)
                for k in range(DIRS):
                    it = sp.snap(pr * DIRS + k)
                    sp.wait_ge(dt_ready, it * (3 * NCHUNK) + 1)
                    sp.dma_start(w_x[:], ap["L2_x"][k]).then_inc(wx_in, 16)

                    def load_dt(i):
                        sp.wait_ge(dt_ready, it * (3 * NCHUNK) + i * NCHUNK + 1)
                        sp.dma_start(w_dt[:], ap["L2_dt"][k][bass.ds(i, 1), :, :].rearrange("a p n -> (a p) n"))\
                          .then_inc(wdt_in, 16)

                    load_dt(0)
                    sp.wait_ge(split, it * SPLITS + SPLITS)
                    sp.wait_ge(y_ready, it * (3 * TILE_N) + RING)
                    for dst, row in ((bs, 32), (cs, 48)):
                        for e in range(2):
                            for i in range(3):
                                at = 48 * e + 16 * i
                                sp.dma_start(dst[at:at + 16, :],
                                             part[i][64 * e + row:64 * e + row + 16, :]).then_inc(gathered, 16)
                    with sp.Fori(1, 3) as i:
                        load_dt(i)
                sp.wait_ge(y_added, pr * (DIRS * 3 * NSPAN) + DIRS * 3 * NSPAN + 1)
                for s in range(2):
                    sp.wait_ge(z_stored[s], pr * (16 * ZUSES[s]) + 16 * ZUSES[s])

                def load(t):
                    s = t % 2
                    sp.dma_start(zc[:, 3 * s:3 * s + 3, :],
                                 z_dram[bass.ds(pr, 1), :, :, t * CHUNK:(t + 1) * CHUNK]
                                 .rearrange("a p i n -> (a p) i n")).then_inc(fin_in, 16)
                    for place, src in image_parts(x_in, pr, lambda i: xr[:, 3 * s + i, :], t * CHUNK, CHUNK):
                        sp.dma_start(place, src).then_inc(fin_in, 16)

                load(0)
                for t in range(NCHUNK):
                    s = t % 2
                    if t + 1 < NCHUNK:
                        sp.wait_ge(fin_in, pr * (80 * NCHUNK) + 80 * (t + 1))
                        if t >= 1:
                            sp.wait_ge(out_done, pr * NCHUNK + t + 1)
                        load(t + 1)
                    sp.wait_ge(out_done, pr * NCHUNK + t + 2)
                    for place, dst in image_parts(x_out, pr, lambda i: oc[:, 3 * s + i, :], t * CHUNK, CHUNK):
                        sp.dma_start(dst, place).then_inc(x_stored[s], 16)
            for s in range(2):
                sp.wait_ge(x_stored[s], 64 * OUSES[s] * PAIRS + 64)

        @block.gpsimd
        def _(pool):
            pool.sem_inc(kept, STATES)
            pool.sem_inc(hc_done, RING)
            pool.wait_ge(made, 1)
            with pool.Fori(0, PAIRS) as pr:
                pool.wait_ge(out_done, pr * NCHUNK + 1)
                for s in range(2):
                    pool.wait_ge(x_stored[s], pr * (64 * OUSES[s]) + 64)
                steady(pool)
                pool.memset(pad[:], 0.0).then_inc(bordered, 1)
                with pool.Fori(0, DIRS) as k:
                    it = pool.snap(pr * DIRS + k)
                    split0 = pool.snap(it * SPLITS)
                    for q, (lo, hi) in enumerate(((0, 3), (3, NCHUNK))):
                        span = slice(lo * CHUNK, hi * CHUNK)
                        pool.wait_ge(f_out, it * NCHUNK + hi)
                        steady(pool)
                        pool.tensor_copy(part[0][:, span], f[:, span]).then_inc(split, 1)
                        pool.wait_ge(split, split0 + (4 * q + 1))
                        pool.tensor_tensor(rest[:, span], f[:, span], part[0][:, span], ALU.subtract).then_inc(split, 1)
                        pool.wait_ge(split, split0 + (4 * q + 2))
                        steady(pool)
                        pool.tensor_copy(part[1][:, span], rest[:, span]).then_inc(split, 1)
                        pool.wait_ge(split, split0 + (4 * q + 3))
                        pool.tensor_tensor(part[2][:, span], rest[:, span], part[1][:, span], ALU.subtract)\
                            .then_inc(split, 1)
                    with pool.Fori(0, 3 * NSPAN) as c:
                        n0 = pool.snap((it * (3 * NSPAN) + c) * STATES)
                        for n in range(STATES):
                            r = n % RING
                            pool.wait_ge(scanned, n0 + (n + 1 + RING))
                            steady(pool)
                            pool.tensor_copy(state[:, n:n + 1], hs[:, r, SPAN - 1:SPAN]).then_inc(kept, 1)
                            pool.wait_ge(c_out, n0 + (n + 1))
                            pool.wait_ge(y_ready, n0 + (n + 1))
                            pool.tensor_tensor(hc[:, r, :], hs[:, r, :], cb[:, n % 2, :], ALU.mult)\
                                .then_inc(hc_done, 1)

        @block.tensor
        def _(pe):
            pe.sem_inc(dt_ready, 1)
            pe.sem_inc(y_ready, RING)
            pe.wait_ge(const_in, 16 * CONSTS)
            pe.wait_ge(made, 1)

            def mix(w, src, out_of, i):
                for q, (w_i, s_i) in enumerate(MIX[i]):
                    mm = pe.matmul(out_of, w[:, w_i, :], src(s_i), start=(q == 0), stop=(q == len(MIX[i]) - 1))
                return mm

            with pe.Fori(0, PAIRS) as pr:
                pe.wait_ge(out_done, pr * NCHUNK + 1)
                pe.wait_ge(step, pr * STEPS + 4)
                for i in range(3):
                    mm = mix(w_gn, lambda s: mv[:, s, :], ps[:, 7, 2 * i:2 * i + 2], i)
                mm.then_inc(gn_ready, 1)
                pe.wait_ge(normed, pr * 3 + 3)
                out0 = pe.snap(pr * MIXES)
                for n in range(MIXES):
                    i, q = n // (2 * NCHUNK), n % (2 * NCHUNK)
                    t = q % NCHUNK
                    if n >= 4:
                        pe.wait_ge(mix_out, out0 + (n - 4 + 2))
                    mix(w_ssm if q < NCHUNK else w_z, lambda s: xn[:, s, t * CHUNK:(t + 1) * CHUNK],
                        ps[:, n % 4, 0:CHUNK], i).then_inc(mix_ready, 1)

                for k in range(DIRS):
                    it = pe.snap(pr * DIRS + k)
                    pe.wait_ge(wx_in, it * 16 + 16)
                    pe.wait_ge(xc_done, pr * 3 + 3)
                    for t in range(NCHUNK):
                        if t >= 2:
                            pe.wait_ge(f_out, it * NCHUNK + (t - 1))
                        for i in range(3):
                            mm = pe.matmul(ps[:, t % 2, 0:CHUNK], w_x[:, i, :],
                                           scan_view(xc[:, i, :], k)[:, 8 * t:8 * t + 8, :],
                                           start=(i == 0), stop=(i == 2))
                        mm.then_inc(f_ready, 1)
                    pe.wait_ge(f_out, it * NCHUNK + NCHUNK)
                    steady(pe)
                    with pe.Fori(0, 3) as i:
                        ti = pe.snap(it * 3 + i)
                        sp0 = pe.snap(ti * (4 * ND))
                        pe.wait_ge(wdt_in, ti * 16 + 16)
                        for t in range(NCHUNK):
                            if t >= 4 and t % 2 == 0:
                                pe.wait_ge(sp_done, sp0 + (3 * (t // 2 - 2) + 2))
                            pe.matmul(ps[:, t % 4, 0:CHUNK], w_dt[:], f[:, t * CHUNK:(t + 1) * CHUNK],
                                      start=True, stop=True).then_inc(dt_ready, 1)
                        pe.wait_ge(sp_done, sp0 + 3 * ND)
                        pe.wait_ge(gathered, it * GATHER + GATHER)
                        steady(pe)

                        def spread(rows, c, n, bank):
                            at = (c + n // STATES) * SPAN
                            for h in range(2):
                                mm = pe.matmul(ps[:, bank + h, 0:HSPAN],
                                               sel[:, bass.ds(i, 1), n % STATES, :].rearrange("p a m -> p (a m)"),
                                               rows[:, bass.ds(at + h * HSPAN, HSPAN)], start=True, stop=True)
                            return mm

                        def b_row(c, n, n0):
                            if n >= 2:
                                pe.wait_ge(b_done, n0 + (n - 1))
                                steady(pe)
                            spread(bs, c, n, 2 * (n % 2)).then_inc(b_ready, 1)

                        def c_row(c, n, n0):
                            if n >= 1:
                                pe.wait_ge(c_out, n0 + n)
                                steady(pe)
                            spread(cs, c, n, 4).then_inc(c_ready, 1)

                        def sum_span(c, last):
                            n0 = pe.snap((ti * NSPAN + c) * STATES)

                            def share(n):
                                pe.wait_ge(hc_done, n0 + (n + 1 + RING))
                                if n == 0:
                                    pe.wait_ge(y_added, ti * NSPAN + c + 1)
                                for h in range(2):
                                    mm = pe.matmul(ps[:, 6 + h, 0:HSPAN], ident[:],
                                                   hc[:, n % RING, h * HSPAN:(h + 1) * HSPAN],
                                                   start=(n == 0), stop=(n == STATES - 1))
                                mm.then_inc(y_ready, 1)

                            for n in range(STATES):
                                if n + 3 < STATES or not last:
                                    b_row(c, n + 3, n0)
                                if n + 2 < STATES or not last:
                                    c_row(c, n + 2, n0)
                                share(n)

                        first = pe.snap(ti * TILE_N)
                        b_row(0, 0, first)
                        c_row(0, 0, first)
                        b_row(0, 1, first)
                        b_row(0, 2, first)
                        c_row(0, 1, first)
                        with pe.Fori(0, NSPAN - 1) as c:
                            sum_span(c, False)
                        sum_span(NSPAN - 1, True)
                pe.wait_ge(y_added, (pr + 1) * (DIRS * 3 * NSPAN) + 1)
                c0 = pe.snap(pr * NCHUNK)

                def moments(t):
                    if t == 1:
                        pe.wait_ge(dev_done, c0 + 1)
                    elif t >= 2:
                        pe.wait_ge(out_done, c0 + t)
                    for i in range(3):
                        mm = mix(w_ln, lambda s: y[:, s, t * CHUNK:(t + 1) * CHUNK], ps[:, i, 0:CHUNK], i)
                    mm.then_inc(mean_ready, 1)
                    pe.wait_ge(squared, c0 + (t + 1))
                    if t >= 1:
                        pe.wait_ge(inv_step, pr * (2 * NCHUNK) + (2 * t - 1))
                    mix(w_ln, lambda s: squ[:, s, :], ps[:, 6, 0:CHUNK], 2).then_inc(var_ready, 1)

                def spread_inv(t):
                    pe.wait_ge(rooted, c0 + (t + 1))
                    if t >= 1:
                        pe.wait_ge(gate_step, pr * (GATES * NCHUNK) + (GATES * (t - 1) + 1))
                    for i in range(3):
                        mm = pe.matmul(ps[:, 3 + i, 0:CHUNK], w_spread[:, i, :], rs[:, t % 2, :], start=True, stop=True)
                    mm.then_inc(inv_ready, 1)

                moments(0)
                spread_inv(0)
                for t in range(NCHUNK):
                    if t + 1 < NCHUNK:
                        moments(t + 1)
                        pe.wait_ge(dev_done, c0 + (t + 2))
                    pe.wait_ge(gate_step, pr * (GATES * NCHUNK) + GATES * (t + 1))
                    for i in range(3):
                        mm = mix(w_out, lambda s: dev[:, 3 * (t % 2) + s, :], ps[:, i, 0:CHUNK], i)
                    mm.then_inc(share_ready, 1)
                    if t + 1 < NCHUNK:
                        spread_inv(t + 1)

        @block.scalar
        def _(act):
            act.sem_inc(mix_out, 1)
            act.wait_ge(const_in, 16 * CONSTS)
            act.activation(vec[:, :, V_A:V_END], vec[:, :, V_A:V_END], ACT.Exp).then_inc(exp_made, 1)
            act.wait_ge(made2, 1)
            act.activation(ln1[:], ln1[:], ACT.Ln).then_inc(exp_made, 1)
            act.wait_ge(made, 1)
            with act.Fori(0, PAIRS) as pr:
                act.wait_ge(step, pr * STEPS + 9)
                act.activation(rstd[:], gv[:], ACT.Sqrt).then_inc(rstd_done, 1)
                mix0 = act.snap(pr * MIXES)

                def silu_xc(i):
                    act.wait_ge(tap_done, pr * (3 * TAPS9) + (TAPS9 * (i + 1) + 1))
                    act.activation(xc[:, i, :], xc[:, i, :], ACT.Silu).then_inc(xc_done, 1)

                for n in range(MIXES):
                    i, q = n // (2 * NCHUNK), n % (2 * NCHUNK)
                    t = q % NCHUNK
                    if q >= NCHUNK:
                        zi = NCHUNK * i + t
                        if zi >= 2:
                            act.wait_ge(z_stored[zi % 2], pr * (16 * ZUSES[zi % 2]) + 16 * (zi // 2))
                        act.wait_ge(mix_ready, mix0 + (n + 1))
                        act.activation(zs[:, zi % 2, :], ps[:, n % 4, 0:CHUNK], ACT.Silu).then_inc(mix_out, 1)
                    else:
                        if t == 0 and i:
                            silu_xc(i - 1)
                        if t == 0 and not i:
                            act.wait_ge(bordered, pr + 1)
                        act.wait_ge(mix_ready, mix0 + (n + 1))
                        act.copy(pad[:, 1 + 8 * t:9 + 8 * t, 1:1 + SIDE],
                                 ps[:, n % 4, 0:CHUNK].rearrange("p (h w) -> p h w", w=SIDE)).then_inc(mix_out, 1)
                silu_xc(2)

                for k in range(DIRS):
                    it = act.snap(pr * DIRS + k)
                    for t in range(NCHUNK):
                        act.wait_ge(f_ready, it * NCHUNK + (t + 1))
                        act.copy(f[:, t * CHUNK:(t + 1) * CHUNK], ps[:, t % 2, 0:CHUNK]).then_inc(f_out, 1)
                    with act.Fori(0, 3) as i:
                        ti = act.snap(it * 3 + i)
                        sp0 = act.snap(ti * (4 * ND))
                        dt0 = act.snap(ti * NCHUNK + 1)
                        d0 = act.snap(ti * (5 * ND))
                        bias = dtb[:, bass.ds(i * DIRS + k, 1)]
                        for h in range(2):
                            act.wait_ge(z_stored[h], (pr + 1) * (16 * ZUSES[h]))
                        steady(act)
                        for q, (lo, hi) in enumerate(DPIECES):
                            x = ps[:, lo % 4:lo % 4 + hi - lo, 0:CHUNK]
                            d_q, e_q = (v[:, lo * CHUNK:hi * CHUNK].rearrange("p (a n) -> p a n", a=hi - lo)
                                        for v in (d, du))
                            act.wait_ge(dt_ready, dt0 + hi)
                            steady(act)
                            act.activation(e_q, x, ACT.Abs, bias=bias).then_inc(sp_done, 1)
                            act.activation(d_q, x, ACT.Relu, bias=bias).then_inc(sp_done, 1)
                            act.wait_ge(sp_done, sp0 + (3 * q + 1))
                            act.activation(e_q, e_q, ACT.Exp, scale=-1.0).then_inc(sp_done, 1)
                        for q, (lo, hi) in enumerate(DPIECES):
                            act.wait_ge(d_step, d0 + (3 * q + 1))
                            if q >= 2:
                                act.wait_ge(d_step, d0 + (3 * ND + max(2 * (q - 2), 1)))
                            act.activation(t_ln[:, q % 2, 0:(hi - lo) * CHUNK], one_e[:, lo * CHUNK:hi * CHUNK], ACT.Ln)\
                               .then_inc(sp_done, 1)

                        def decay(c, n, n0):
                            act.wait_ge(scanned, n0 + (n + 3))
                            steady(act)
                            act.activation(da[:, n % 2, :], d[:, bass.ds((c + n // STATES) * SPAN, SPAN)], ACT.Exp,
                                           scale=nega[:, bass.ds(i * (DIRS * STATES) + (k * STATES + n % STATES), 1)])\
                               .then_inc(a_ready, 1)

                        def decay_span(c, last):
                            n0 = act.snap((ti * NSPAN + c) * STATES)
                            for n in range(STATES):
                                if n + 1 < STATES or not last:
                                    decay(c, n + 1, n0)
                                act.wait_ge(c_ready, n0 + (n + 1))
                                act.wait_ge(hc_done, n0 + (n + 3))
                                act.copy(cb[:, n % 2, :].rearrange("p (a n) -> p a n", a=2),
                                         ps[:, 4:6, 0:HSPAN]).then_inc(c_out, 1)

                        act.wait_ge(d_step, d0 + (3 * ND + 1))
                        act.wait_ge(sp_done, sp0 + 4 * ND)
                        decay(0, 0, act.snap(ti * (NSPAN * STATES)))
                        act.wait_ge(d_step, d0 + 5 * ND)
                        for c in range(NSPAN):
                            decay_span(c, c == NSPAN - 1)
                c0 = act.snap(pr * NCHUNK)
                for t in range(NCHUNK):
                    part_of = slice(3 * (t % 2), 3 * (t % 2) + 3)
                    act.wait_ge(dev_done, c0 + (t + 1))
                    if t >= 1:
                        act.wait_ge(var_ready, c0 + t)
                    act.activation(squ[:], dev[:, part_of, :], ACT.Square).then_inc(squared, 1)
                    act.wait_ge(inv_step, pr * (2 * NCHUNK) + (2 * t + 2))
                    act.activation(rs[:, t % 2, :], rs[:, t % 2, :], ACT.Sqrt).then_inc(rooted, 1)

        @block.vector
        def _(dve):
            dve.sem_inc(tap_done, 1)
            dve.sem_inc(scanned, RING)
            dve.sem_inc(y_added, 1)
            dve.sem_inc(out_done, 1)
            dve.sem_inc(x_stored[0], 64)
            dve.sem_inc(x_stored[1], 64)
            dve.wait_ge(const_in, 16 * CONSTS)
            dve.memset(ln1[:], 1.0).then_inc(made2, 1)
            dve.tensor_copy(sel[:], sel_f).then_inc(made2, 1)
            dve.tensor_tensor(dsum[:], vec[:, :, V_D], vec[:, :, V_D + 1], ALU.add).then_inc(made2, 1)
            for q in (2, 3):
                dve.wait_ge(made2, q + 1)
                dve.tensor_tensor(dsum[:], dsum[:], vec[:, :, V_D + q], ALU.add).then_inc(made2, 1)
            dve.tensor_tensor(dtb[:].rearrange("p (i k) -> p i k", i=3), vec[:, :, V_DT:V_A],
                              vec[:, :, V_DT:V_A], ALU.add).then_inc(made2, 1)
            dve.wait_ge(exp_made, 2)
            dve.tensor_scalar(nega[:].rearrange("p (i n) -> p i n", i=3), vec[:, :, V_A:V_END], -1.0, None,
                              ALU.mult).then_inc(made2, 1)
            dve.wait_ge(made2, 7)
            dve.sem_inc(made, 1)

            with dve.Fori(0, PAIRS) as pr:
                done = [0]
                step0 = dve.snap(pr * STEPS)

                def own(ins):
                    done[0] += 1
                    ins.then_inc(step, 1)
                    dve.wait_ge(step, step0 + done[0])

                dve.wait_ge(x_loaded, pr * 64 + 64)
                for i in range(3):
                    for t in range(NCHUNK):
                        ins = dve.bn_stats(bn[:, i, t, :], xn[:, i, t * CHUNK:(t + 1) * CHUNK])
                own(ins)
                steady(dve)
                for i in range(3):
                    ins = dve.bn_aggr(mv[:, i, :], bn[:, i, :, :].rearrange("p t s -> p (t s)"))
                own(ins)
                own(dve.tensor_tensor(m2[:], mv[:, :, 0], mv[:, :, 0], ALU.mult))
                own(dve.tensor_tensor(mv[:, :, 1], mv[:, :, 1], m2[:], ALU.add))
                dve.wait_ge(gn_ready, pr + 1)
                own(dve.tensor_copy(gs[:], ps[:, 7, 0:6]))
                own(dve.tensor_tensor(m2[:], gs[:, 0:6:2], gs[:, 0:6:2], ALU.mult))
                own(dve.tensor_tensor(gv[:], gs[:, 1:6:2], m2[:], ALU.subtract))
                own(dve.tensor_scalar(gv[:], gv[:], GN_EPS, None, ALU.add))
                own(dve.reciprocal(gv[:], gv[:]))
                dve.wait_ge(rstd_done, pr + 1)
                own(dve.scalar_tensor_tensor(out=shift[:], in0=gs[:, 0:6:2], scalar=-1.0, in1=rstd[:],
                                             op0=ALU.mult, op1=ALU.mult))
                assert done[0] == STEPS
                for i in range(3):
                    dve.tensor_scalar(xn[:, i, :], xn[:, i, :], rstd[:, i:i + 1], shift[:, i:i + 1],
                                      ALU.mult, ALU.add).then_inc(normed, 1)
                tap0 = dve.snap(pr * (3 * TAPS9) + 1)
                for i in range(3):
                    dve.wait_ge(mix_out, pr * MIXES + (2 * NCHUNK * i + NCHUNK + 1))
                    acc = xc[:, i, :].rearrange("p (h w) -> p h w", w=SIDE)
                    for q in range(TAPS9):
                        src = pad[:, q // 3:q // 3 + SIDE, q % 3:q % 3 + SIDE]
                        w = vec[:, i, V_CONV + q:V_CONV + q + 1]
                        if q == 0:
                            dve.tensor_scalar(acc, src, w, vec[:, i, V_CB:V_CB + 1], ALU.mult, ALU.add)\
                               .then_inc(tap_done, 1)
                        else:
                            dve.wait_ge(tap_done, tap0 + (TAPS9 * i + q))
                            dve.scalar_tensor_tensor(out=acc, in0=src, scalar=w, in1=acc, op0=ALU.mult,
                                                     op1=ALU.add).then_inc(tap_done, 1)
                for i in range(3):
                    dve.wait_ge(xc_done, pr * 3 + (i + 1))
                    dve.tensor_scalar(y[:, i, :], xc[:, i, :], dsum[:, i:i + 1], None, ALU.mult).then_inc(y_init, 1)

                for k in range(DIRS):
                    it = dve.snap(pr * DIRS + k)
                    dve.wait_ge(y_init, pr * 3 + 3)
                    steady(dve)
                    with dve.Fori(0, 3) as i:
                        ti = dve.snap(it * 3 + i)
                        sp0 = dve.snap(ti * (4 * ND))
                        d0 = dve.snap(ti * (5 * ND))
                        u_k = image_view(tile(xc, i), k)
                        for q, (lo, hi) in enumerate(DPIECES):
                            span = slice(lo * CHUNK, hi * CHUNK)
                            dve.wait_ge(sp_done, sp0 + (3 * q + 3))
                            dve.tensor_scalar(one_e[:, span], du[:, span], 1.0, None, ALU.add).then_inc(d_step, 1)
                            dve.wait_ge(d_step, d0 + (3 * q + 1))
                            dve.scalar_tensor_tensor(out=du[:, span], in0=one_e[:, span], scalar=-1.0,
                                                     in1=du[:, span], op0=ALU.add, op1=ALU.subtract).then_inc(d_step, 1)
                            dve.wait_ge(d_step, d0 + (3 * q + 2))
                            dve.tensor_tensor(d[:, span], d[:, span], du[:, span], ALU.subtract).then_inc(d_step, 1)

                        def times_u(q):
                            dve.wait_ge(d_step, d0 + (3 * ND + max(2 * q, 1)))
                            lo, hi = DPIECES[q]
                            span = slice(lo * CHUNK, hi * CHUNK)
                            du_q, d_q = (v[:, span].rearrange("p (a b) -> p a b", b=SIDE) for v in (du, d))
                            rows = slice(8 * lo, 8 * hi)
                            if k % 2:
                                du_q, d_q, rows = du_q[:, ::-1, ::-1], d_q[:, ::-1, ::-1], slice(SIDE - 8 * hi, SIDE - 8 * lo)
                            dve.tensor_tensor(du_q, d_q, u_k[:, rows, :], ALU.mult).then_inc(d_step, 1)

                        for q, (lo, hi) in enumerate(DPIECES):
                            span = slice(lo * CHUNK, hi * CHUNK)
                            dve.wait_ge(sp_done, sp0 + (3 * ND + q + 1))
                            if q == 0:
                                dve.wait_ge(d_step, d0 + 3 * ND)
                            dve.scalar_tensor_tensor(out=d[:, span], in0=t_ln[:, q % 2, 0:(hi - lo) * CHUNK], scalar=ln1[:],
                                                     in1=d[:, span], op0=ALU.subtract, op1=ALU.add)\
                               .then_inc(d_step, 1)
                            if q >= 1:
                                times_u(q - 1)
                        times_u(ND - 1)
                        dve.wait_ge(d_step, d0 + 5 * ND)
                        dve.wait_ge(kept, ti * TILE_N + STATES)
                        steady(dve)
                        dve.memset(state[:], 0.0).then_inc(zeroed, 1)
                        dve.wait_ge(zeroed, ti + 1)
                        steady(dve)

                        def times_b(c, n, n0):
                            dve.wait_ge(b_ready, n0 + (n + 1))
                            dve.wait_ge(scanned, n0 + (n + 1))
                            b = 2 * (n % 2)
                            dve.tensor_tensor(db[:, n % RING, :].rearrange("p (a n) -> p a n", a=2),
                                              ps[:, b:b + 2, 0:HSPAN],
                                              du[:, bass.ds((c + n // STATES) * SPAN, SPAN)]
                                              .rearrange("p (a n) -> p a n", a=2), ALU.mult).then_inc(b_done, 1)

                        def add_y(c):
                            dve.wait_ge(y_ready, ti * TILE_N + (c * STATES + (STATES + RING)))
                            rows = SPAN // SIDE
                            total = ps[:, 6:8, 0:HSPAN].rearrange("p a (r w) -> p a r w", w=SIDE)
                            row = c * rows
                            if k % 2:
                                total, row = total[:, ::-1, ::-1, ::-1], c * -rows + (SIDE - rows)
                            place = image_view(tile(y, i), k)[:, bass.ds(row, rows), :]\
                                .rearrange("p (a r) w -> p a r w", a=2)
                            dve.tensor_tensor(place, place, total, ALU.add).then_inc(y_added, 1)

                        def scan_span(c, first, last):
                            n0 = dve.snap((ti * NSPAN + c) * STATES)
                            for n in range(STATES):
                                if n + 1 < STATES or not last:
                                    times_b(c, n + 1, n0)
                                dve.wait_ge(a_ready, n0 + (n + 1))
                                dve.wait_ge(b_done, n0 + (n + 1))
                                dve.wait_ge(kept, n0 + (n + 1))
                                dve.wait_ge(hc_done, n0 + (n + 1))
                                dve.tensor_tensor_scan(hs[:, n % RING, :], da[:, n % 2, :], db[:, n % RING, :],
                                                       state[:, n:n + 1], ALU.mult, ALU.add).then_inc(scanned, 1)
                                if n == 1 and not first:
                                    add_y(c - 1)

                        times_b(0, 0, dve.snap(ti * TILE_N))
                        scan_span(0, True, False)
                        with dve.Fori(1, NSPAN - 1) as c:
                            scan_span(c, False, False)
                        scan_span(NSPAN - 1, False, True)
                        add_y(NSPAN - 1)
                dve.wait_ge(y_added, (pr + 1) * (DIRS * 3 * NSPAN) + 1)
                c0 = dve.snap(pr * NCHUNK)
                inv0 = dve.snap(pr * (2 * NCHUNK))
                gate0 = dve.snap(pr * (GATES * NCHUNK))

                def half(t):
                    return slice(3 * (t % 2), 3 * (t % 2) + 3)

                def deviate(t):
                    dve.wait_ge(mean_ready, c0 + (t + 1))
                    dve.tensor_tensor(dev[:, half(t), :], y[:, :, t * CHUNK:(t + 1) * CHUNK], ps[:, 0:3, 0:CHUNK],
                                      ALU.subtract).then_inc(dev_done, 1)

                def invert(t):
                    dve.wait_ge(var_ready, c0 + (t + 1))
                    dve.tensor_scalar(rs[:, t % 2, :], ps[:, 6, 0:CHUNK], LN_EPS, None, ALU.add)\
                       .then_inc(inv_step, 1)
                    dve.wait_ge(inv_step, inv0 + (2 * t + 1))
                    dve.reciprocal(rs[:, t % 2, :], rs[:, t % 2, :]).then_inc(inv_step, 1)

                deviate(0)
                invert(0)
                for t in range(NCHUNK):
                    dv = dev[:, half(t), :]
                    dve.wait_ge(inv_ready, c0 + (t + 1))
                    dve.tensor_tensor(dv, dv, ps[:, 3:6, 0:CHUNK], ALU.mult).then_inc(gate_step, 1)
                    if t + 1 < NCHUNK:
                        deviate(t + 1)
                    dve.wait_ge(gate_step, gate0 + (GATES * t + 1))
                    for i in range(3):
                        dve.tensor_scalar(dv[:, i, :], dv[:, i, :], vec[:, i, V_G:V_G + 1], vec[:, i, V_B:V_B + 1],
                                          ALU.mult, ALU.add).then_inc(gate_step, 1)
                    dve.wait_ge(gate_step, gate0 + (GATES * t + 4))
                    dve.wait_ge(fin_in, pr * (80 * NCHUNK) + 80 * (t + 1))
                    dve.tensor_tensor(dv, dv, zc[:, half(t), :], ALU.mult).then_inc(gate_step, 1)
                    if t + 1 < NCHUNK:
                        invert(t + 1)
                    dve.wait_ge(share_ready, c0 + (t + 1))
                    dve.wait_ge(x_stored[t % 2], pr * (64 * OUSES[t % 2]) + (64 * (t // 2) + 64))
                    dve.tensor_tensor(oc[:, half(t), :], xr[:, half(t), :], ps[:, 0:3, 0:CHUNK],
                                      ALU.add).then_inc(out_done, 1)


def host_layout(arrays):
    import numpy as np

    f = {k: np.asarray(v) for k, v in arrays.items()}
    out = {"x": np.ascontiguousarray(f["x"].reshape(8, TOK, CH).transpose(0, 2, 1))}
    for tag in ("L0", "L1"):
        a = lambda n: f[f"{tag}_conv_{n}"]
        w = np.zeros((GROUPS, 128, WCOLS + 3), np.float32)
        for kind, n in enumerate("qvp"):
            v = a(f"{n}_w").reshape(GROUPS, HALF, 2, HALF).transpose(0, 3, 2, 1)
            for j in range(XTILES):
                cols = slice((3 * j + kind) * HALF, (3 * j + kind + 1) * HALF)
                w[:, :HALF, cols] = v[:, :, min(j, 1), :]
                w[:, HALF:, cols] = v[:, REST * j:REST * (j + 1), 0, :]
            w[:, :HALF, BIAS + kind] = a(f"{n}_b").reshape(GROUPS, HALF)
        out[f"{tag}_w"] = w
        out[f"{tag}_ow"] = np.ascontiguousarray(a("o_w").T.reshape(GROUPS, HALF, CH))
        out[f"{tag}_ob"] = np.ascontiguousarray(a("o_b").reshape(2, HALF).T)
        out[f"{tag}_slope"] = np.ascontiguousarray(a("slope").reshape(GROUPS, HALF).T)
        for k in (1, 2):
            h = np.zeros((32, 96 + D1 + 4), np.float32)
            for i in range(3):
                h[:, 32 * i:32 * i + 32] = a(f"t{k}_ws")[i].T
                h[:, 96 + D1 + 1 + i] = a(f"t{k}_bs")[i]
            h[:, 96:96 + D1] = a(f"t{k}_wo").T
            h[:, 96 + D1] = a(f"t{k}_b0")
            out[f"{tag}_t{k}_hid"] = h
            out[f"{tag}_t{k}_w0"] = np.ascontiguousarray(a(f"t{k}_w0").T)
            out[f"{tag}_t{k}_bo"] = np.ascontiguousarray(a(f"t{k}_bo").reshape(GROUPS, HALF).T)
    nei = np.array([[2, 1], [1, 2], [0, 2], [0, 1], [1, 0], [2, 0]])
    k, s = np.arange(12) % 6, np.arange(12) // 6
    sign = np.where(s == 0, 1, -1)
    act = (k[:, None] + sign[:, None] * np.arange(6)[None, :]) % 6
    mult = (k[:, None] + sign[:, None] * k[None, :]) % 6 + 6 * (s[:, None] ^ s[None, :])
    ke = np.zeros((3, 3, 12, 16, 12, 16), np.float32)
    kern = f["L3_conv_kernel"]
    for g in range(12):
        for t in range(7):
            yy, xx = (1, 1) if t == 0 else nei[act[g, t - 1]]
            for h in range(12):
                ke[yy, xx, mult[g, h], :, g, :] = kern[t, h]
    ke = ke.reshape(3, 3, CH, CH)
    taps = np.stack([ke[dy, dx].reshape(2, HALF, CH) for dy, dx in TAPS]).transpose(1, 2, 0, 3)
    out["L3_w"] = np.stack([np.concatenate([taps[min(j, 1)], taps[0, REST * j:REST * (j + 1)]])
                            for j in range(XTILES)]).reshape(XTILES, 128, len(TAPS) * CH)
    a = lambda n: f[f"L2_conv_{n}"]

    def mixed(w):
        o = np.zeros((128, 6, 128), np.float32)
        o[:, 0] = w[:128, :128]
        o[:64, 1] = o[64:, 2] = w[128:, :128]
        o[:, 3, :64] = o[:, 4, 64:] = w[:128, 128:]
        o[:64, 5, :64] = o[64:, 5, 64:] = w[128:, 128:]
        return o

    def tiled(v):
        return np.stack([v[:128], v[:128], np.concatenate([v[128:], v[128:]])], 1)

    out["L2_ssm"], out["L2_z"] = mixed(a("in_proj_w")[:, :CH]), mixed(a("in_proj_w")[:, CH:])
    out["L2_out"] = mixed(a("out_w"))
    c = np.arange(CH)
    out["c_mixgn"] = mixed(((c[:, None] // 6 == c[None] // 6) / 6.0).astype(np.float32))
    out["c_mixln"] = mixed(np.full((CH, CH), 1.0 / CH, np.float32))
    spread = np.zeros((128, 3, 128), np.float32)
    spread[0, 0, :] = spread[64, 1, :] = spread[0, 2, :64] = spread[64, 2, 64:] = 1.0
    out["c_spread"] = spread
    out["L2_vec"] = np.ascontiguousarray(tiled(np.concatenate(
        [a("conv_w").reshape(CH, 9), a("conv_b")[:, None], a("ln_g")[:, None], a("ln_b")[:, None], a("Ds").T,
         a("dt_b").T, a("A_logs").transpose(1, 0, 2).reshape(CH, DIRS * STATES)], 1)))
    wx = np.zeros((DIRS, 128, 3, 128), np.float32)
    wdt = np.zeros((DIRS, 3, 128, 128), np.float32)
    for k in range(DIRS):
        w = np.zeros((CH, 64), np.float32)
        w[:, :RANK], w[:, 32:64] = a("x_proj_w")[k][:, :RANK], a("x_proj_w")[k][:, RANK:]
        wx[k, :, 0, :64] = wx[k, :, 1, 64:] = w[:128]
        wx[k, :64, 2, :64] = wx[k, 64:, 2, 64:] = w[128:]
        dt = a("dt_w")[k]
        wdt[k, 0, :RANK] = wdt[k, 1, 64:64 + RANK] = dt[:, :128]
        wdt[k, 2, :RANK, :64] = wdt[k, 2, 64:64 + RANK, 64:] = dt[:, 128:]
    out["L2_x"], out["L2_dt"] = wx, wdt
    sel = np.zeros((2, 3, STATES, 3, STATES, 128), np.float32)
    for n in range(STATES):
        sel[0, :, n, 0, n, :] = sel[1, :, n, 1, n, :] = 1.0
        sel[0, :, n, 2, n, :64] = sel[1, :, n, 2, n, 64:] = 1.0
    out["c_sel"] = sel.reshape(96, 3, STATES, 128)
    lag = np.arange(LAGS) - (SIDE - 1)
    out["c_pos"] = np.where(lag == SIDE, 0, np.where(lag >= 0, lag, -(SIDE + lag))).astype(np.float32)[None]
    out["c_expo"] = np.tile(np.where(lag == SIDE, 0, np.abs(lag)).astype(np.float32), (HALF, 1))
    out["c_ident"] = np.eye(128, dtype=np.float32)
    c = np.arange(HALF)
    out["c_gmean"] = ((c[:, None] // 6 == c[None] // 6) / 6.0).astype(np.float32)
    return out


def network(nc, ap, out):
    consts = {k: ap[f"c_{k}"] for k in ("pos", "expo", "ident", "gmean")}
    x1, x2, x3 = (nc.dram_tensor(n, (BATCH, CH, TOK), F32).ap() for n in ("x1", "x2", "x3"))
    z = nc.dram_tensor("z", (PAIRS, 128, 3, TOK), F32).ap()
    taps = [[nc.dram_tensor(f"taps{n}_{k}", (D1, LAGS), F32).ap() for k in range(2)] for n in range(2)]
    tables = [[nc.dram_tensor(f"table{n}_{k}", (SIDE, D1, SIDE), F32).ap() for k in range(2)] for n in range(2)]
    with ExitStack() as sems:
        for n in (1, 0):
            mlp = [{part: ap[f"L{n}_t{k}_{part}"] for part in ("w0", "hid", "bo")} for k in (1, 2)]
            toeplitz_taps(nc, sems, f"L{n}t", mlp, ap[f"L{n}_slope"], consts["pos"], consts, taps[n])
        for n, (x_in, x_out) in enumerate(((ap["x"], x1), (x1, x2))):
            tno_layer(nc, sems, f"L{n}", x_in, x_out, ap[f"L{n}_w"], ap[f"L{n}_ow"], ap[f"L{n}_ob"], tables[n], consts,
                      taps=taps[0] if n == 0 else None, later=(taps[1], tables[1]) if n == 0 else None)
        scan_layer(nc, sems, "L2", x2, x3, ap, z, consts)
        conv_layer(nc, sems, "L3", x3, out, ap["L3_w"], consts)


def kernel(**inputs):
    import numpy as np
    import concourse.bacc as bacc
    from concourse.bass_utils import run_bass_kernel_spmd

    arrays = host_layout(inputs)
    nc = bacc.Bacc("TRN2", target_bir_lowering=False, num_devices=1)
    ap = {n: nc.dram_tensor(n, a.shape, F32, kind="ExternalInput").ap() for n, a in arrays.items()}
    out = nc.dram_tensor("out", (BATCH, CH, TOK), F32, kind="ExternalOutput").ap()
    network(nc, ap, out)
    r = run_bass_kernel_spmd(nc, [arrays], core_ids=[0])
    y = np.asarray(r.results[0]["out"]).reshape(BATCH, CH, TOK)
    return np.ascontiguousarray(y.transpose(0, 2, 1)).reshape(BATCH, SIDE, SIDE, CH)
```
